# Optimizing a Trainium2 kernel written in Bass

```python
import numpy as np
import jax
import jax.numpy as jnp

def _softmax(x, axis=-1):
    return jax.nn.softmax(x, axis=axis)

def _gelu(x):
    return jax.nn.gelu(x, approximate=True)

def _silu(x):
    return jax.nn.silu(x)

def _sigmoid(x):
    return jax.nn.sigmoid(x)

def _layernorm(x, axis=-1, eps=1e-05):
    m = jnp.mean(x, axis=axis, keepdims=True)
    v = jnp.var(x, axis=axis, keepdims=True)
    return (x - m) / jnp.sqrt(v + eps)

def _scatter_add(tgt, idx, src, axis=0):
    return tgt.at[idx].add(src)

def _segment_sum(src, seg, n):
    return jax.ops.segment_sum(src, seg, n)
kernel_name = 'mk_decoder_postln_d2_seqx_r8_776542'

def setup_inputs(seed: int=0):
    np.random.seed(seed)
    _w = jnp.asarray

    def _rec_inputs():
        import jax
        import jax.numpy as jnp
        _rk = jax.random.key(seed)
        x = 7.22e-05 + 1 * jax.random.normal(jax.random.fold_in(_rk, 1), (8, 128, 256), jnp.float32)
        _lenS = 128 - jax.random.randint(jax.random.fold_in(_rk, 7), (8,), 0, max(1, 128 // 4) + 1, jnp.int32)
        _lenS2 = 128 - jax.random.randint(jax.random.fold_in(_rk, 8), (8,), 0, max(1, 128 // 4) + 1, jnp.int32)
        _ctx_512P = jax.random.normal(jax.random.fold_in(_rk, 11), (8, 16, 64), jnp.float32)
        _ctx_512c = jax.random.dirichlet(jax.random.fold_in(_rk, 511), 0.3 * jnp.ones((16,), jnp.float32), (8, 128))
        _ctx_512t = jnp.einsum('bsk,bkd->bsd', _ctx_512c, _ctx_512P)
        _ctx_512t = _ctx_512t * jax.lax.rsqrt(jnp.mean(jnp.square(_ctx_512t)) + 1e-12) * 0.953939
        ctx_512 = -0.000514642 + 1.00011 * (_ctx_512t + 0.3 * jax.random.normal(jax.random.fold_in(_rk, 611), (8, 128, 64), jnp.float32))
        return (x, ctx_512)
    x, ctx_512 = _rec_inputs()

    def _L0_attn_setup():
        import jax, jax.numpy as jnp
        import numpy as np
        N_HEADS = 16
        key = jax.random.key(seed)
        ks = jax.random.split(key, 9)
        B, S, D = (2, 256, 256)
        s = 0.02
        return {'X': jax.random.normal(ks[0], (B, S, D), jnp.float32), 'Wq': jax.random.normal(ks[1], (D, D), jnp.float32) * s, 'bq': jax.random.normal(ks[2], (D,), jnp.float32) * s, 'Wk': jax.random.normal(ks[3], (D, D), jnp.float32) * s, 'bk': jax.random.normal(ks[4], (D,), jnp.float32) * s, 'Wv': jax.random.normal(ks[5], (D, D), jnp.float32) * s, 'bv': jax.random.normal(ks[6], (D,), jnp.float32) * s, 'Wo': jax.random.normal(ks[7], (D, D), jnp.float32) * s, 'bo': jax.random.normal(ks[8], (D,), jnp.float32) * s}
    _L0_attn_all = _L0_attn_setup()
    _L0_attn_in = {k: v for k, v in _L0_attn_all.items() if k in ('Wq', 'bq', 'Wk', 'bk', 'Wv', 'bv', 'Wo', 'bo')}
    del _L0_attn_all

    def _L0_xattn_setup():
        import jax, jax.numpy as jnp
        import numpy as np
        import math
        NUM_Q_HEADS = 32
        NUM_KV_HEADS = 8
        key = jax.random.key(seed)
        k1, k2, k3 = jax.random.split(key, 3)
        B, S, E = (2, 256, 256)
        kv_E = NUM_KV_HEADS * (E // NUM_Q_HEADS)
        q = jax.random.normal(k1, (B, S, E), dtype=jnp.float32)
        k = jax.random.normal(k2, (B, S, kv_E), dtype=jnp.float32)
        v = jax.random.normal(k3, (B, S, kv_E), dtype=jnp.float32)
        return {'q': q, 'k': k, 'v': v}
    _L0_xattn_all = _L0_xattn_setup()
    _L0_xattn_in = {k: v for k, v in _L0_xattn_all.items() if k in ()}
    del _L0_xattn_all

    def _L0_ffn_setup():
        import jax, jax.numpy as jnp
        import numpy as np
        TOP_K = 2
        key = jax.random.key(seed)
        ks = jax.random.split(key, 7)
        B, S, H = (2, 256, 256)
        E, A, NS = (8, 64, 2048)
        x = jax.random.normal(ks[0], (B, S, H), jnp.float32)
        gate_w = jax.random.normal(ks[1], (E, H), jnp.float32) * 0.01
        W = jax.random.normal(ks[2], (H, H), jnp.float32) * 0.02
        atoms = jax.random.normal(ks[3], (A, NS), jnp.float32) * 0.02
        expert_atom_weights = jax.random.normal(ks[4], (E, A), jnp.float32) * 0.1
        importance = jax.random.normal(ks[5], (E, NS), jnp.float32) * 0.1
        mask_idx = jax.random.randint(ks[6], (NS,), 0, H * H, jnp.int32)
        return dict(x=x, gate_w=gate_w, W=W, atoms=atoms, expert_atom_weights=expert_atom_weights, importance=importance, mask_idx=mask_idx)
    _L0_ffn_all = _L0_ffn_setup()
    _L0_ffn_in = {k: v for k, v in _L0_ffn_all.items() if k in ('gate_w', 'W', 'atoms', 'expert_atom_weights', 'importance', 'mask_idx')}
    del _L0_ffn_all

    def _L1_attn_setup():
        import jax, jax.numpy as jnp
        import numpy as np
        import math
        HIDDEN = 256
        NUM_HEADS = 32
        KV_HEADS = 8
        HEAD_DIM = HIDDEN // NUM_HEADS
        ROPE_BASE = 10000.0

        def _rotate_half(t):
            mid = t.shape[-1] // 2
            return jnp.concatenate([-t[..., mid:], t[..., :mid]], axis=-1)

        def _rope_tables(seq_len, dtype):
            freq = 1.0 / ROPE_BASE ** (jnp.arange(0, HEAD_DIM, 2, dtype=jnp.float32) / HEAD_DIM)
            t = jnp.arange(seq_len, dtype=jnp.float32)
            freqs = t[:, None] * freq[None, :]
            emb = jnp.concatenate([freqs, freqs], -1).astype(dtype)
            return (jnp.cos(emb), jnp.sin(emb))
        key = jax.random.key(seed)
        ks = jax.random.split(key, 5)
        B, S = (2, 256)
        scale = 0.02
        x = jax.random.normal(ks[0], (B, S, HIDDEN), dtype=jnp.float32)
        Wq = jax.random.normal(ks[1], (NUM_HEADS * HEAD_DIM, HIDDEN), dtype=jnp.float32) * scale
        Wk = jax.random.normal(ks[2], (KV_HEADS * HEAD_DIM, HIDDEN), dtype=jnp.float32) * scale
        Wv = jax.random.normal(ks[3], (KV_HEADS * HEAD_DIM, HIDDEN), dtype=jnp.float32) * scale
        Wo = jax.random.normal(ks[4], (HIDDEN, HIDDEN), dtype=jnp.float32) * scale
        return {'x': x, 'Wq': Wq, 'Wk': Wk, 'Wv': Wv, 'Wo': Wo}
    _L1_attn_all = _L1_attn_setup()
    _L1_attn_in = {k: v for k, v in _L1_attn_all.items() if k in ('Wq', 'Wk', 'Wv', 'Wo')}
    del _L1_attn_all

    def _L1_xattn_setup():
        import jax, jax.numpy as jnp
        import numpy as np
        B, S, H, NH, L = (2, 256, 256, 16, 64)
        HD = H // NH
        key = jax.random.key(seed)
        k1, k2, k3, k4, k5 = jax.random.split(key, 5)
        scale = 0.02
        return {'q': jax.random.normal(k1, (B, S, H), dtype=jnp.float32), 'latent_kv': jax.random.normal(k2, (B, S, L), dtype=jnp.float32), 'Wq': jax.random.normal(k3, (H, H), dtype=jnp.float32) * scale, 'Wkv_expand': jax.random.normal(k4, (2 * H, L), dtype=jnp.float32) * scale, 'Wout': jax.random.normal(k5, (H, H), dtype=jnp.float32) * scale}
    _L1_xattn_all = _L1_xattn_setup()
    _L1_xattn_in = {k: v for k, v in _L1_xattn_all.items() if k in ('Wq', 'Wkv_expand', 'Wout')}
    del _L1_xattn_all

    def _L1_ffn_setup():
        import jax, jax.numpy as jnp
        import numpy as np
        NUM_EXPERTS = 32
        TOP_K = 6
        N_GROUPS = 4
        N_LIMITED_GROUPS = 2
        key = jax.random.key(seed)
        ks = jax.random.split(key, 8)
        H, M = (256, 176)
        SH = 2 * M
        s = 0.02
        return {'hidden_states': jax.random.normal(ks[0], (4, 256, H), jnp.float32), 'gate_w': jax.random.normal(ks[1], (H, NUM_EXPERTS), jnp.float32) * s, 'w_gate': jax.random.normal(ks[2], (NUM_EXPERTS, H, M), jnp.float32) * s, 'w_up': jax.random.normal(ks[3], (NUM_EXPERTS, H, M), jnp.float32) * s, 'w_down': jax.random.normal(ks[4], (NUM_EXPERTS, M, H), jnp.float32) * s, 'sw_gate': jax.random.normal(ks[5], (H, SH), jnp.float32) * s, 'sw_up': jax.random.normal(ks[6], (H, SH), jnp.float32) * s, 'sw_down': jax.random.normal(ks[7], (SH, H), jnp.float32) * s}
    _L1_ffn_all = _L1_ffn_setup()
    _L1_ffn_in = {k: v for k, v in _L1_ffn_all.items() if k in ('gate_w', 'w_gate', 'w_up', 'w_down', 'sw_gate', 'sw_up', 'sw_down')}
    del _L1_ffn_all
    return {'x': x, 'ctx_512': ctx_512, 'L0_attn_Wq': _L0_attn_in['Wq'], 'L0_attn_bq': _L0_attn_in['bq'], 'L0_attn_Wk': _L0_attn_in['Wk'], 'L0_attn_bk': _L0_attn_in['bk'], 'L0_attn_Wv': _L0_attn_in['Wv'], 'L0_attn_bv': _L0_attn_in['bv'], 'L0_attn_Wo': _L0_attn_in['Wo'], 'L0_attn_bo': _L0_attn_in['bo'], 'L0_ffn_gate_w': _L0_ffn_in['gate_w'], 'L0_ffn_W': _L0_ffn_in['W'], 'L0_ffn_atoms': _L0_ffn_in['atoms'], 'L0_ffn_expert_atom_weights': _L0_ffn_in['expert_atom_weights'], 'L0_ffn_importance': _L0_ffn_in['importance'], 'L0_ffn_mask_idx': _L0_ffn_in['mask_idx'], 'L1_attn_Wq': _L1_attn_in['Wq'], 'L1_attn_Wk': _L1_attn_in['Wk'], 'L1_attn_Wv': _L1_attn_in['Wv'], 'L1_attn_Wo': _L1_attn_in['Wo'], 'L1_xattn_Wq': _L1_xattn_in['Wq'], 'L1_xattn_Wkv_expand': _L1_xattn_in['Wkv_expand'], 'L1_xattn_Wout': _L1_xattn_in['Wout'], 'L1_ffn_gate_w': _L1_ffn_in['gate_w'], 'L1_ffn_w_gate': _L1_ffn_in['w_gate'], 'L1_ffn_w_up': _L1_ffn_in['w_up'], 'L1_ffn_w_down': _L1_ffn_in['w_down'], 'L1_ffn_sw_gate': _L1_ffn_in['sw_gate'], 'L1_ffn_sw_up': _L1_ffn_in['sw_up'], 'L1_ffn_sw_down': _L1_ffn_in['sw_down']}

def reference(x, ctx_512, L0_attn_Wq, L0_attn_bq, L0_attn_Wk, L0_attn_bk, L0_attn_Wv, L0_attn_bv, L0_attn_Wo, L0_attn_bo, L0_ffn_gate_w, L0_ffn_W, L0_ffn_atoms, L0_ffn_expert_atom_weights, L0_ffn_importance, L0_ffn_mask_idx, L1_attn_Wq, L1_attn_Wk, L1_attn_Wv, L1_attn_Wo, L1_xattn_Wq, L1_xattn_Wkv_expand, L1_xattn_Wout, L1_ffn_gate_w, L1_ffn_w_gate, L1_ffn_w_up, L1_ffn_w_down, L1_ffn_sw_gate, L1_ffn_sw_up, L1_ffn_sw_down):
    import jax
    import jax.numpy as jnp

    def _L0_attn_ref(X, Wq, bq, Wk, bk, Wv, bv, Wo, bo):
        import jax, jax.numpy as jnp
        import numpy as np
        N_HEADS = 16
        B, S, D = X.shape
        H = N_HEADS
        d_head = D // H
        scale = jnp.asarray(1.0 / np.sqrt(np.sqrt(d_head)), X.dtype)
        Q = (X @ Wq.T + bq).reshape(B, S, H, d_head) * scale
        K = (X @ Wk.T + bk).reshape(B, S, H, d_head) * scale
        V = (X @ Wv.T + bv).reshape(B, S, H, d_head)
        scores = jnp.einsum('bqhd,bkhd->bhqk', Q, K)
        causal = jnp.tril(jnp.ones((S, S), bool))
        scores = jnp.where(causal[None, None], scores, -jnp.inf)
        attn = jax.nn.softmax(scores.astype(jnp.float32), axis=-1).astype(X.dtype)
        out = jnp.einsum('bhqk,bkhd->bqhd', attn, V).reshape(B, S, D)
        return out @ Wo.T + bo

    def _L0_xattn_ref(q, k, v):
        import jax, jax.numpy as jnp
        import numpy as np
        import math
        NUM_Q_HEADS = 32
        NUM_KV_HEADS = 8
        B, S, E = q.shape
        H, KV = (NUM_Q_HEADS, NUM_KV_HEADS)
        D = E // H
        G = H // KV
        scale = math.sqrt(D)
        qh = q.reshape(B, S, KV, G, D).transpose(0, 2, 3, 1, 4)
        kh = k.reshape(B, S, KV, D).transpose(0, 2, 1, 3)
        vh = v.reshape(B, S, KV, D).transpose(0, 2, 1, 3)
        scores = jnp.einsum('bkgsd,bktd->bkgst', qh, kh) / scale
        weights = jax.nn.softmax(scores, axis=-1)
        out = jnp.einsum('bkgst,bktd->bkgsd', weights, vh)
        return out.transpose(0, 3, 1, 2, 4).reshape(B, S, E)

    def _L0_ffn_ref(x, gate_w, W, atoms, expert_atom_weights, importance, mask_idx):
        import jax, jax.numpy as jnp
        import numpy as np
        TOP_K = 2
        B, S, H = x.shape
        xt = x.reshape(-1, H)
        logits = jnp.clip(xt @ gate_w.T, -50.0, 50.0)
        top_w, top_idx = jax.lax.top_k(logits, TOP_K)
        rw = jax.nn.softmax(top_w, axis=-1)
        deltas = jax.nn.softmax(expert_atom_weights, axis=-1) @ atoms
        weighted = deltas * jax.nn.sigmoid(importance)
        rows = mask_idx // H
        cols = mask_idx % H
        vals = jnp.einsum('tk,tks->ts', rw, weighted[top_idx])
        xg = xt[:, cols]
        contrib = jax.ops.segment_sum((xg * vals).T, rows, num_segments=H)
        out = xt @ W.T + contrib.T
        return out.reshape(B, S, H)

    def _L1_attn_ref(x, Wq, Wk, Wv, Wo):
        import jax, jax.numpy as jnp
        import numpy as np
        import math
        HIDDEN = 256
        NUM_HEADS = 32
        KV_HEADS = 8
        HEAD_DIM = HIDDEN // NUM_HEADS
        ROPE_BASE = 10000.0

        def _rotate_half(t):
            mid = t.shape[-1] // 2
            return jnp.concatenate([-t[..., mid:], t[..., :mid]], axis=-1)

        def _rope_tables(seq_len, dtype):
            freq = 1.0 / ROPE_BASE ** (jnp.arange(0, HEAD_DIM, 2, dtype=jnp.float32) / HEAD_DIM)
            t = jnp.arange(seq_len, dtype=jnp.float32)
            freqs = t[:, None] * freq[None, :]
            emb = jnp.concatenate([freqs, freqs], -1).astype(dtype)
            return (jnp.cos(emb), jnp.sin(emb))
        B, S, H = x.shape
        n_rep = NUM_HEADS // KV_HEADS
        q = (x @ Wq.T).reshape(B, S, NUM_HEADS, HEAD_DIM).transpose(0, 2, 1, 3)
        k = (x @ Wk.T).reshape(B, S, KV_HEADS, HEAD_DIM).transpose(0, 2, 1, 3)
        v = (x @ Wv.T).reshape(B, S, KV_HEADS, HEAD_DIM).transpose(0, 2, 1, 3)
        cos, sin = _rope_tables(S, x.dtype)
        cos = cos[None, None, :, :]
        sin = sin[None, None, :, :]
        q = q * cos + _rotate_half(q) * sin
        k = k * cos + _rotate_half(k) * sin
        k = jnp.repeat(k, n_rep, axis=1)
        v = jnp.repeat(v, n_rep, axis=1)
        scores = jnp.einsum('bhqd,bhkd->bhqk', q, k) * (1.0 / math.sqrt(HEAD_DIM))
        i = jnp.arange(S)[:, None]
        j = jnp.arange(S)[None, :]
        causal = (i >= j)[None, None, :, :]
        scores = jnp.where(causal, scores, jnp.float32(-jnp.inf).astype(scores.dtype))
        probs = jax.nn.softmax(scores, axis=-1)
        out = jnp.einsum('bhqk,bhkd->bhqd', probs, v)
        out = out.transpose(0, 2, 1, 3).reshape(B, S, H)
        return out @ Wo.T

    def _L1_xattn_ref(q, latent_kv, Wq, Wkv_expand, Wout):
        import jax, jax.numpy as jnp
        import numpy as np
        B, S, H, NH, L = (2, 256, 256, 16, 64)
        HD = H // NH
        b, sq, _ = q.shape
        sk = latent_kv.shape[1]
        qp = q @ Wq.T
        kv = latent_kv @ Wkv_expand.T
        k, v = jnp.split(kv, 2, axis=-1)
        qh = qp.reshape(b, sq, NH, HD).transpose(0, 2, 1, 3)
        kh = k.reshape(b, sk, NH, HD).transpose(0, 2, 1, 3)
        vh = v.reshape(b, sk, NH, HD).transpose(0, 2, 1, 3)
        inv_sqrt_d = 1.0 / jnp.sqrt(jnp.float32(HD))
        scores = jnp.einsum('bhqd,bhkd->bhqk', qh, kh) * inv_sqrt_d
        causal = jnp.tril(jnp.ones((sq, sk), dtype=bool))
        scores = jnp.where(causal, scores, jnp.finfo(scores.dtype).min)
        attn = jax.nn.softmax(scores, axis=-1)
        out = jnp.einsum('bhqk,bhkd->bhqd', attn, vh)
        out = out.transpose(0, 2, 1, 3).reshape(b, sq, H)
        return out @ Wout.T

    def _L1_ffn_ref(hidden_states, gate_w, w_gate, w_up, w_down, sw_gate, sw_up, sw_down):
        import jax, jax.numpy as jnp
        import numpy as np
        NUM_EXPERTS = 32
        TOP_K = 6
        N_GROUPS = 4
        N_LIMITED_GROUPS = 2
        B, S, H = hidden_states.shape
        E, K = (NUM_EXPERTS, TOP_K)
        x = hidden_states.reshape(-1, H)
        T = x.shape[0]
        scores = jax.nn.sigmoid(x @ gate_w)
        original_scores = scores
        epg = E // N_GROUPS
        sg = scores.reshape(T, N_GROUPS, epg)
        group_scores = jnp.max(sg, axis=-1)
        _, top_groups = jax.lax.top_k(group_scores, N_LIMITED_GROUPS)
        mask = jnp.ones((T, N_GROUPS), dtype=bool)
        mask = mask.at[jnp.arange(T)[:, None], top_groups].set(False)
        sg = jnp.where(mask[:, :, None], -jnp.inf, sg)
        masked_scores = sg.reshape(T, E)
        _, selected_experts = jax.lax.top_k(masked_scores, K)
        weights = jnp.take_along_axis(original_scores, selected_experts, axis=-1)
        weights = weights / jnp.sum(weights, axis=-1, keepdims=True)
        sel_flat = selected_experts.ravel()
        x_exp = jnp.repeat(x, K, axis=0)
        sort_idx = jnp.argsort(sel_flat)
        xs = x_exp[sort_idx]
        group_sizes = jnp.bincount(sel_flat, length=E).astype(jnp.int32)
        g = jax.lax.ragged_dot(xs, w_gate, group_sizes)
        u = jax.lax.ragged_dot(xs, w_up, group_sizes)
        d = jax.lax.ragged_dot(jax.nn.silu(g) * u, w_down, group_sizes)
        unsort_idx = jnp.argsort(sort_idx)
        out = d[unsort_idx].reshape(T, K, H)
        expert_out = jnp.sum(out * weights[..., None], axis=1)
        shared = jax.nn.silu(x @ sw_gate) * (x @ sw_up) @ sw_down
        return (expert_out + shared).reshape(B, S, H)
    x = _layernorm(x + _L0_attn_ref(x, L0_attn_Wq, L0_attn_bq, L0_attn_Wk, L0_attn_bk, L0_attn_Wv, L0_attn_bv, L0_attn_Wo, L0_attn_bo), axis=-1)
    x = _layernorm(x + _L0_xattn_ref(x, ctx_512, ctx_512), axis=-1)
    x = _layernorm(x + _L0_ffn_ref(x, L0_ffn_gate_w, L0_ffn_W, L0_ffn_atoms, L0_ffn_expert_atom_weights, L0_ffn_importance, L0_ffn_mask_idx), axis=-1)
    x = _layernorm(x + _L1_attn_ref(x, L1_attn_Wq, L1_attn_Wk, L1_attn_Wv, L1_attn_Wo), axis=-1)
    x = _layernorm(x + _L1_xattn_ref(x, ctx_512, L1_xattn_Wq, L1_xattn_Wkv_expand, L1_xattn_Wout), axis=-1)
    x = _layernorm(x + _L1_ffn_ref(x, L1_ffn_gate_w, L1_ffn_w_gate, L1_ffn_w_up, L1_ffn_w_down, L1_ffn_sw_gate, L1_ffn_sw_up, L1_ffn_sw_down), axis=-1)
    return x

_drawn_inputs = setup_inputs


def setup_inputs(seed=0):
    import zlib

    import numpy as np

    out = dict(_drawn_inputs(seed))
    spreads = {}
    factors = {'L0_attn_Wq': 8.0,
     'L0_attn_bq': 8.0,
     'L0_attn_Wk': 8.0,
     'L0_attn_bk': 8.0,
     'L0_attn_Wv': 2.885,
     'L0_attn_bv': 8.0,
     'L0_attn_Wo': 2.768,
     'L0_attn_bo': 3.269,
     'L0_ffn_gate_w': 8.0,
     'L0_ffn_atoms': 8.0,
     'L0_ffn_expert_atom_weights': 8.0,
     'L0_ffn_importance': 8.0,
     'L1_attn_Wq': 8.0,
     'L1_attn_Wk': 8.0,
     'L1_xattn_Wq': 8.0,
     'L1_ffn_gate_w': 8.0,
     'L1_ffn_w_gate': 8.0,
     'L1_ffn_w_up': 8.0,
     'L1_ffn_w_down': 8.0,
     'L1_ffn_sw_gate': 2.885,
     'L1_ffn_sw_up': 2.862,
     'L1_ffn_sw_down': 2.863}
    for name, (base, spread) in spreads.items():
        noise = np.random.default_rng([zlib.crc32(name.encode()), seed]).standard_normal(out[name].shape)
        drawn = base * np.exp(spread * noise) if base else spread * noise
        out[name] = jnp.asarray(drawn.astype(out[name].dtype))
    for name, factor in factors.items():
        out[name] = (out[name] * factor).astype(out[name].dtype)
    return out
```

```python
from contextlib import ExitStack

import numpy as np

import concourse.bass as bass
from concourse import mybir

F32 = mybir.dt.float32
F32R = mybir.dt.float32r
BF16 = mybir.dt.bfloat16
I32 = mybir.dt.int32
U32 = mybir.dt.uint32
ALU = mybir.AluOpType
ACT = mybir.ActivationFunctionType
AX = mybir.AxisListType

B, S, D = 8, 128, 256
KT = D // 128
CTX = 64
EPS = 1e-5
HEAD_ROWS = 64
MAX_HI, MAX_LO = 64, 72
MAX_END = 80
MASKED = -1e30
E0, ATOMS, NS = 8, 64, 2048
E1, TOP, MI = 32, 6, 176
GROUPS, TOP_GROUPS = 4, 2
UNITS = E1 + 2
MH = MI // 2


class Cfg:

    def __init__(self, name, wide, causal, scale, own_kv, project, rope, bias, out):
        self.name, self.causal, self.scale = name, causal, scale
        self.wide = wide
        self.own_kv, self.project, self.rope, self.bias, self.out = own_kv, project, rope, bias, out
        self.quads = 4 if wide else 8
        self.blocks = 16 if wide else 8
        self.kv_heads = 16 if wide else 8
        self.d = 16 if wide else 8
        self.kcols = 4 if wide else 1


ATTN0 = Cfg("a0", True, True, 0.25, True, True, False, True, True)
CROSS0 = Cfg("x0", False, False, 8.0 ** -0.5, False, False, False, False, False)
ATTN1 = Cfg("a1", False, True, 8.0 ** -0.5, True, True, True, False, True)
CROSS1 = Cfg("x1", True, True, 0.25, False, True, False, False, True)


def wait_apart(T, eng, sem, value):
    eng.wait_ge(sem, value)
    eng.sem_inc(T.passed, 1)


class Stage:

    def __init__(self, nc, prefix):
        self.nc, self.prefix, self.sems = nc, prefix, []

    def sem(self, name):
        self.sems.append(self.nc.alloc_semaphore(f"{self.prefix}_{name}"))
        return self.sems[-1]

    def __enter__(self):
        return self

    def __exit__(self, *failed):
        if not failed[0]:
            self.nc.clear_and_free_semaphores(self.sems)
            self.nc.all_engine_barrier()


def attention(nc, cfg, T):
    NQ, d, KVH = cfg.quads, cfg.d, cfg.kv_heads
    HEADS = 16 if cfg.wide else 32
    with Stage(nc, cfg.name) as stage, ExitStack() as ctx:
        sem = stage.sem

        loaded = [sem("loaded0"), sem("loaded1")]
        xt_done = sem("xt_done")
        xt_copied = sem("xt_copied")
        proj_done = sem("proj_done")
        qk_copied = sem("qk_copied")
        v_copied = sem("v_copied")
        t2_done = sem("t2_done")
        rounded = sem("rounded")
        split = sem("split")
        q_ready = sem("q_ready")
        q_clear = sem("q_clear")
        k_ready = sem("k_ready")
        k2_ready = sem("k2_ready")
        ones_set = sem("ones_set")
        s_done = sem("s_done")
        max_done = sem("max_done")
        nm_hi = sem("nm_hi")
        nm_split = sem("nm_split")
        nm_done = sem("nm_done")
        nm_ready = sem("nm_ready")
        st_done = sem("st_done")
        exp_done = sem("exp_done")
        pv_done = sem("pv_done")
        rec_done = sem("rec_done")
        att_ready = sem("att_ready")
        at_done = sem("at_done")
        at_copied = sem("at_copied")
        out_done = sem("out_done")
        bias_done = sem("bias_done")
        res_done = sem("res_done")
        stat_done = sem("stat_done")
        aggr_done = sem("aggr_done")
        var_done = sem("var_done")
        rstd_done = sem("rstd_done")
        ln_done = sem("ln_done")
        permuted = sem("permuted")
        rope_a = sem("rope_a")

        block = ctx.enter_context(nc.Block())
        PA, PB, M, PV = T.PA, T.PB, T.M, T.PV
        SB, STB = T.SB, T.STB

        @block.sync
        def _(sp):
            def load(n, par):
                if cfg.project:
                    sp.dma_start(T.xs[par][:], T.x_all[:, bass.ds(n, 1), :].rearrange("p a c -> p (a c)")).then_inc(loaded[par], 16)
                if not cfg.own_kv:
                    sp.dma_start(T.cs[par][:], T.ctx_tiles[bass.ds(n, 1), :, :].rearrange("a p c -> p (a c)")).then_inc(loaded[par], 16)

            load(0, 0)
            load(1, 1)
            with sp.Fori(1, B // 2) as i:
                for par in range(2):
                    if cfg.project:
                        sp.wait_ge(xt_done, i * 2 + (par - 1))
                    else:
                        sp.wait_ge(v_copied, i * 2 + (par - 1))
                        sp.wait_ge(split, i * 2 + (par - 1))
                    load(i * 2 + par, par)

        per_load = 16 if cfg.own_kv or not cfg.project else 32

        def wait_loaded(eng, n, par):
            if isinstance(n, int):
                eng.wait_ge(loaded[par], (n // 2 + 1) * per_load)
            else:
                eng.wait_ge(loaded[par], (n + (2 - par)) * (per_load // 2))

        @block.tensor
        def _(pe):
            def project(n):
                pe.wait_ge(xt_copied, n + 1)
                if not (isinstance(n, int) and n == 0):
                    pe.wait_ge(q_ready, n)
                    pe.wait_ge(k_ready, n)
                if cfg is ATTN0:
                    parts = [(PA[:, 0:512], T.a0_wqk), (PB[:, 0:256], T.a0_wv)]
                elif cfg is ATTN1:
                    parts = [(PA[:, 0:320], T.a1_wqkv[:, :, 0:320]), (PB[:, 0:64], T.a1_wqkv[:, :, 320:384])]
                else:
                    parts = [(PB[:, 0:256], T.x1_wq)]
                    pe.matmul(PA[:, 0:512], T.xT[0:CTX, 256:384], T.x1_wkv[0:CTX, :], start=True, stop=True)
                for out, w in parts:
                    for j in range(KT):
                        last = pe.matmul(out, T.xT[:, j * 128:(j + 1) * 128], w[:, j, :], start=(j == 0), stop=(j == KT - 1))
                last.then_inc(proj_done, 1)

            def transpose_qk(n):
                pe.wait_ge(rounded, n + 1)
                pe.wait_ge(split, n + 1)
                if cfg.project:
                    pe.wait_ge(v_copied, n + 1)
                pe.sem_inc(T.passed, 1)
                for g in range(4):
                    pe.transpose(PA[:, g * 128:(g + 1) * 128], T.qs[:, g, :].bitcast(F32), T.ident[:])
                for c in range(cfg.kcols):
                    pe.transpose(PB[:, c * 128:(c + 1) * 128], T.ks1[:, c, :].bitcast(F32), T.ident[:])
                for c in range(cfg.kcols):
                    last = pe.transpose(M[0:64, c * 128:(c + 1) * 128], T.ks2[:, c, :].bitcast(F32), T.ident[:])
                last.then_inc(t2_done, 1)

            def scores(b, par):
                pe.wait_ge(q_ready, b + 1)
                pe.wait_ge(q_clear, b + 1)
                pe.wait_ge(k_ready, b + 1)
                pe.wait_ge(k2_ready, b + 1)
                if isinstance(b, int) and b == 0:
                    pe.wait_ge(ones_set, 2)
                for i in range(NQ):
                    if not (isinstance(b, int) and b == 0 and i < 2):
                        pe.wait_ge(max_done, b * NQ + (i - 1))
                    bank = SB[i % 2]
                    if cfg.causal:
                        pe.matmul(bank[:, :], T.ident_bf[:], T.mask_qk[:], start=True, stop=False)
                    g = i if cfg.wide else i // 2
                    blocks = slice(4 * i, 4 * i + 4) if cfg.wide else slice(4 * (i % 2), 4 * (i % 2) + 4)
                    pe.matmul(bank[:, :], T.q1[par][:, g, :], T.kb1[par][:, blocks, :], start=not cfg.causal, stop=False)
                    pe.matmul(bank[:, :], T.q2[par][:, g, :], T.kb2[par][:, blocks, :], start=False, stop=True).then_inc(s_done, 1)

            def scores_t(b, par, i):
                if i == 0:
                    pe.wait_ge(nm_ready, b + 1)
                if not (isinstance(b, int) and b == 0 and i < 2):
                    pe.wait_ge(exp_done, b * NQ + (i - 1))
                bank = STB[i % 2]
                if cfg.wide:
                    for j in range(4):
                        block = bank[:, j * 128:(j + 1) * 128]
                        pe.matmul(block, T.ident_bf[:], T.mask_kq[:, 0:128], start=True, stop=False)
                        pe.matmul(block, T.kb1[par][:, 4 * i + j, :], T.q1[par][:, i, :], start=False, stop=False)
                        last = pe.matmul(block, T.kb2[par][:, 4 * i + j, :], T.q2[par][:, i, :], start=False, stop=True)
                else:
                    if cfg.causal:
                        pe.matmul(bank[:, :], T.ident_bf[:], T.mask_kq[:], start=True, stop=False)
                    pe.matmul(bank[:, :], T.kb1[par][:, i, :], T.q1[par][:, :, :], start=not cfg.causal, stop=False)
                    last = pe.matmul(bank[:, :], T.kb2[par][:, i, :], T.q2[par][:, :, :], start=False, stop=True)
                last.then_inc(st_done, 1)

            def values(b, par, i):
                pe.wait_ge(exp_done, b * NQ + (i + 1))
                if i == 0:
                    pe.wait_ge(v_copied, b + 1)
                    if not (isinstance(b, int) and b == 0):
                        pe.wait_ge(att_ready, b)
                for j in range(4):
                    h = 4 * i + j
                    kv = h if cfg.wide else i
                    last = pe.matmul(PV[:, h * (d + 1):(h + 1) * (d + 1)], T.pt[i % 2][:, j * 128:(j + 1) * 128],
                                     T.vaug[par][:, kv * (d + 1):(kv + 1) * (d + 1)], start=True, stop=True)
                if i == NQ - 1:
                    last.then_inc(pv_done, 1)

            def project_out(m):
                pe.wait_ge(at_copied, m + 1)
                for j in range(KT):
                    last = pe.matmul(M[:, 0:256], T.atT[:, j * 128:(j + 1) * 128], T.wo[cfg.name][:, j, :],
                                     start=(j == 0), stop=(j == KT - 1))
                last.then_inc(out_done, 1)

            def iteration(b, par, has_prev, has_next):
                if cfg.project and has_next:
                    wait_loaded(pe, b + 1, 1 - par)
                    pe.wait_ge(k2_ready, b + 1)
                    for j in range(KT):
                        last = pe.transpose(M[:, j * 128:(j + 1) * 128], T.xs[1 - par][:, j * 128:(j + 1) * 128], T.ident[:])
                    if not cfg.own_kv:
                        last = pe.transpose(M[0:CTX, 256:384], T.cs[1 - par][:], T.ident[:])
                    last.then_inc(xt_done, 1)
                scores(b, par)
                if cfg.out and has_prev:
                    pe.wait_ge(att_ready, b)
                    if has_next:
                        pe.wait_ge(xt_copied, b + 2)
                    else:
                        pe.wait_ge(nm_ready, b)
                    for j in range(KT):
                        last = pe.transpose(M[:, j * 128:(j + 1) * 128], T.att[:, j * 128:(j + 1) * 128], T.ident[:])
                    last.then_inc(at_done, 1)
                    project_out(b - 1)
                if cfg.project and has_next:
                    project(b + 1)
                pe.wait_ge(nm_split, b + 1)
                if cfg.out and has_prev:
                    pe.wait_ge(res_done, b)
                elif cfg.project and has_next:
                    pe.wait_ge(xt_copied, b + 2)
                elif has_prev:
                    pe.wait_ge(nm_ready, b)
                for g in range(4):
                    last = pe.transpose(M[:, g * 128:(g + 1) * 128], T.nm[:, g, :].bitcast(F32), T.ident[:])
                last.then_inc(nm_done, 1)
                for i in range(NQ):
                    scores_t(b, par, i)
                    if i >= 1:
                        values(b, par, i - 1)
                    if i == NQ // 2 and has_next:
                        transpose_qk(b + 1)
                values(b, par, NQ - 1)

            if cfg.project:
                wait_loaded(pe, 0, 0)
                for j in range(KT):
                    last = pe.transpose(M[:, j * 128:(j + 1) * 128], T.xs[0][:, j * 128:(j + 1) * 128], T.ident[:])
                if not cfg.own_kv:
                    last = pe.transpose(M[0:CTX, 256:384], T.cs[0][:], T.ident[:])
                last.then_inc(xt_done, 1)
                project(0)
            transpose_qk(0)
            if cfg.project:
                pe.wait_ge(xt_copied, 1)
            iteration(0, 0, False, True)
            with pe.Fori(0, B // 2 - 1) as i:
                iteration(i * 2 + 1, 1, True, True)
                iteration(i * 2 + 2, 0, True, True)
            iteration(B - 1, 1, True, False)
            if cfg.out:
                pe.wait_ge(att_ready, B)
                pe.wait_ge(nm_ready, B)
                for j in range(KT):
                    last = pe.transpose(M[:, j * 128:(j + 1) * 128], T.att[:, j * 128:(j + 1) * 128], T.ident[:])
                last.then_inc(at_done, 1)
                project_out(B - 1)

        @block.scalar
        def _(act):
            def copy_xt(n):
                act.wait_ge(xt_done, n + 1)
                last = act.activation(T.xT[:, 0:256], M[:, 0:256], ACT.Copy)
                if not cfg.own_kv:
                    last = act.activation(T.xT[0:CTX, 256:384], M[0:CTX, 256:384], ACT.Copy)
                last.then_inc(xt_copied, 1)

            def copy_proj(n, par):
                if cfg is ATTN0:
                    return
                act.wait_ge(proj_done, n + 1)
                vout = T.vaug[par][:, 0:KVH * (d + 1)].rearrange("p (h e) -> p h e", e=d + 1)[:, :, 0:d]
                if cfg is ATTN1:
                    act.activation(vout, PB[:, 0:64].rearrange("p (h e) -> p h e", e=d), ACT.Copy).then_inc(v_copied, 1)
                else:
                    act.activation(T.qk[:, 0:256], PB[:, 0:256], ACT.Copy)
                    act.activation(T.qk[:, 256:512], PA[:, 0:256], ACT.Copy).then_inc(qk_copied, 1)
                    act.activation(vout, PA[:, 256:512].rearrange("p (h e) -> p h e", e=d), ACT.Copy).then_inc(v_copied, 1)

            def round_qk(n, par):
                if cfg.project:
                    act.wait_ge(qk_copied, n + 1)
                    k = T.qk[:, 256:256 + 64 * cfg.kcols]
                else:
                    act.wait_ge(permuted, n + 1)
                    wait_loaded(act, n, par)
                    k = T.cs[par][:, :]
                if not (isinstance(n, int) and n == 0):
                    act.wait_ge(t2_done, n)
                act.activation(T.qs[:, :, 0:64], T.qk[:, 0:256].rearrange("p (g c) -> p g c", g=4), ACT.Copy)
                k3 = k.rearrange("p (c e) -> p c e", e=64)
                act.activation(T.ks1[:, 0:cfg.kcols, 0:64], k3, ACT.Copy)
                act.activation(T.ks1[:, 0:cfg.kcols, 64:128], k3, ACT.Copy).then_inc(rounded, 1)
                if not cfg.project:
                    vout = T.vaug[par][:, 0:KVH * (d + 1)].rearrange("p (h e) -> p h e", e=d + 1)[:, :, 0:d]
                    act.activation(vout, T.cs[par][:, :].rearrange("p (h e) -> p h e", e=d), ACT.Copy).then_inc(v_copied, 1)

            def copy_q(n, par):
                act.wait_ge(t2_done, n + 1)
                act.activation(T.q1[par][:, :, :].rearrange("p g q -> p (g q)"), PA[:, :], ACT.Copy)
                act.activation(T.q2[par][0:64, :, :].rearrange("p g q -> p (g q)"), PA[0:64, :], ACT.Copy).then_inc(q_ready, 1)
                if cfg.wide:
                    out = T.kb2[par][0:64, :, :].rearrange("p (c j) k -> p c j k", j=4)
                    for j in range(4):
                        last = act.activation(out[:, :, j, :], M[0:64, :].rearrange("p (c k) -> p c k", c=4), ACT.Copy,
                                              scale=T.blockmask[0:64, 8 + j:9 + j])
                    last.then_inc(k2_ready, 1)

            def iteration(b, par, has_prev, has_next):
                if cfg.project and has_next:
                    copy_xt(b + 1)
                if cfg.out and has_prev:
                    act.wait_ge(at_done, b)
                    act.activation(T.atT[:], M[:, 0:256], ACT.Copy).then_inc(at_copied, 1)
                if cfg.project and has_next:
                    copy_proj(b + 1, 1 - par)
                act.wait_ge(nm_done, b + 1)
                act.activation(T.q2[par][MAX_HI:MAX_END, :, :].rearrange("p g q -> p (g q)"),
                               M[MAX_HI:MAX_END, :], ACT.Copy).then_inc(nm_ready, 1)
                if has_next:
                    round_qk(b + 1, 1 - par)
                for i in range(NQ):
                    act.wait_ge(st_done, b * NQ + (i + 1))
                    act.activation(T.pt[i % 2][:, :], STB[i % 2][:, :], ACT.Exp, scale=cfg.scale).then_inc(exp_done, 1)
                    if i == NQ // 2 and has_next:
                        copy_q(b + 1, 1 - par)

            if cfg.project:
                copy_xt(0)
                copy_proj(0, 0)
            round_qk(0, 0)
            copy_q(0, 0)
            iteration(0, 0, False, True)
            with act.Fori(0, B // 2 - 1) as i:
                iteration(i * 2 + 1, 1, True, True)
                iteration(i * 2 + 2, 0, True, True)
            iteration(B - 1, 1, True, False)
            if cfg.out:
                act.wait_ge(at_done, B)
                act.activation(T.atT[:], M[:, 0:256], ACT.Copy).then_inc(at_copied, 1)

        @block.vector
        def _(dve):
            def proj(n, par):
                if cfg is ATTN0:
                    dve.wait_ge(proj_done, n + 1)
                    dve.tensor_tensor(T.qk[:, :], PA[:, 0:512], T.b_qk[:], ALU.add).then_inc(qk_copied, 1)
                    vout = T.vaug[par][:, :].rearrange("p (h e) -> p h e", e=d + 1)[:, :, 0:d]
                    dve.tensor_tensor(vout, PB[:, 0:256].rearrange("p (h e) -> p h e", e=d),
                                      T.b_v[:].rearrange("p (h e) -> p h e", e=d), ALU.add).then_inc(v_copied, 1)
                elif cfg is ATTN1:
                    dve.wait_ge(proj_done, n + 1)
                    src = PA[:, 0:320].rearrange("p (h e) -> p h e", e=d)
                    cos = T.rope[:, 0:8].unsqueeze(1).broadcast_to([128, 40, 8])
                    half = d // 2
                    a = T.rope_a[:, :].rearrange("p (h e) -> p h e", e=d)
                    r = T.rope_b[:, :].rearrange("p (h e) -> p h e", e=d)
                    dve.tensor_tensor(a, src, cos, ALU.mult).then_inc(rope_a, 1)
                    for lo in (0, half):
                        sin = T.rope[:, 8 + lo:8 + lo + half].unsqueeze(1).broadcast_to([128, 40, half])
                        dve.tensor_tensor(r[:, :, lo:lo + half], src[:, :, half - lo:d - lo], sin, ALU.mult).then_inc(rope_a, 1)
                    dve.wait_ge(rope_a, (n + 1) * 3)
                    dve.tensor_tensor(T.qk[:, 0:320], T.rope_a[:, :], T.rope_b[:, :], ALU.add).then_inc(qk_copied, 1)

            def keys(n, par):
                dve.wait_ge(t2_done, n + 1)
                if cfg.wide:
                    out = T.kb1[par][:, :, :].rearrange("p (c j) k -> p c j k", j=4)
                    for j in range(4):
                        last = dve.tensor_scalar(out[:, :, j, :], PB[:, :].rearrange("p (c k) -> p c k", c=4),
                                                 T.blockmask[:, 8 + j:9 + j], None, ALU.mult)
                    last.then_inc(k_ready, 1)
                else:
                    for rows, out, bank, ready in ((128, T.kb1[par], PB, k_ready), (64, T.kb2[par], M, k2_ready)):
                        dve.tensor_tensor(out[0:rows, 0:8, :], bank[0:rows, 0:128].unsqueeze(1).broadcast_to([rows, 8, 128]),
                                          T.blockmask[0:rows, 0:8].unsqueeze(2).broadcast_to([rows, 8, 128]),
                                          ALU.mult).then_inc(ready, 1)

            def normalise(m):
                dve.wait_ge(pv_done, m + 1)
                pv = PV[:, 0:HEADS * (d + 1)].rearrange("p (h e) -> p h e", e=d + 1)
                dve.reciprocal(T.rec[:, 0:HEADS], pv[:, :, d]).then_inc(rec_done, 1)
                dve.wait_ge(rec_done, m + 1)
                dve.tensor_tensor(T.att[:, :].rearrange("p (h e) -> p h e", e=d), pv[:, :, 0:d],
                                  T.rec[:, 0:HEADS].unsqueeze(2).broadcast_to([128, HEADS, d]), ALU.mult).then_inc(att_ready, 1)

            def residual(m):
                x = T.x_all[:, bass.ds(m, 1), :].rearrange("p a c -> p (a c)")
                if cfg.out:
                    if cfg.bias:
                        dve.tensor_tensor(T.xb[:], x, T.b_o[:], ALU.add).then_inc(bias_done, 1)
                        dve.wait_ge(bias_done, m + 1)
                        x = T.xb[:]
                    dve.wait_ge(out_done, m + 1)
                    dve.tensor_tensor(T.res[:], M[:, 0:256], x, ALU.add).then_inc(res_done, 1)
                else:
                    dve.wait_ge(att_ready, m + 1)
                    dve.tensor_tensor(T.res[:], T.att[:], x, ALU.add).then_inc(res_done, 1)

            def norm(m):
                dve.wait_ge(res_done, m + 1)
                dve.bn_stats(T.stats[:], T.res[:]).then_inc(stat_done, 1)
                wait_apart(T, dve, stat_done, m + 1)
                dve.bn_aggr(T.mv[:], T.stats[:]).then_inc(aggr_done, 1)
                dve.wait_ge(aggr_done, m + 1)
                dve.tensor_scalar(T.vare[:], T.mv[:, 1:2], EPS, None, ALU.add).then_inc(var_done, 1)
                dve.wait_ge(rstd_done, m + 1)
                x = T.x_all[:, bass.ds(m, 1), :].rearrange("p a c -> p (a c)")
                dve.tensor_scalar(x, T.res[:], T.mv[:, 0:1], T.rstd[:], ALU.subtract, ALU.mult).then_inc(ln_done, 1)

            def iteration(b, par, has_prev, has_next):
                if has_prev:
                    normalise(b - 1)
                for i in range(NQ):
                    dve.wait_ge(s_done, b * NQ + (i + 1))
                    g = i if cfg.wide else i // 2
                    at = 0 if cfg.wide else 4 * (i % 2)
                    dve.tensor_reduce(T.nmf[:, g, at:at + 4], SB[i % 2][:, :].rearrange("p (h k) -> p h k", h=4),
                                      AX.X, ALU.max, negate=True).then_inc(max_done, 1)
                n = 4 if cfg.wide else 8
                dve.wait_ge(max_done, b * NQ + NQ)
                dve.tensor_copy(T.nm[:, :, MAX_HI:MAX_HI + n], T.nmf[:, :, 0:n]).then_inc(nm_hi, 1)
                dve.wait_ge(nm_hi, b + 1)
                dve.tensor_tensor(T.nm[:, :, MAX_LO:MAX_LO + n], T.nmf[:, :, 0:n], T.nm[:, :, MAX_HI:MAX_HI + n].bitcast(F32),
                                  ALU.subtract).then_inc(nm_split, 1)
                if has_prev:
                    residual(b - 1)
                if cfg.project and has_next:
                    proj(b + 1, 1 - par)
                if has_prev:
                    norm(b - 1)
                if has_next:
                    keys(b + 1, 1 - par)

            blocks = T.onerows[64:128, 8:24] if cfg.wide else T.onerows[64:128, 0:8]
            for par in range(2):
                dve.tensor_copy(T.kb2[par][64:128, 0:cfg.blocks, :], blocks.unsqueeze(2).broadcast_to([64, cfg.blocks, 128])).then_inc(ones_set, 1)
            if cfg.project:
                proj(0, 0)
            keys(0, 0)
            iteration(0, 0, False, True)
            with dve.Fori(0, B // 2 - 1) as i:
                iteration(i * 2 + 1, 1, True, True)
                iteration(i * 2 + 2, 0, True, True)
            iteration(B - 1, 1, True, False)
            normalise(B - 1)
            residual(B - 1)
            norm(B - 1)

        @block.gpsimd
        def _(pool):
            def permute(n):
                if not (isinstance(n, int) and n == 0):
                    pool.wait_ge(rounded, n)
                    pool.wait_ge(split, n)
                pool.tensor_copy(T.qk[:, 0:256].rearrange("p (g v d) -> p g v d", g=4, d=8),
                                 T.x_all[:, bass.ds(n, 1), :].rearrange("p a (v g d) -> p (a g) v d", g=4, d=8)
                                 ).then_inc(permuted, 1)

            def low_parts(n, par):
                pool.wait_ge(rounded, n + 1)
                k = T.qk[:, 256:256 + 64 * cfg.kcols] if cfg.project else T.cs[par][:, :]
                pool.tensor_tensor(T.qs[:, :, 64:128], T.qk[:, 0:256].rearrange("p (g c) -> p g c", g=4),
                                   T.qs[:, :, 0:64].bitcast(F32), ALU.subtract)
                pool.tensor_tensor(T.ks2[:, 0:cfg.kcols, :], k.rearrange("p (c e) -> p c e", e=64),
                                   T.ks1[:, 0:cfg.kcols, 0:64].bitcast(F32), ALU.subtract).then_inc(split, 1)

            def clear(n, par, after_rstd):
                pool.wait_ge(t2_done, n + 1)
                pool.wait_ge(split, n + 1)
                if after_rstd:
                    pool.wait_ge(rstd_done, n - 1)
                pool.sem_inc(T.passed, 1)
                pool.memset(T.q2[par][64:128, :, :].bitcast(F32), 0.0).then_inc(q_clear, 1)

            def rstd(m):
                pool.wait_ge(var_done, m + 1)
                pool.tensor_tensor(T.rstd[:], T.vare[:], T.half[:], ALU.pow).then_inc(rstd_done, 1)

            def iteration(b, par, has_prev, has_next):
                pool.wait_ge(q_clear, b + 1)
                if has_next:
                    if not cfg.project:
                        permute(b + 1)
                    low_parts(b + 1, 1 - par)
                if has_prev:
                    rstd(b - 1)
                if has_next:
                    clear(b + 1, 1 - par, has_prev)

            if not cfg.project:
                permute(0)
            low_parts(0, 0)
            clear(0, 0, False)
            iteration(0, 0, False, True)
            with pool.Fori(0, B // 2 - 1) as i:
                iteration(i * 2 + 1, 1, True, True)
                iteration(i * 2 + 2, 0, True, True)
            iteration(B - 1, 1, True, False)
            rstd(B - 1)


class Memory:

    def __init__(self, nc, start, end):
        self.nc, self.at, self.end = nc, start, end

    def __call__(self, name, shape, dt=F32):
        size = int(np.prod(shape[1:])) * (2 if dt == BF16 else 4)
        size = (size + 31) // 32 * 32
        assert self.at + size <= self.end, f"{name} does not fit: {self.at + size} > {self.end}"
        t = self.nc.alloc_sbuf_tensor_at(name, list(shape), dt, offset=self.at)
        self.at += size
        return t


class Tensors:
    pass


def flat(x_all, t):
    return x_all[:, bass.ds(t, 1), :].rearrange("p a c -> p (a c)")


def ktiles(w):
    return w.rearrange("(k p) n -> p k n", p=128)


def broadcast(v):
    return v.rearrange("(a n) -> a n", a=1).broadcast_to([128, v.shape[0]])


def load_first(nc, a, T):
    loads = [(T.x_all[:], a["x"].rearrange("b p c -> p b c")), (T.ident[:], a["ident"]),
             (T.masks[:], a["masks"]), (T.blockmask[:], a["blockmask"]), (T.rope[:], a["rope"]), (T.onerows[:], a["onerows"]),
             (T.a0_wqk[:, :, 0:256], ktiles(a["L0_attn_Wq"])), (T.a0_wqk[:, :, 256:512], ktiles(a["L0_attn_Wk"])),
             (T.a0_wv[:], ktiles(a["L0_attn_Wv"])), (T.a0_wo[:], ktiles(a["L0_attn_Wo"])),
             (T.b_qk[:, 0:256], broadcast(a["L0_attn_bq"])), (T.b_qk[:, 256:512], broadcast(a["L0_attn_bk"])),
             (T.b_v[:], broadcast(a["L0_attn_bv"])), (T.b_o[:], broadcast(a["L0_attn_bo"])),
             (T.a1_wqkv[:, :, 0:256], ktiles(a["L1_attn_Wq"])), (T.a1_wqkv[:, :, 256:320], ktiles(a["L1_attn_Wk"])),
             (T.a1_wqkv[:, :, 320:384], ktiles(a["L1_attn_Wv"])), (T.a1_wo[:], ktiles(a["L1_attn_Wo"])),
             (T.x1_wq[:], ktiles(a["L1_xattn_Wq"])), (T.x1_wkv[:], a["L1_xattn_Wkv_expand"]),
             (T.x1_wo[:], ktiles(a["L1_xattn_Wout"])), (T.f0_wg[:, :, 0:256], ktiles(a["L0_ffn_W"])),
             (T.f0_wg[:, :, 256:264], ktiles(a["L0_ffn_gate_w"])), (T.f1_gate[:], ktiles(a["L1_ffn_gate_w"])),
             (T.iota[:], broadcast(a["iota"])), (T.lower[:], broadcast(a["lower"]))]
    with ExitStack() as ctx:
        loaded = ctx.enter_context(nc.semaphore("first_loaded"))
        block = ctx.enter_context(nc.Block())

        @block.sync
        def _(sp):
            for dst, src in loads:
                sp.dma_start(dst, src).then_inc(loaded, 16)

        @block.gpsimd
        def _(pool):
            pool.memset(T.wd[64:128, UNITS - LOW:, :, :].rearrange("p u j n -> p (u j n)"), 0.0).then_inc(T.low_cleared, 1)

        @block.scalar
        def _(act):
            act.wait_ge(T.low_cleared, 1)
            T.low_count = load_units(a, T, range(LOW), act, T.low_loaded)

        @block.vector
        def _(dve):
            dve.memset(T.nm[:].bitcast(F32), 0.0)
            dve.memset(T.half[:], -0.5)
            dve.wait_ge(loaded, 16 * len(loads))
            dve.tensor_copy(T.ident_bf[:], T.ident[:])
            for i, m in enumerate((T.mask_qk, T.mask_kq)):
                dve.tensor_copy(m[:].rearrange("p (h k) -> p h k", h=4),
                                T.masks[:, i * 128:(i + 1) * 128].unsqueeze(1).broadcast_to([128, 4, 128]))


def ones_beside_v(nc, T, width):
    with ExitStack() as ctx:
        block = ctx.enter_context(nc.Block())
        heads = 16 if width == 17 else 8

        @block.vector
        def _(dve):
            for par in range(2):
                dve.memset(T.vaug[par][:, 0:heads * width].rearrange("p (h e) -> p h e", e=width)[:, :, width - 1], 1.0)


def sparse_experts(nc, a, T, F, banks):
    ST = NS // 128
    with Stage(nc, "m") as stage, ExitStack() as ctx:
        sem = stage.sem

        loaded = sem("loaded")
        cleared = sem("cleared")
        zeroed = sem("zeroed")
        v = sem("v")
        act = sem("act")
        pe_s = sem("pe")
        eq_ready = sem("eq_ready")
        eq_used = sem("eq_used")
        placed = sem("placed")
        back = sem("back")
        block = ctx.enter_context(nc.Block())
        table = F.table
        bank_t, bank_d, bank_c = banks[0], banks[1], banks[2]

        @block.sync
        def _(sp):
            for dst, src in ((F.eaw[:], a["L0_ffn_expert_atom_weights"]), (F.atoms[:], a["L0_ffn_atoms"]),
                             (F.imp[:], a["importance"]), (F.idx_row[:], broadcast(a["L0_ffn_mask_idx"])),
                             (F.idx_col[:], a["mask_idx_columns"])):
                sp.dma_start(dst, src).then_inc(loaded, 16)
            sp.wait_ge(cleared, 1)
            for j in range(KT):
                sp.dma_start(table[j * 128 * 256:(j + 1) * 128 * 256, :].rearrange("(p r) e -> p (r e)", p=128),
                             F.m_re[:, j, :]).then_inc(zeroed, 16)
            sp.wait_ge(placed, 16 * ST)
            for j in range(KT):
                sp.dma_start(F.m_re[:, j, :], table[j * 128 * 256:(j + 1) * 128 * 256, :]
                             .rearrange("(p r) e -> p (r e)", p=128)).then_inc(back, 16)

        @block.scalar
        def _(eng):
            eng.wait_ge(v, 1)
            eng.activation(F.eaw[:], F.eaw[:], ACT.Exp, bias=F.eawmax[:], accum_out=F.eawsum[:]).then_inc(act, 1)
            eng.activation(F.imp[:], F.imp[:], ACT.Exp, scale=-1.0).then_inc(act, 1)

        @block.tensor
        def _(pe):
            pe.wait_ge(v, 3)
            pe.transpose(bank_t[0:ATOMS, 0:E0], F.eaw[:], T.ident[0:E0, 0:E0]).then_inc(pe_s, 1)
            pe.wait_ge(v, 4)
            for t in range(ST):
                last = pe.matmul(bank_d[:, t * E0:(t + 1) * E0], F.atoms[:, t * 128:(t + 1) * 128], F.eawT[:],
                                 start=True, stop=True)
            last.then_inc(pe_s, 1)
            pe.wait_ge(v, 12)
            for t in range(ST):
                pe.wait_ge(eq_ready, t + 1)
                for u in range(ST):
                    last = pe.matmul(bank_c[:, u * 24:(u + 1) * 24], F.eq[t % 2][:, u * 128:(u + 1) * 128],
                                     F.w3[:, t, :], start=(t == 0 and u == 0), stop=(t == ST - 1), skip_group_check=True)
                last.then_inc(eq_used, 1)

        @block.vector
        def _(dve):
            dve.memset(F.m_re[:], 0.0).then_inc(cleared, 1)
            dve.wait_ge(loaded, 80)
            dve.tensor_reduce(F.eawmax[:], F.eaw[:], AX.X, ALU.max, negate=True).then_inc(v, 1)
            dve.wait_ge(act, 1)
            dve.reciprocal(F.eawsum[:], F.eawsum[:]).then_inc(v, 1)
            dve.wait_ge(v, 2)
            dve.tensor_scalar(F.eaw[:], F.eaw[:], F.eawsum[:], None, ALU.mult).then_inc(v, 1)
            dve.wait_ge(pe_s, 1)
            dve.tensor_copy(F.eawT[:], bank_t[0:ATOMS, 0:E0]).then_inc(v, 1)
            dve.wait_ge(act, 2)
            dve.tensor_scalar(F.imp[:], F.imp[:], 1.0, None, ALU.add).then_inc(v, 1)
            dve.wait_ge(v, 5)
            dve.reciprocal(F.imp[:], F.imp[:]).then_inc(v, 1)
            dve.wait_ge(v, 6)
            dve.wait_ge(pe_s, 2)
            dve.tensor_tensor(F.imp[:], bank_d[:, 0:ST * E0], F.imp[:], ALU.mult).then_inc(v, 1)
            imp = F.imp[:].rearrange("p (t e) -> p t e", e=E0)
            steps = 7
            for part in range(3):
                dve.wait_ge(v, steps)
                dve.tensor_copy(F.w3[:, :, part * 8:(part + 1) * 8], imp).then_inc(v, 1)
                steps += 1
                if part < 2:
                    dve.wait_ge(v, steps)
                    dve.tensor_tensor(imp, imp, F.w3[:, :, part * 8:(part + 1) * 8], ALU.subtract).then_inc(v, 1)
                    steps += 1
            dve.tensor_copy(F.col_f[:], F.idx_col[:]).then_inc(v, 1)
            dve.wait_ge(v, 13)
            for t in range(ST):
                if t >= 2:
                    dve.wait_ge(eq_used, t - 1)
                dve.tensor_scalar(F.eq[t % 2][:], F.idx_row[:], F.col_f[:, t:t + 1], None, ALU.is_equal).then_inc(eq_ready, 1)
            dve.tensor_scalar(F.pos_hi[:], F.idx_col[:], D - 1, 8, ALU.bitwise_and, ALU.logical_shift_left).then_inc(v, 1)
            dve.tensor_scalar(F.pos[:], F.idx_col[:], 8, None, ALU.logical_shift_right).then_inc(v, 1)
            dve.wait_ge(v, 15)
            dve.tensor_tensor(F.pos[:], F.pos[:], F.pos_hi[:], ALU.bitwise_or).then_inc(v, 1)
            dve.wait_ge(eq_used, ST)
            c = bank_c[:, 0:ST * 24].rearrange("p (t s e) -> p t s e", s=3, e=E0)
            dve.tensor_copy(F.sum8[:], c[:, :, 2, :]).then_inc(v, 1)
            for part, n in ((1, 17), (0, 18)):
                dve.wait_ge(v, n)
                dve.tensor_tensor(F.sum8[:], c[:, :, part, :], F.sum8[:], ALU.add).then_inc(v, 1)
            dve.wait_ge(back, 16 * KT)
            for j in range(KT):
                dve.tensor_copy(F.m[:, j, :, :], F.m_re[:, j, :].rearrange("p (r e) -> p e r", e=E0))

        @block.gpsimd
        def _(pool):
            pool.wait_ge(v, 19)
            pool.wait_ge(zeroed, 16 * KT)
            for t in range(ST):
                if t:
                    pool.wait_ge(placed, 16 * t)
                pool.indirect_dma_start(table[:, :], bass.IndirectOffsetOnAxis(ap=F.pos[:, t:t + 1], axis=0),
                                        F.sum8[:, t, :], None).then_inc(placed, 16)


def ffn0(nc, T, F, banks):
    STEPS = 12
    with Stage(nc, "f0") as stage, ExitStack() as ctx:
        sem = stage.sem

        loaded = [sem("loaded0"), sem("loaded1")]
        xt_done = sem("xt_done")
        xt_copied = sem("xt_copied")
        base_done = sem("base_done")
        pair_done = sem("pair_done")
        added = sem("added")
        stat = sem("stat")
        base_used = sem("base_used")
        step = sem("step")
        weight_exp = sem("weight_exp")
        var_done = sem("var_done")
        rstd_done = sem("rstd_done")
        block = ctx.enter_context(nc.Block())
        pairs, base, tr = banks[0:4], banks[4], banks[5]

        @block.sync
        def _(sp):
            def load(t, par):
                sp.dma_start(F.xs[par][:], flat(T.x_all, t)).then_inc(loaded[par], 16)
            load(0, 0)
            load(1, 1)
            with sp.Fori(0, B // 2 - 1) as i:
                for par in range(2):
                    sp.wait_ge(xt_done, i * 2 + (par + 1))
                    load(i * 2 + (par + 2), par)

        @block.tensor
        def _(pe):
            def tile(i, par, first):
                t = i * 2 + par
                pe.wait_ge(loaded[par], i * 16 + 16)
                if not (first and par == 0):
                    pe.wait_ge(xt_copied, t)
                for j in range(KT):
                    last = pe.transpose(tr[:, j * 128:(j + 1) * 128], F.xs[par][:, j * 128:(j + 1) * 128], T.ident[:])
                last.then_inc(xt_done, 1)
                pe.wait_ge(xt_copied, t + 1)
                if not (first and par == 0):
                    pe.wait_ge(base_used, t)
                for j in range(KT):
                    last = pe.matmul(base[:, 0:264], F.xT[par][:, j * 128:(j + 1) * 128], T.f0_wg[:, j, :],
                                     start=(j == 0), stop=(j == KT - 1))
                last.then_inc(base_done, 1)
                for q in range(4):
                    if not (first and par == 0):
                        pe.wait_ge(added, t * E0 + (2 * q + 2 - E0))
                    for j in range(KT):
                        last = pe.matmul(pairs[q][:, :], F.xT[par][:, j * 128:(j + 1) * 128], F.m[:, j, 2 * q:2 * q + 2, :],
                                         start=(j == 0), stop=(j == KT - 1))
                    last.then_inc(pair_done, 1)
            tile(0, 0, True)
            tile(0, 1, True)
            with pe.Fori(1, B // 2) as i:
                tile(i, 0, False)
                tile(i, 1, False)

        @block.scalar
        def _(act):
            with act.Fori(0, B // 2) as i:
                for par in range(2):
                    t = i * 2 + par
                    act.wait_ge(xt_done, t + 1)
                    act.activation(F.xT[par][:], tr[:, 0:256], ACT.Copy).then_inc(xt_copied, 1)
                    act.wait_ge(step, t * STEPS + 3)
                    act.activation(F.wexp[:], F.wdiff[:], ACT.Exp).then_inc(weight_exp, 1)

        @block.gpsimd
        def _(pool):
            with pool.Fori(0, B) as t:
                pool.wait_ge(var_done, t + 1)
                pool.tensor_tensor(T.rstd[:], T.vare[:], T.half[:], ALU.pow).then_inc(rstd_done, 1)

        @block.vector
        def _(dve):
            with dve.Fori(0, B) as t:
                def after(k):
                    dve.wait_ge(step, t * STEPS + k)

                x = flat(T.x_all, t)
                dve.wait_ge(base_done, t + 1)
                dve.tensor_scalar(F.logit[:], base[:, 256:264], -50.0, 50.0, ALU.max, ALU.min).then_inc(step, 1)
                wait_apart(T, dve, step, t * STEPS + 1)
                dve.max(F.top[:], F.logit[:]).then_inc(step, 1)
                after(2)
                dve.tensor_tensor(F.wdiff[:], F.top[:, 1:2], F.top[:, 0:1], ALU.subtract).then_inc(step, 1)
                dve.max_index(F.topi[:], F.top[:], F.logit[:]).then_inc(step, 1)
                after(4)
                dve.tensor_copy(F.topf[:], F.topi[:]).then_inc(step, 1)
                dve.wait_ge(weight_exp, t + 1)
                dve.tensor_scalar(F.p1[:], F.wexp[:], 1.0, None, ALU.add).then_inc(step, 1)
                after(6)
                dve.reciprocal(F.p0[:], F.p1[:]).then_inc(step, 1)
                after(7)
                dve.tensor_tensor(F.p1[:], F.p0[:], F.wexp[:], ALU.mult).then_inc(step, 1)
                dve.tensor_scalar(F.rw[:], T.iota[:, 0:E0], F.topf[:, 0:1], F.p0[:], ALU.is_equal, ALU.mult).then_inc(step, 1)
                after(9)
                dve.tensor_scalar(F.rw1[:], T.iota[:, 0:E0], F.topf[:, 1:2], F.p1[:], ALU.is_equal, ALU.mult).then_inc(step, 1)
                after(10)
                dve.tensor_tensor(F.rw[:], F.rw[:], F.rw1[:], ALU.add).then_inc(step, 1)
                dve.tensor_tensor(F.acc[:, 0, :], base[:, 0:256], x, ALU.add).then_inc(base_used, 1)
                dve.wait_ge(base_used, t + 1)
                after(11)
                for e in range(E0):
                    if e % 2 == 0:
                        dve.wait_ge(pair_done, t * 4 + (e // 2 + 1))
                    if e:
                        dve.wait_ge(added, t * E0 + e)
                    dve.scalar_tensor_tensor(F.acc[:, (e + 1) % 2, :], pairs[e // 2][:, (e % 2) * 256:(e % 2 + 1) * 256],
                                                   F.rw[:, e:e + 1], F.acc[:, e % 2, :], ALU.mult, ALU.add).then_inc(added, 1)
                acc = F.acc[:, 0, :]
                dve.wait_ge(added, (t + 1) * E0)
                dve.bn_stats(T.stats[:], acc).then_inc(stat, 1)
                wait_apart(T, dve, stat, t * 2 + 1)
                dve.bn_aggr(T.mv[:], T.stats[:]).then_inc(stat, 1)
                dve.wait_ge(stat, t * 2 + 2)
                dve.tensor_scalar(T.vare[:], T.mv[:, 1:2], EPS, None, ALU.add).then_inc(var_done, 1)
                dve.wait_ge(rstd_done, t + 1)
                dve.tensor_scalar(x, acc, T.mv[:, 0:1], T.rstd[:], ALU.subtract, ALU.mult).then_inc(step, 1)


def route(nc, a, T, G, banks):
    with Stage(nc, "r") as stage, ExitStack() as ctx:
        sem = stage.sem

        xt_done = sem("xt_done")
        xt_copied = sem("xt_copied")
        logits_done = sem("logits_done")
        exp_done = sem("exp_done")
        step = sem("step")
        block = ctx.enter_context(nc.Block())
        tr, logits = banks[0:2], banks[2]

        @block.gpsimd
        def _(pool):
            pool.memset(T.wd[64:128, 0:UNITS - LOW, :, :].rearrange("p u j n -> p (u j n)"), 0.0).then_inc(T.high_cleared, 1)

        @block.sync
        def _(sp):
            sp.wait_ge(T.high_cleared, 1)
            T.high_count = load_units(a, T, range(LOW, UNITS), sp, T.high_loaded)

        @block.tensor
        def _(pe):
            for t in range(B):
                if t >= 2:
                    pe.wait_ge(xt_copied, t - 1)
                for j in range(KT):
                    last = pe.transpose(tr[t % 2][:, j * 128:(j + 1) * 128], T.x_all[:, t, j * 128:(j + 1) * 128], T.ident[:])
                last.then_inc(xt_done, 1)
            for t in range(B):
                pe.wait_ge(xt_copied, t + 1)
                for j in range(KT):
                    last = pe.matmul(logits[:, t * E1:(t + 1) * E1], G.xT[:, t, j * 128:(j + 1) * 128], T.f1_gate[:, j, :],
                                     start=(j == 0), stop=(j == KT - 1))
            last.then_inc(logits_done, 1)

        @block.scalar
        def _(act):
            for t in range(B):
                act.wait_ge(xt_done, t + 1)
                act.activation(G.xT[:, t, :], tr[t % 2][:, 0:256], ACT.Copy).then_inc(xt_copied, 1)
            act.wait_ge(logits_done, 1)
            act.activation(G.score[:], logits[:, 0:B * E1], ACT.Exp, scale=-1.0).then_inc(exp_done, 1)

        @block.vector
        def _(dve):
            done = 0

            def then(ins):
                nonlocal done
                done += 1
                ins.then_inc(step, 1)
                dve.wait_ge(step, done)

            dve.wait_ge(exp_done, 1)
            then(dve.tensor_scalar(G.score[:], G.score[:], 1.0, None, ALU.add))
            then(dve.reciprocal(G.score[:], G.score[:]))
            grouped_scores = G.score[:].rearrange("p (t g e) -> p t g e", t=B, g=GROUPS)
            then(dve.tensor_reduce(G.gmax[:], grouped_scores, AX.X, ALU.max))
            this = G.gmax[:].unsqueeze(3).broadcast_to([128, B, GROUPS, GROUPS])
            other = G.gmax[:].unsqueeze(2).broadcast_to([128, B, GROUPS, GROUPS])
            then(dve.tensor_tensor(G.before[:], other, this, ALU.is_gt))
            then(dve.tensor_tensor(G.tied[:], other, this, ALU.is_equal))
            lower = T.lower[:].rearrange("p (g h) -> p g h", g=GROUPS).unsqueeze(1).broadcast_to([128, B, GROUPS, GROUPS])
            then(dve.tensor_tensor(G.tied[:], G.tied[:], lower, ALU.mult))
            then(dve.tensor_tensor(G.before[:], G.before[:], G.tied[:], ALU.add))
            then(dve.tensor_reduce(G.rank[:], G.before[:], AX.X, ALU.add))
            then(dve.tensor_scalar(G.rank[:], G.rank[:], float(TOP_GROUPS), None, ALU.is_lt))
            allowed = G.rank[:].unsqueeze(3).broadcast_to([128, B, GROUPS, E1 // GROUPS])
            masked = G.masked[:].rearrange("p (t g e) -> p t g e", t=B, g=GROUPS)
            then(dve.tensor_scalar(G.masked[:], G.score[:], 1.0, None, ALU.add))
            then(dve.tensor_tensor(masked, masked, allowed, ALU.mult))
            then(dve.tensor_scalar(G.masked[:], G.masked[:], -1.0, None, ALU.add))
            for t in range(B):
                then(dve.max(G.top[:, t, :], G.masked[:, t * E1:(t + 1) * E1]))
                then(dve.max_index(G.topi[:, t, :], G.top[:, t, :], G.masked[:, t * E1:(t + 1) * E1]))
            then(dve.tensor_copy(G.topf[:], G.topi[:]))
            experts = T.iota[:, 0:E1].unsqueeze(1).broadcast_to([128, B, E1])
            chosen = G.masked[:].rearrange("p (t e) -> p t e", t=B)
            for k in range(TOP):
                index = G.topf[:, :, k:k + 1].broadcast_to([128, B, E1])
                then(dve.tensor_tensor((G.hit if k else chosen)[:], experts, index, ALU.is_equal))
                if k:
                    then(dve.tensor_tensor(chosen, chosen, G.hit[:], ALU.add))
            scores = G.score[:].rearrange("p (t e) -> p t e", t=B)
            then(dve.tensor_tensor(chosen, chosen, scores, ALU.mult))
            then(dve.tensor_reduce(G.total[:], chosen, AX.X, ALU.add))
            then(dve.reciprocal(G.total[:], G.total[:]))
            then(dve.tensor_tensor(G.w[:, :, 0:E1], chosen, G.total[:].unsqueeze(2).broadcast_to([128, B, E1]), ALU.mult))
            dve.memset(G.w[:, :, E1:UNITS], 1.0)


LOW = 18


def load_units(a, T, units, eng, sem):
    lo, hi = units.start, min(units.stop, E1)
    n = hi - lo
    for j in range(KT):
        rows = slice(j * 128, (j + 1) * 128)
        eng.dma_start(T.wgu[:, lo:hi, j, 0:MI], a["L1_ffn_w_gate"][lo:hi, rows, :].rearrange("e p m -> p e m")).then_inc(sem, 16)
        eng.dma_start(T.wgu[:, lo:hi, j, MI:2 * MI], a["L1_ffn_w_up"][lo:hi, rows, :].rearrange("e p m -> p e m")).then_inc(sem, 16)
    for e in range(lo, hi):
        eng.dma_start(T.wd[0:MH, UNITS - 1 - e, :, :], a["L1_ffn_w_down"][e].rearrange("(j p) n -> p j n", p=MH)).then_inc(sem, 16)
    count = 2 * KT + n
    for u in range(hi, units.stop):
        m = slice((u - E1) * MI, (u - E1 + 1) * MI)
        eng.dma_start(T.wgu[:, u, :, 0:MI], ktiles(a["L1_ffn_sw_gate"][:, m])).then_inc(sem, 16)
        eng.dma_start(T.wgu[:, u, :, MI:2 * MI], ktiles(a["L1_ffn_sw_up"][:, m])).then_inc(sem, 16)
        eng.dma_start(T.wd[0:MH, UNITS - 1 - u, :, :], a["L1_ffn_sw_down"][m, :].rearrange("(j p) n -> p j n", p=MH)).then_inc(sem, 16)
        count += 3
    return 16 * count


def experts(nc, a, T, G, banks, out):
    with Stage(nc, "e") as stage, ExitStack() as ctx:
        sem = stage.sem

        zero = sem("zero")
        gu_done = sem("gu_done")
        sil_ready = sem("sil_ready")
        h_ready = sem("h_ready")
        tr_done = sem("tr_done")
        ht_ready = sem("ht_ready")
        down_done = sem("down_done")
        res = sem("res")
        stat = sem("stat")
        rstd_done = sem("rstd_done")
        stored = sem("stored")
        block = ctx.enter_context(nc.Block())
        acc, gu, tr = banks[0:4], banks[4:6], banks[6:8]
        LAST = UNITS - 1

        @block.gpsimd
        def _(pool):
            pool.wait_ge(res, 17)
            pool.tensor_tensor(G.rstd[:], G.vare[:], T.half[:, 0:1].broadcast_to([128, B]), ALU.pow).then_inc(rstd_done, 1)

        @block.sync
        def _(sp):
            for t in range(B):
                sp.wait_ge(res, 17 + t + 1)
                sp.dma_start(out[t, :, :], T.x_all[:, t, :]).then_inc(stored, 16)
            sp.wait_ge(stored, 16 * B)

        @block.tensor
        def _(pe):
            def gate_up(e, t, first=False):
                u = e * B + t
                if not first:
                    pe.wait_ge(h_ready, u - 1)
                for j in range(KT):
                    last = pe.matmul(gu[t % 2][:, 0:2 * MI], G.xT[:, t, j * 128:(j + 1) * 128],
                                     T.wgu[:, bass.ds(e, 1), j, :].rearrange("p a n -> p (a n)"), start=(j == 0), stop=(j == KT - 1))
                last.then_inc(gu_done, 1)

            def transpose_h(e, t, first=False):
                u = e * B + t
                pe.wait_ge(h_ready, u + 1)
                if not first:
                    pe.wait_ge(ht_ready, u if t == 1 else u - 1)
                for j in range(2):
                    last = pe.transpose(tr[t % 2][0:MH, j * 128:(j + 1) * 128], G.h[t % 2][:, j * MH:(j + 1) * MH], T.ident[:])
                last.then_inc(tr_done, 1)

            def down(e, t):
                u = e * B + t
                pe.wait_ge(ht_ready, u + 1)
                for j in range(2):
                    last = pe.matmul(acc[t // 2][:, (t % 2) * 256:(t % 2 + 1) * 256], G.hT[t % 2][:, j * 128:(j + 1) * 128],
                                     T.wd[:, bass.ds(e * -1 + LAST, 1), j, :].rearrange("p a n -> p (a n)"),
                                     start=False, stop=True, skip_group_check=True)
                return last

            def unit(e, final):
                for t in range(B):
                    if t < B - 2:
                        gate_up(e, t + 2)
                    elif not final:
                        gate_up(e + 1, t + 2 - B)
                    if t < B - 1:
                        transpose_h(e, t + 1)
                    elif not final:
                        transpose_h(e + 1, 0)
                    last = down(e, t)
                if final:
                    last.then_inc(down_done, 1)

            pe.wait_ge(zero, 4 + 2)
            pe.wait_ge(T.low_loaded, T.low_count)
            pe.wait_ge(T.high_loaded, T.high_count)
            gate_up(0, 0, True)
            gate_up(0, 1, True)
            transpose_h(0, 0, True)
            with pe.Fori(0, LAST) as e:
                unit(e, False)
            unit(LAST, True)

        @block.scalar
        def _(act):
            def silu(e, t):
                act.wait_ge(gu_done, e * B + (t + 1))
                act.activation(G.sil[t % 2][:], gu[t % 2][:, 0:MI], ACT.Silu).then_inc(sil_ready, 1)

            def copy_ht(e, t):
                act.wait_ge(tr_done, e * B + (t + 1))
                act.activation(G.hT[t % 2][0:MH, :], tr[t % 2][0:MH, 0:256], ACT.Copy).then_inc(ht_ready, 1)

            def unit(e, final):
                for t in range(B):
                    if t < B - 2:
                        silu(e, t + 2)
                    elif not final:
                        silu(e + 1, t + 2 - B)
                    if t < B - 1:
                        copy_ht(e, t + 1)
                    elif not final:
                        copy_ht(e + 1, 0)

            act.wait_ge(zero, 6)
            silu(0, 0)
            silu(0, 1)
            copy_ht(0, 0)
            with act.Fori(0, LAST) as e:
                unit(e, False)
            unit(LAST, True)

        @block.vector
        def _(dve):
            for bank in acc:
                dve.memset(bank[:], 0.0).then_inc(zero, 1)
            for par in range(2):
                dve.memset(G.hT[par][64:128, :], 0.0).then_inc(zero, 1)

            with dve.Fori(0, UNITS) as e:
                for t in range(B):
                    u = e * B + t
                    dve.wait_ge(sil_ready, u + 1)
                    dve.scalar_tensor_tensor(G.h[t % 2][:], gu[t % 2][:, MI:2 * MI],
                                             G.w[:, t, bass.ds(e, 1)], G.sil[t % 2][:], ALU.mult, ALU.mult).then_inc(h_ready, 1)
            dve.wait_ge(down_done, 1)
            for t in range(B):
                dve.tensor_tensor(T.x_all[:, t, :], acc[t // 2][:, (t % 2) * 256:(t % 2 + 1) * 256], T.x_all[:, t, :], ALU.add).then_inc(res, 1)
            for t in range(B):
                dve.wait_ge(res, t + 1)
                dve.bn_stats(G.stats[:, t, :], T.x_all[:, t, :]).then_inc(stat, 1)
            for t in range(B):
                dve.wait_ge(stat, t + 1)
                dve.bn_aggr(G.mv[:, t, :], G.stats[:, t, :]).then_inc(res, 1)
            dve.wait_ge(res, 16)
            dve.tensor_scalar(G.vare[:], G.mv[:, :, 1], EPS, None, ALU.add).then_inc(res, 1)
            dve.wait_ge(rstd_done, 1)
            dve.wait_ge(res, 17)
            for t in range(B):
                dve.tensor_scalar(T.x_all[:, t, :], T.x_all[:, t, :], G.mv[:, t, 0:1], G.rstd[:, t:t + 1],
                                  ALU.subtract, ALU.mult).then_inc(res, 1)


def store(nc, T, out):
    with ExitStack() as c2:
        st = c2.enter_context(nc.semaphore("st"))
        block = c2.enter_context(nc.Block())

        @block.sync
        def _(sp):
            sp.wait_ge(T.low_loaded, T.low_count)
            sp.dma_start(out.rearrange("b p c -> p b c"), T.x_all[:]).then_inc(st, 16)
            sp.wait_ge(st, 16)


STAGES = ("a0", "x0", "f0", "a1", "x1", "f1")


def decoder(nc, a, out):
    with ExitStack() as ctx:
        T, F, G = Tensors(), Tensors(), Tensors()
        banks = [ctx.enter_context(nc.psum_tensor(f"bank{i}", [128, 512], F32)) for i in range(8)]
        T.SB, T.STB, T.PV, T.PA, T.PB, T.M = banks[0:2], banks[2:4], banks[4], banks[5], banks[6], banks[7]
        start = (nc.sbuf_base + 31) // 32 * 32
        end = nc.sbuf_usable_end // 32 * 32
        weights = UNITS * (2 * KT * MI + 2 * D) * 4
        keep = Memory(nc, start, end - weights)
        units = Memory(nc, end - weights, end)
        T.wgu = units("wgu", [128, UNITS, KT, 2 * MI])
        middle = units.at
        T.wd = units("wd", [128, UNITS, 2, D])

        T.x_all = keep("x_all", [128, B, D])
        T.ident = keep("ident", [128, 128])
        T.half = keep("half", [128, 1])
        T.iota = keep("iota", [128, E1])
        T.lower = keep("lower", [128, GROUPS * GROUPS])
        T.f1_gate = keep("f1_gate", [128, KT, E1])
        T.rstd, T.vare = keep("rstd", [128, 1]), keep("vare", [128, 1])
        T.stats, T.mv = keep("stats", [128, 6]), keep("mv", [128, 2])
        kept = keep.at

        G.xT = keep("g_xT", [128, B, D])
        G.w = keep("g_w", [128, B, UNITS])
        G.score, G.masked = keep("g_score", [128, B * E1]), keep("g_masked", [128, B * E1])
        G.hit = keep("g_hit", [128, B, E1])
        G.gmax, G.rank = keep("g_gmax", [128, B, GROUPS]), keep("g_rank", [128, B, GROUPS])
        G.before, G.tied = keep("g_before", [128, B, GROUPS, GROUPS]), keep("g_tied", [128, B, GROUPS, GROUPS])
        G.top, G.topi, G.topf = keep("g_top", [128, B, 8]), keep("g_topi", [128, B, 8], U32), keep("g_topf", [128, B, 8])
        G.total = keep("g_total", [128, B])
        G.sil = [keep(f"g_sil{i}", [128, MI]) for i in range(2)]
        G.h = [keep(f"g_h{i}", [128, MI]) for i in range(2)]
        G.hT = [keep(f"g_hT{i}", [128, 256]) for i in range(2)]
        G.stats, G.mv = keep("g_stats", [128, B, 6]), keep("g_mv", [128, B, 2])
        G.vare, G.rstd = keep("g_vare", [128, B]), keep("g_rstd", [128, B])

        shared_start = middle - (UNITS - LOW) * KT * 2 * MI * 4
        shared_end = middle + (UNITS - LOW) * 2 * D * 4
        early = Memory(nc, kept, end - weights)
        at = Memory(nc, shared_start, shared_end)
        T.masks, T.blockmask, T.rope = early("masks", [128, 256]), early("blockmask", [128, 12]), early("rope", [128, 16])
        T.onerows = early("onerows", [128, 24])
        T.ident_bf = early("ident_bf", [128, 128], BF16)
        T.mask_qk, T.mask_kq = early("mask_qk", [128, 512], BF16), early("mask_kq", [128, 512], BF16)
        T.b_qk, T.b_v, T.b_o = early("b_qk", [128, 512]), early("b_v", [128, 256]), early("b_o", [128, 256])
        T.a0_wqk, T.a0_wv, T.a0_wo = early("a0_wqk", [128, KT, 512]), early("a0_wv", [128, KT, 256]), early("a0_wo", [128, KT, 256])
        T.a1_wqkv, T.a1_wo = early("a1_wqkv", [128, KT, 384]), early("a1_wo", [128, KT, 256])
        T.x1_wq, T.x1_wkv, T.x1_wo = early("x1_wq", [128, KT, 256]), early("x1_wkv", [CTX, 512]), early("x1_wo", [128, KT, 256])
        T.wo = {"a0": T.a0_wo, "a1": T.a1_wo, "x1": T.x1_wo}
        T.f0_wg = early("f0_wg", [128, KT, 264])
        T.nm, T.nmf = at("nm", [128, 4, 128], F32R), at("nmf", [128, 4, 8])
        ff = Memory(nc, at.at, shared_end)
        T.kb1, T.kb2 = ([at(f"{n}_{i}", [128, 16, 128], F32R) for i in range(2)] for n in ("kb1", "kb2"))
        T.q1, T.q2 = ([at(f"{n}_{i}", [128, 4, 128], F32R) for i in range(2)] for n in ("q1", "q2"))
        T.qs, T.ks1, T.ks2 = at("qs", [128, 4, 128], F32R), at("ks1", [128, 4, 128], F32R), at("ks2", [128, 4, 64], F32R)
        T.pt = [at(f"pt{i}", [128, 512]) for i in range(2)]
        T.xs = [at(f"xs{i}", [128, D]) for i in range(2)]
        T.cs = [at(f"cs{i}", [128, CTX]) for i in range(2)]
        T.vaug = [at(f"vaug{i}", [128, 16 * 17]) for i in range(2)]
        T.xT, T.qk = at("xT", [128, 384]), at("qk", [128, 512])
        T.att, T.atT, T.rec, T.res, T.xb = at("att", [128, D]), at("atT", [128, D]), at("rec", [128, 32]), at("res", [128, D]), at("xb", [128, D])
        T.rope_a, T.rope_b = at("rope_a", [128, 320]), at("rope_b", [128, 320])
        T.ctx_tiles = a["ctx_512"]

        ST = NS // 128
        F.table = nc.dram_tensor("sparse_table", [D * D, E0], F32).ap()
        F.m = ff("f_m", [128, KT, E0, D])
        own = ff.at
        F.m_re = ff("f_m_re", [128, KT, D * E0])
        F.eaw, F.eawmax, F.eawsum = ff("f_eaw", [E0, ATOMS]), ff("f_eawmax", [E0, 1]), ff("f_eawsum", [E0, 1])
        F.atoms, F.eawT, F.imp = ff("f_atoms", [ATOMS, NS]), ff("f_eawT", [ATOMS, E0]), ff("f_imp", [128, ST * E0])
        F.idx_row, F.idx_col = ff("f_idx_row", [128, NS], I32), ff("f_idx_col", [128, ST], I32)
        F.col_f = ff("f_col_f", [128, ST])
        F.pos_hi, F.pos = ff("f_pos_hi", [128, ST], I32), ff("f_pos", [128, ST], I32)
        F.w3, F.sum8 = ff("f_w3", [128, ST, 3 * E0], BF16), ff("f_sum8", [128, ST, E0])
        F.eq = [ff(f"f_eq{i}", [128, NS], BF16) for i in range(2)]
        own = Memory(nc, own, shared_end)
        F.xs = [own(f"f_xs{i}", [128, D]) for i in range(2)]
        F.xT = [own(f"f_xT{i}", [128, D]) for i in range(2)]
        F.acc = own("f_acc", [128, 2, D])
        F.logit, F.top, F.topi, F.topf = own("f_logit", [128, 8]), own("f_top", [128, 8]), own("f_topi", [128, 8], U32), own("f_topf", [128, 8])
        F.wdiff, F.wexp, F.p0, F.p1 = (own(n, [128, 1]) for n in ("f_wdiff", "f_wexp", "f_p0", "f_p1"))
        F.rw, F.rw1 = own("f_rw", [128, 8]), own("f_rw1", [128, 8])

        T.passed, T.low_loaded, T.low_cleared, T.high_loaded, T.high_cleared = (
            ctx.enter_context(nc.semaphore(n)) for n in ("passed", "low_loaded", "low_cleared", "high_loaded", "high_cleared"))
        load_first(nc, a, T)
        if "a0" in STAGES:
            ones_beside_v(nc, T, 17)
            attention(nc, ATTN0, T)
        if "x0" in STAGES:
            ones_beside_v(nc, T, 9)
            attention(nc, CROSS0, T)
        if "f0" in STAGES:
            sparse_experts(nc, a, T, F, banks)
            ffn0(nc, T, F, banks)
        if "a1" in STAGES:
            ones_beside_v(nc, T, 9)
            attention(nc, ATTN1, T)
        if "x1" in STAGES:
            ones_beside_v(nc, T, 17)
            attention(nc, CROSS1, T)
        if "f1" in STAGES:
            route(nc, a, T, G, banks)
            experts(nc, a, T, G, banks, out)
        else:
            store(nc, T, out)


def constants():
    q, k = np.arange(128)[:, None], np.arange(128)[None, :]
    masks = np.concatenate([np.where(k > q, MASKED, 0.0), np.where(q > k, MASKED, 0.0)], 1).astype(np.float32)
    row = np.arange(128)[:, None] % 64
    blockmask = np.concatenate([row // 8 == np.arange(8), row // 16 == np.arange(4)], 1).astype(np.float32)
    onerows = np.zeros((128, 24), np.float32)
    for j in range(8):
        onerows[[MAX_HI + j, MAX_LO + j], j] = 1.0
        if j < 4:
            onerows[[[MAX_HI + j], [MAX_LO + j]], 8 + j + 4 * np.arange(4)] = 1.0
    freq = (1.0 / 10000.0 ** (np.arange(0, 8, 2, dtype=np.float32) / 8)).astype(np.float32)
    ang = np.arange(128, dtype=np.float32)[:, None] * freq[None, :]
    cos, sin = np.cos(ang), np.sin(ang)
    rope = np.concatenate([cos, cos, -sin, sin], 1).astype(np.float32)
    g = np.arange(GROUPS)
    return {"ident": np.eye(128, dtype=np.float32), "masks": masks, "blockmask": blockmask,
            "onerows": onerows, "rope": rope,
            "iota": np.arange(E1, dtype=np.float32),
            "lower": (g[None, :] < g[:, None]).astype(np.float32).reshape(-1)}


TRANSPOSED = ("L0_attn_Wq", "L0_attn_Wk", "L0_attn_Wv", "L0_attn_Wo", "L1_attn_Wk", "L1_attn_Wv", "L1_attn_Wo",
              "L1_xattn_Wq", "L1_xattn_Wkv_expand", "L1_xattn_Wout", "L0_ffn_W", "L0_ffn_gate_w")


def layout(inputs):
    a = {k: np.asarray(v) for k, v in inputs.items()}
    for name in TRANSPOSED:
        a[name] = a[name].T
    a["L1_attn_Wq"] = a["L1_attn_Wq"].reshape(8, 4, 8, D).transpose(1, 0, 2, 3).reshape(D, D).T
    a["importance"] = a.pop("L0_ffn_importance").reshape(E0, NS // 128, 128).transpose(2, 1, 0).reshape(128, -1)
    a["mask_idx_columns"] = a["L0_ffn_mask_idx"].reshape(NS // 128, 128).T
    a = {k: np.ascontiguousarray(v) for k, v in a.items()}
    a.update(constants())
    return a


def kernel(**inputs):
    import concourse.bacc as bacc
    from concourse.bass_utils import run_bass_kernel_spmd

    nc = bacc.Bacc("TRN2", target_bir_lowering=False, num_devices=1)
    arrays = {f"in_{k}": v for k, v in layout(inputs).items()}
    aps = {k[3:]: nc.dram_tensor(k, v.shape, mybir.dt.from_np(v.dtype), kind="ExternalInput").ap() for k, v in arrays.items()}
    out = nc.dram_tensor("out", (B, S, D), F32, kind="ExternalOutput").ap()
    decoder(nc, aps, out)
    return run_bass_kernel_spmd(nc, [arrays], core_ids=[0]).results[0]["out"]
```

```python
from contextlib import ExitStack

import numpy as np

import concourse.bass as bass
from concourse import mybir

F32 = mybir.dt.float32
F32R = mybir.dt.float32r
BF16 = mybir.dt.bfloat16
I32 = mybir.dt.int32
U32 = mybir.dt.uint32
ALU = mybir.AluOpType
ACT = mybir.ActivationFunctionType
AX = mybir.AxisListType

B, S, D = 8, 128, 256
KT = D // 128
CTX = 64
EPS = 1e-5
HEAD_ROWS = 64
MAX_HI, MAX_LO = 64, 72
MAX_END = 80
MASKED = -1e30
E0, ATOMS, NS = 8, 64, 2048
E1, TOP, MI = 32, 6, 176
GROUPS, TOP_GROUPS = 4, 2
UNITS = E1 + 2
MH = MI // 2
LEAD = 2


class Cfg:

    def __init__(self, name, wide, causal, scale, own_kv, project, rope, bias, out):
        self.name, self.causal, self.scale = name, causal, scale
        self.wide = wide
        self.own_kv, self.project, self.rope, self.bias, self.out = own_kv, project, rope, bias, out
        self.quads = 4 if wide else 8
        self.blocks = 16 if wide else 8
        self.kv_heads = 16 if wide else 8
        self.d = 16 if wide else 8
        self.kcols = 4 if wide else 1
        self.rows = self.quads * (self.d + 1)

    def values(self, vaug):
        step = self.kv_heads // self.quads * self.rows
        v = vaug[:, 0:self.quads * (step + self.d + 1)].rearrange("p (i z) -> p i z", i=self.quads)
        if self.wide:
            return v[:, :, 0:step].rearrange("p i (j r) -> p i j r", r=self.rows)[:, :, :, 0:self.d + 1]
        return v[:, :, 0:self.d + 1]

    def heads(self, v):
        if self.wide:
            return v.rearrange("p (i j e) -> p i j e", i=4, e=self.d)
        return v.rearrange("p (i e) -> p i e", e=self.d)


ATTN0 = Cfg("a0", True, True, 0.25, True, True, False, True, True)
CROSS0 = Cfg("x0", False, False, 8.0 ** -0.5, False, False, False, False, False)
ATTN1 = Cfg("a1", False, True, 8.0 ** -0.5, True, True, True, False, True)
CROSS1 = Cfg("x1", True, True, 0.25, False, True, False, False, True)


def wait_apart(T, eng, sem, value):
    eng.wait_ge(sem, value)
    eng.sem_inc(T.passed, 1)


class Stage:

    def __init__(self, nc, prefix):
        self.nc, self.prefix, self.sems = nc, prefix, []

    def sem(self, name):
        self.sems.append(self.nc.alloc_semaphore(f"{self.prefix}_{name}"))
        return self.sems[-1]

    def __enter__(self):
        return self

    def __exit__(self, *failed):
        if not failed[0]:
            self.nc.clear_and_free_semaphores(self.sems)
            self.nc.all_engine_barrier()


def attention(nc, cfg, T):
    NQ, d, KVH = cfg.quads, cfg.d, cfg.kv_heads
    HEADS = 16 if cfg.wide else 32
    R = cfg.rows
    with Stage(nc, cfg.name) as stage, ExitStack() as ctx:
        sem = stage.sem

        loaded = [sem("loaded0"), sem("loaded1")]
        xt_done = sem("xt_done")
        xt_copied = sem("xt_copied")
        proj_done = sem("proj_done")
        qk_copied = sem("qk_copied")
        v_copied = sem("v_copied")
        t2_done = sem("t2_done")
        t2_low_done = sem("t2_low_done")
        rounded = sem("rounded")
        split = sem("split")
        q_ready = sem("q_ready")
        q_clear = sem("q_clear")
        k_ready = sem("k_ready")
        k2_ready = sem("k2_ready")
        ones_set = sem("ones_set")
        s_done = sem("s_done")
        max_done = sem("max_done")
        nm_hi = sem("nm_hi")
        nm_split = sem("nm_split")
        nm_done = sem("nm_done")
        nm_ready = sem("nm_ready")
        st_done = sem("st_done")
        exp_done = sem("exp_done")
        pv_done = sem("pv_done")
        pv_copied = sem("pv_copied")
        pv_ready = sem("pv_ready")
        rec_done = sem("rec_done")
        att_ready = sem("att_ready")
        at_done = sem("at_done")
        at_copied = sem("at_copied")
        out_done = sem("out_done")
        bias_done = sem("bias_done")
        res_done = sem("res_done")
        stat_done = sem("stat_done")
        aggr_done = sem("aggr_done")
        var_done = sem("var_done")
        rstd_done = sem("rstd_done")
        ln_done = sem("ln_done")
        permuted = sem("permuted")
        rope_a = sem("rope_a")

        block = ctx.enter_context(nc.Block())
        PA, PB, M, PV = T.PA, T.PB, T.M, T.PV
        SB, STB = T.SB, T.STB

        @block.sync
        def _(sp):
            def load(n, par):
                if cfg.project:
                    sp.dma_start(T.xs[par][:], T.x_all[:, bass.ds(n, 1), :].rearrange("p a c -> p (a c)")).then_inc(loaded[par], 16)
                if not cfg.own_kv:
                    sp.dma_start(T.cs[par][:], T.ctx_tiles[bass.ds(n, 1), :, :].rearrange("a p c -> p (a c)")).then_inc(loaded[par], 16)

            load(0, 0)
            load(1, 1)
            with sp.Fori(1, B // 2) as i:
                for par in range(2):
                    if cfg.project:
                        sp.wait_ge(xt_done, i * 2 + (par - 1))
                    else:
                        sp.wait_ge(v_copied, i * 2 + (par - 1))
                        sp.wait_ge(split, i * 2 + (par - 1))
                    load(i * 2 + par, par)

        per_load = 16 if cfg.own_kv or not cfg.project else 32

        def wait_loaded(eng, n, par):
            if isinstance(n, int):
                eng.wait_ge(loaded[par], (n // 2 + 1) * per_load)
            else:
                eng.wait_ge(loaded[par], (n + (2 - par)) * (per_load // 2))

        def all_batches(eng, iteration):
            iteration(0, 0, False, True, True)
            iteration(1, 1, True, True, True)
            with eng.Fori(1, B // 2 - 1) as i:
                iteration(i * 2, 0, True, True, True)
                iteration(i * 2 + 1, 1, True, True, True)
            iteration(B - 2, 0, True, True, False)
            iteration(B - 1, 1, True, False, False)

        @block.tensor
        def _(pe):
            def transpose_x(n, par):
                wait_loaded(pe, n, par)
                if not (isinstance(n, int) and n == 0):
                    pe.wait_ge(q_ready, n)
                for j in range(KT):
                    last = pe.transpose(PA[:, j * 128:(j + 1) * 128], T.xs[par][:, j * 128:(j + 1) * 128], T.ident[:])
                if not cfg.own_kv:
                    last = pe.transpose(PA[0:CTX, 256:384], T.cs[par][:], T.ident[:])
                last.then_inc(xt_done, 1)

            def project(n):
                pe.wait_ge(xt_copied, n + 1)
                if not (isinstance(n, int) and n == 0):
                    pe.wait_ge(k_ready, n)
                if cfg is ATTN0:
                    parts = [(PA[:, 0:512], T.a0_wqk), (PB[:, 0:256], T.a0_wv)]
                elif cfg is ATTN1:
                    parts = [(PA[:, 0:320], T.a1_wqkv[:, :, 0:320]), (PB[:, 0:64], T.a1_wqkv[:, :, 320:384])]
                else:
                    parts = [(PB[:, 0:256], T.x1_wq)]
                    pe.matmul(PA[:, 0:512], T.xT[0:CTX, 256:384], T.x1_wkv[0:CTX, :], start=True, stop=True)
                for out, w in parts:
                    for j in range(KT):
                        last = pe.matmul(out, T.xT[:, j * 128:(j + 1) * 128], w[:, j, :], start=(j == 0), stop=(j == KT - 1))
                last.then_inc(proj_done, 1)

            def transpose_qk(n):
                pe.wait_ge(rounded, n + 1)
                pe.wait_ge(split, n + 1)
                pe.wait_ge(v_copied, n + 1)
                if not cfg.project and not (isinstance(n, int) and n == 0):
                    pe.wait_ge(q_ready, n)
                    pe.wait_ge(k_ready, n)
                pe.sem_inc(T.passed, 1)
                for g in range(4):
                    pe.transpose(PA[:, g * 128:(g + 1) * 128], T.qs[:, g, :].bitcast(F32), T.ident[:])
                for c in range(cfg.kcols):
                    last = pe.transpose(PB[:, c * 128:(c + 1) * 128], T.ks1[:, c, :].bitcast(F32), T.ident[:])
                last.then_inc(t2_done, 1)

            def transpose_k_low(n):
                if not (isinstance(n, int) and n == 0):
                    wait_apart(T, pe, nm_ready, n)
                for c in range(cfg.kcols):
                    last = pe.transpose(M[0:64, c * 128:(c + 1) * 128], T.ks2[:, c, :].bitcast(F32), T.ident[:])
                last.then_inc(t2_low_done, 1)

            def scores(n, par, i):
                if i == 0:
                    pe.wait_ge(q_ready, n + 1)
                    pe.wait_ge(q_clear, n + 1)
                    pe.wait_ge(k_ready, n + 1)
                    pe.wait_ge(k2_ready, n + 1)
                    if isinstance(n, int) and n == 0:
                        pe.wait_ge(ones_set, 2)
                if not (isinstance(n, int) and n == 0 and i < 2):
                    pe.wait_ge(max_done, n * NQ + (i - 1))
                bank = SB[i % 2]
                if cfg.causal:
                    pe.matmul(bank[:, :], T.ident_bf[:], T.mask_qk[:], start=True, stop=False)
                g = i if cfg.wide else i // 2
                blocks = slice(4 * i, 4 * i + 4) if cfg.wide else slice(4 * (i % 2), 4 * (i % 2) + 4)
                pe.matmul(bank[:, :], T.q1[par][:, g, :], T.kb1[par][:, blocks, :], start=not cfg.causal, stop=False)
                pe.matmul(bank[:, :], T.q2[par][:, g, :], T.kb2[par][:, blocks, :], start=False, stop=True).then_inc(s_done, 1)

            def transpose_maxima(n):
                pe.wait_ge(nm_split, n + 1)
                pe.wait_ge(k2_ready, n + 1)
                if cfg.out and not (isinstance(n, int) and n < 2):
                    pe.wait_ge(res_done, n - 1)
                for g in range(4):
                    last = pe.transpose(M[:, g * 128:(g + 1) * 128], T.nm[:, g, :].bitcast(F32), T.ident[:])
                last.then_inc(nm_done, 1)

            def scores_t(b, par, i):
                if i == 0:
                    pe.wait_ge(nm_ready, b + 1)
                if not (isinstance(b, int) and b == 0 and i < 2):
                    pe.wait_ge(exp_done, b * NQ + (i - 1))
                bank = STB[i % 2]
                if cfg.wide:
                    for j in range(4):
                        block = bank[:, j * 128:(j + 1) * 128]
                        pe.matmul(block, T.ident_bf[:], T.mask_kq[:, 0:128], start=True, stop=False)
                        pe.matmul(block, T.kb1[par][:, 4 * i + j, :], T.q1[par][:, i, :], start=False, stop=False)
                        last = pe.matmul(block, T.kb2[par][:, 4 * i + j, :], T.q2[par][:, i, :], start=False, stop=True)
                else:
                    if cfg.causal:
                        pe.matmul(bank[:, :], T.ident_bf[:], T.mask_kq[:], start=True, stop=False)
                    pe.matmul(bank[:, :], T.kb1[par][:, i, :], T.q1[par][:, :, :], start=not cfg.causal, stop=False)
                    last = pe.matmul(bank[:, :], T.kb2[par][:, i, :], T.q2[par][:, :, :], start=False, stop=True)
                last.then_inc(st_done, 1)

            def values(b, par, i):
                pe.wait_ge(exp_done, b * NQ + (i + 1))
                if i == 0:
                    pe.wait_ge(v_copied, b + 1)
                    if not (isinstance(b, int) and b == 0):
                        pe.wait_ge(att_ready, b)
                per_quad = KVH // NQ
                width = 512 // per_quad
                for j in range(per_quad):
                    block = (i * per_quad + j) * R
                    last = pe.matmul(PV[0:R, j * width:(j + 1) * width], T.vaug[par][:, block:block + R],
                                     T.pt[i % 2][:, j * width:(j + 1) * width], start=(i == 0 and j == 0), stop=(i == NQ - 1),
                                     skip_group_check=True)
                if i == NQ - 1:
                    last.then_inc(pv_done, 1)

            def transpose_pv(b):
                wait_apart(T, pe, pv_copied, b + 1)
                for j in range(4):
                    last = pe.transpose(PV[:, j * R:(j + 1) * R], T.pvs[0:R, j * 128:(j + 1) * 128], T.ident[0:R, 0:R])
                last.then_inc(pv_ready, 1)

            def project_out(m):
                pe.wait_ge(at_copied, m + 1)
                for j in range(KT):
                    last = pe.matmul(M[:, 0:256], T.atT[:, j * 128:(j + 1) * 128], T.wo[cfg.name][:, j, :],
                                     start=(j == 0), stop=(j == KT - 1))
                last.then_inc(out_done, 1)

            def transpose_att(m, has_later):
                pe.wait_ge(att_ready, m + 1)
                if has_later:
                    pe.wait_ge(k2_ready, m + 3)
                elif isinstance(m, int) and m == B - 1:
                    pe.wait_ge(res_done, m)
                for j in range(KT):
                    last = pe.transpose(M[:, j * 128:(j + 1) * 128], T.att[:, j * 128:(j + 1) * 128], T.ident[:])
                last.then_inc(at_done, 1)

            def iteration(b, par, has_prev, has_next, has_second):
                for i in range(NQ + LEAD):
                    if i < NQ:
                        scores_t(b, par, i)
                    if i == 0 and cfg.project and has_second:
                        transpose_x(b + 2, par)
                    if 1 <= i <= NQ:
                        values(b, par, i - 1)
                    if i == 1 and cfg.out and has_prev:
                        transpose_att(b - 1, has_next)
                    if i == 2 and cfg.project and has_second:
                        project(b + 2)
                    if i >= LEAD and has_next:
                        scores(b + 1, 1 - par, i - LEAD)
                    if i == 3 and cfg.out and has_prev:
                        project_out(b - 1)
                if has_second:
                    transpose_qk(b + 2)
                transpose_pv(b)
                if has_next:
                    transpose_maxima(b + 1)
                if has_second:
                    transpose_k_low(b + 2)

            if cfg.project:
                transpose_x(0, 0)
                project(0)
            transpose_qk(0)
            transpose_k_low(0)
            if cfg.project:
                transpose_x(1, 1)
            for i in range(NQ):
                scores(0, 0, i)
            if cfg.project:
                project(1)
            transpose_maxima(0)
            transpose_qk(1)
            transpose_k_low(1)
            all_batches(pe, iteration)
            if cfg.out:
                transpose_att(B - 1, False)
                project_out(B - 1)

        @block.scalar
        def _(act):
            def copy_xt(n):
                act.wait_ge(xt_done, n + 1)
                last = act.activation(T.xT[:, 0:256], PA[:, 0:256], ACT.Copy)
                if not cfg.own_kv:
                    last = act.activation(T.xT[0:CTX, 256:384], PA[0:CTX, 256:384], ACT.Copy)
                last.then_inc(xt_copied, 1)

            def copy_proj(n):
                if cfg is CROSS1:
                    act.wait_ge(proj_done, n + 1)
                    act.activation(T.qk[:, 0:256], PB[:, 0:256], ACT.Copy)
                    act.activation(T.qk[:, 256:512], PA[:, 0:256], ACT.Copy).then_inc(qk_copied, 1)

            def copy_v(n, par):
                if cfg is ATTN0:
                    return
                if not (isinstance(n, int) and n < 2):
                    act.wait_ge(pv_done, n - 1)
                if cfg is ATTN1:
                    act.wait_ge(proj_done, n + 1)
                    v = PB[:, 0:64]
                else:
                    v = PA[:, 256:512] if cfg.project else T.cs[par][:, :]
                act.activation(cfg.values(T.vaug[par])[..., 0:d], cfg.heads(v), ACT.Copy).then_inc(v_copied, 1)

            def round_qk(n, par):
                if cfg.project:
                    act.wait_ge(qk_copied, n + 1)
                    k = T.qk[:, 256:256 + 64 * cfg.kcols]
                else:
                    act.wait_ge(permuted, n + 1)
                    wait_loaded(act, n, par)
                    k = T.cs[par][:, :]
                if not (isinstance(n, int) and n == 0):
                    act.wait_ge(t2_low_done, n)
                act.activation(T.qs[:, :, 0:64], T.qk[:, 0:256].rearrange("p (g c) -> p g c", g=4), ACT.Copy)
                k3 = k.rearrange("p (c e) -> p c e", e=64)
                act.activation(T.ks1[:, 0:cfg.kcols, 0:64], k3, ACT.Copy)
                act.activation(T.ks1[:, 0:cfg.kcols, 64:128], k3, ACT.Copy).then_inc(rounded, 1)

            def copy_q(n, par):
                act.wait_ge(t2_done, n + 1)
                act.activation(T.q1[par][:, :, :].rearrange("p g q -> p (g q)"), PA[:, :], ACT.Copy)
                act.activation(T.q2[par][0:64, :, :].rearrange("p g q -> p (g q)"), PA[0:64, :], ACT.Copy).then_inc(q_ready, 1)

            def copy_k_low(n, par):
                if cfg.wide:
                    act.wait_ge(t2_low_done, n + 1)
                    out = T.kb2[par][0:64, :, :].rearrange("p (c j) k -> p c j k", j=4)
                    for j in range(4):
                        last = act.activation(out[:, :, j, :], M[0:64, :].rearrange("p (c k) -> p c k", c=4), ACT.Copy,
                                              scale=T.blockmask[0:64, 8 + j:9 + j])
                    last.then_inc(k2_ready, 1)

            def copy_maxima(n, par):
                act.wait_ge(nm_done, n + 1)
                act.activation(T.q2[par][MAX_HI:MAX_END, :, :].rearrange("p g q -> p (g q)"),
                               M[MAX_HI:MAX_END, :], ACT.Copy).then_inc(nm_ready, 1)

            def copy_att(m):
                act.wait_ge(at_done, m + 1)
                act.activation(T.atT[:], M[:, 0:256], ACT.Copy).then_inc(at_copied, 1)

            def iteration(b, par, has_prev, has_next, has_second):
                if has_next:
                    copy_q(b + 1, 1 - par)
                for i in range(NQ):
                    act.wait_ge(st_done, b * NQ + (i + 1))
                    act.activation(T.pt[i % 2][:, :], STB[i % 2][:, :], ACT.Exp, scale=cfg.scale).then_inc(exp_done, 1)
                    if i == 0:
                        if has_next:
                            copy_k_low(b + 1, 1 - par)
                        if cfg.project and has_second:
                            copy_xt(b + 2)
                    if i == 1 and cfg.out and has_prev:
                        copy_att(b - 1)
                    if i == 2 and has_second:
                        copy_proj(b + 2)
                    if i == 3 and has_second:
                        round_qk(b + 2, par)
                act.wait_ge(pv_done, b + 1)
                act.activation(T.pvs[0:R, :], PV[0:R, :], ACT.Copy).then_inc(pv_copied, 1)
                if has_second:
                    copy_v(b + 2, par)
                if has_next:
                    copy_maxima(b + 1, 1 - par)

            if cfg.project:
                copy_xt(0)
            copy_proj(0)
            round_qk(0, 0)
            copy_v(0, 0)
            copy_q(0, 0)
            copy_k_low(0, 0)
            if cfg.project:
                copy_xt(1)
            copy_proj(1)
            copy_maxima(0, 0)
            round_qk(1, 1)
            copy_v(1, 1)
            all_batches(act, iteration)
            if cfg.out:
                copy_att(B - 1)

        @block.vector
        def _(dve):
            def proj(n):
                if cfg is ATTN0:
                    dve.wait_ge(proj_done, n + 1)
                    dve.tensor_tensor(T.qk[:, :], PA[:, 0:512], T.b_qk[:], ALU.add).then_inc(qk_copied, 1)
                elif cfg is ATTN1:
                    dve.wait_ge(proj_done, n + 1)
                    src = PA[:, 0:320].rearrange("p (h e) -> p h e", e=d)
                    cos = T.rope[:, 0:8].unsqueeze(1).broadcast_to([128, 40, 8])
                    half = d // 2
                    a = T.rope_a[:, :].rearrange("p (h e) -> p h e", e=d)
                    r = T.rope_b[:, :].rearrange("p (h e) -> p h e", e=d)
                    dve.tensor_tensor(a, src, cos, ALU.mult).then_inc(rope_a, 1)
                    for lo in (0, half):
                        sin = T.rope[:, 8 + lo:8 + lo + half].unsqueeze(1).broadcast_to([128, 40, half])
                        dve.tensor_tensor(r[:, :, lo:lo + half], src[:, :, half - lo:d - lo], sin, ALU.mult).then_inc(rope_a, 1)
                    dve.wait_ge(rope_a, (n + 1) * 3)
                    dve.tensor_tensor(T.qk[:, 0:320], T.rope_a[:, :], T.rope_b[:, :], ALU.add).then_inc(qk_copied, 1)

            def copy_v(n, par):
                if cfg is ATTN0:
                    if not (isinstance(n, int) and n < 2):
                        dve.wait_ge(pv_done, n - 1)
                    dve.tensor_tensor(cfg.values(T.vaug[par])[..., 0:d], cfg.heads(PB[:, 0:256]), cfg.heads(T.b_v[:]),
                                      ALU.add).then_inc(v_copied, 1)

            def keys(n, par):
                dve.wait_ge(t2_done, n + 1)
                if cfg.wide:
                    out = T.kb1[par][:, :, :].rearrange("p (c j) k -> p c j k", j=4)
                    for j in range(4):
                        last = dve.tensor_scalar(out[:, :, j, :], PB[:, :].rearrange("p (c k) -> p c k", c=4),
                                                 T.blockmask[:, 8 + j:9 + j], None, ALU.mult)
                    last.then_inc(k_ready, 1)
                else:
                    for rows, out, bank, done, ready in ((128, T.kb1[par], PB, t2_done, k_ready), (64, T.kb2[par], M, t2_low_done, k2_ready)):
                        dve.wait_ge(done, n + 1)
                        dve.tensor_tensor(out[0:rows, 0:8, :], bank[0:rows, 0:128].unsqueeze(1).broadcast_to([rows, 8, 128]),
                                          T.blockmask[0:rows, 0:8].unsqueeze(2).broadcast_to([rows, 8, 128]),
                                          ALU.mult).then_inc(ready, 1)

            def normalise(m):
                dve.wait_ge(pv_ready, m + 1)
                pv = PV[:, 0:HEADS * (d + 1)].rearrange("p (h e) -> p h e", e=d + 1)
                dve.reciprocal(T.rec[:, 0:HEADS], pv[:, :, d]).then_inc(rec_done, 1)
                dve.wait_ge(rec_done, m + 1)
                dve.tensor_tensor(T.att[:, :].rearrange("p (i j e) -> p j i e", j=4, e=d),
                                  PV[:, 0:4 * R].rearrange("p (j i e) -> p j i e", j=4, e=d + 1)[:, :, :, 0:d],
                                  T.rec[:, 0:HEADS].rearrange("p (j i) -> p j i", j=4).unsqueeze(3).broadcast_to([128, 4, NQ, d]),
                                  ALU.mult).then_inc(att_ready, 1)

            def residual(m):
                x = T.x_all[:, bass.ds(m, 1), :].rearrange("p a c -> p (a c)")
                if cfg.out:
                    if cfg.bias:
                        dve.tensor_tensor(T.xb[:], x, T.b_o[:], ALU.add).then_inc(bias_done, 1)
                        dve.wait_ge(bias_done, m + 1)
                        x = T.xb[:]
                    dve.wait_ge(out_done, m + 1)
                    dve.tensor_tensor(T.res[:], M[:, 0:256], x, ALU.add).then_inc(res_done, 1)
                else:
                    dve.wait_ge(att_ready, m + 1)
                    dve.tensor_tensor(T.res[:], T.att[:], x, ALU.add).then_inc(res_done, 1)

            def statistics(m):
                dve.wait_ge(res_done, m + 1)
                dve.bn_stats(T.stats[:], T.res[:]).then_inc(stat_done, 1)
                wait_apart(T, dve, stat_done, m + 1)
                dve.bn_aggr(T.mv[:], T.stats[:]).then_inc(aggr_done, 1)
                dve.wait_ge(aggr_done, m + 1)
                dve.tensor_scalar(T.vare[:], T.mv[:, 1:2], EPS, None, ALU.add).then_inc(var_done, 1)

            def norm(m):
                dve.wait_ge(rstd_done, m + 1)
                x = T.x_all[:, bass.ds(m, 1), :].rearrange("p a c -> p (a c)")
                dve.tensor_scalar(x, T.res[:], T.mv[:, 0:1], T.rstd[:], ALU.subtract, ALU.mult).then_inc(ln_done, 1)

            def maxima(n, i):
                dve.wait_ge(s_done, n * NQ + (i + 1))
                g = i if cfg.wide else i // 2
                at = 0 if cfg.wide else 4 * (i % 2)
                dve.tensor_reduce(T.nmf[:, g, at:at + 4], SB[i % 2][:, :].rearrange("p (h k) -> p h k", h=4),
                                  AX.X, ALU.max, negate=True).then_inc(max_done, 1)

            def split_maxima(n):
                heads = 4 if cfg.wide else 8
                dve.wait_ge(max_done, n * NQ + NQ)
                dve.tensor_copy(T.nm[:, :, MAX_HI:MAX_HI + heads], T.nmf[:, :, 0:heads]).then_inc(nm_hi, 1)
                dve.wait_ge(nm_hi, n + 1)
                dve.tensor_tensor(T.nm[:, :, MAX_LO:MAX_LO + heads], T.nmf[:, :, 0:heads],
                                  T.nm[:, :, MAX_HI:MAX_HI + heads].bitcast(F32), ALU.subtract).then_inc(nm_split, 1)

            def iteration(b, par, has_prev, has_next, has_second):
                if has_next:
                    keys(b + 1, 1 - par)
                for i in range(NQ):
                    if i == NQ - 1 and has_second:
                        copy_v(b + 2, par)
                    if has_next:
                        maxima(b + 1, i)
                    if i == 0 and cfg.project and has_second:
                        proj(b + 2)
                    if i == 1 and has_prev:
                        residual(b - 1)
                        statistics(b - 1)
                    if i == 2 and has_prev:
                        norm(b - 1)
                if has_next:
                    split_maxima(b + 1)
                normalise(b)

            blocks = T.onerows[64:128, 8:24] if cfg.wide else T.onerows[64:128, 0:8]
            for par in range(2):
                dve.tensor_copy(T.kb2[par][64:128, 0:cfg.blocks, :], blocks.unsqueeze(2).broadcast_to([64, cfg.blocks, 128])).then_inc(ones_set, 1)
            if cfg.project:
                proj(0)
            copy_v(0, 0)
            keys(0, 0)
            for i in range(NQ):
                maxima(0, i)
            if cfg.project:
                proj(1)
            split_maxima(0)
            copy_v(1, 1)
            all_batches(dve, iteration)
            residual(B - 1)
            statistics(B - 1)
            norm(B - 1)

        @block.gpsimd
        def _(pool):
            def permute(n):
                if not (isinstance(n, int) and n == 0):
                    pool.wait_ge(rounded, n)
                    pool.wait_ge(split, n)
                    pool.wait_ge(q_clear, n)
                pool.tensor_copy(T.qk[:, 0:256].rearrange("p (g v d) -> p g v d", g=4, d=8),
                                 T.x_all[:, bass.ds(n, 1), :].rearrange("p a (v g d) -> p (a g) v d", g=4, d=8)
                                 ).then_inc(permuted, 1)

            def low_parts(n, par):
                pool.wait_ge(rounded, n + 1)
                if not (isinstance(n, int) and n == 0):
                    pool.wait_ge(q_clear, n)
                k = T.qk[:, 256:256 + 64 * cfg.kcols] if cfg.project else T.cs[par][:, :]
                pool.tensor_tensor(T.qs[:, :, 64:128], T.qk[:, 0:256].rearrange("p (g c) -> p g c", g=4),
                                   T.qs[:, :, 0:64].bitcast(F32), ALU.subtract)
                pool.tensor_tensor(T.ks2[:, 0:cfg.kcols, :], k.rearrange("p (c e) -> p c e", e=64),
                                   T.ks1[:, 0:cfg.kcols, 0:64].bitcast(F32), ALU.subtract).then_inc(split, 1)

            def clear(n, par):
                pool.wait_ge(t2_done, n + 1)
                pool.wait_ge(split, n + 1)
                if not (isinstance(n, int) and n < 3):
                    pool.wait_ge(rstd_done, n - 2)
                pool.sem_inc(T.passed, 1)
                pool.memset(T.q2[par][64:128, :, :].bitcast(F32), 0.0).then_inc(q_clear, 1)

            def rstd(m, cleared):
                pool.wait_ge(var_done, m + 1)
                pool.wait_ge(q_clear, cleared)
                pool.tensor_tensor(T.rstd[:], T.vare[:], T.half[:], ALU.pow).then_inc(rstd_done, 1)

            def iteration(b, par, has_prev, has_next, has_second):
                if has_next:
                    clear(b + 1, 1 - par)
                if not cfg.project and has_second:
                    permute(b + 2)
                if has_prev:
                    rstd(b - 1, b + 2 if has_next else B)
                if has_second:
                    low_parts(b + 2, par)

            if not cfg.project:
                permute(0)
            low_parts(0, 0)
            clear(0, 0)
            if not cfg.project:
                permute(1)
            low_parts(1, 1)
            all_batches(pool, iteration)
            rstd(B - 1, B)


class Memory:

    def __init__(self, nc, start, end):
        self.nc, self.at, self.end = nc, start, end

    def __call__(self, name, shape, dt=F32):
        size = int(np.prod(shape[1:])) * (2 if dt == BF16 else 4)
        size = (size + 31) // 32 * 32
        assert self.at + size <= self.end, f"{name} does not fit: {self.at + size} > {self.end}"
        t = self.nc.alloc_sbuf_tensor_at(name, list(shape), dt, offset=self.at)
        self.at += size
        return t


class Tensors:
    pass


def flat(x_all, t):
    return x_all[:, bass.ds(t, 1), :].rearrange("p a c -> p (a c)")


def ktiles(w):
    return w.rearrange("(k p) n -> p k n", p=128)


def broadcast(v):
    return v.rearrange("(a n) -> a n", a=1).broadcast_to([128, v.shape[0]])


def load_first(nc, a, T):
    loads = [(T.x_all[:], a["x"].rearrange("b p c -> p b c")), (T.ident[:], a["ident"]),
             (T.masks[:], a["masks"]), (T.blockmask[:], a["blockmask"]), (T.rope[:], a["rope"]), (T.onerows[:], a["onerows"]),
             (T.a0_wqk[:, :, 0:256], ktiles(a["L0_attn_Wq"])), (T.a0_wqk[:, :, 256:512], ktiles(a["L0_attn_Wk"])),
             (T.a0_wv[:], ktiles(a["L0_attn_Wv"])), (T.a0_wo[:], ktiles(a["L0_attn_Wo"])),
             (T.b_qk[:, 0:256], broadcast(a["L0_attn_bq"])), (T.b_qk[:, 256:512], broadcast(a["L0_attn_bk"])),
             (T.b_v[:], broadcast(a["L0_attn_bv"])), (T.b_o[:], broadcast(a["L0_attn_bo"])),
             (T.a1_wqkv[:, :, 0:256], ktiles(a["L1_attn_Wq"])), (T.a1_wqkv[:, :, 256:320], ktiles(a["L1_attn_Wk"])),
             (T.a1_wqkv[:, :, 320:384], ktiles(a["L1_attn_Wv"])), (T.a1_wo[:], ktiles(a["L1_attn_Wo"])),
             (T.x1_wq[:], ktiles(a["L1_xattn_Wq"])), (T.x1_wkv[:], a["L1_xattn_Wkv_expand"]),
             (T.x1_wo[:], ktiles(a["L1_xattn_Wout"])), (T.f0_wg[:, :, 0:256], ktiles(a["L0_ffn_W"])),
             (T.f0_wg[:, :, 256:264], ktiles(a["L0_ffn_gate_w"])), (T.f1_gate[:], ktiles(a["L1_ffn_gate_w"])),
             (T.iota[:], broadcast(a["iota"])), (T.lower[:], broadcast(a["lower"]))]
    with ExitStack() as ctx:
        loaded = ctx.enter_context(nc.semaphore("first_loaded"))
        block = ctx.enter_context(nc.Block())

        @block.sync
        def _(sp):
            for dst, src in loads:
                sp.dma_start(dst, src).then_inc(loaded, 16)

        @block.gpsimd
        def _(pool):
            pool.memset(T.wd[64:128, UNITS - LOW:, :, :].rearrange("p u j n -> p (u j n)"), 0.0).then_inc(T.low_cleared, 1)

        @block.scalar
        def _(act):
            act.wait_ge(T.low_cleared, 1)
            T.low_count = load_units(a, T, range(LOW), act, T.low_loaded)

        @block.vector
        def _(dve):
            dve.memset(T.nm[:].bitcast(F32), 0.0)
            dve.memset(T.half[:], -0.5)
            dve.wait_ge(loaded, 16 * len(loads))
            dve.tensor_copy(T.ident_bf[:], T.ident[:])
            for i, m in enumerate((T.mask_qk, T.mask_kq)):
                dve.tensor_copy(m[:].rearrange("p (h k) -> p h k", h=4),
                                T.masks[:, i * 128:(i + 1) * 128].unsqueeze(1).broadcast_to([128, 4, 128]))


def ones_beside_v(nc, cfg, T):
    with Stage(nc, cfg.name + "v") as stage, ExitStack() as ctx:
        cleared = stage.sem("cleared")
        block = ctx.enter_context(nc.Block())

        @block.vector
        def _(dve):
            for par in range(2):
                dve.memset(T.vaug[par][:], 0.0).then_inc(cleared, 1)
            for par in range(2):
                dve.wait_ge(cleared, par + 1)
                dve.memset(cfg.values(T.vaug[par])[..., cfg.d:cfg.d + 1], 1.0)


def sparse_experts(nc, a, T, F, banks):
    ST = NS // 128
    with Stage(nc, "m") as stage, ExitStack() as ctx:
        sem = stage.sem

        loaded = sem("loaded")
        cleared = sem("cleared")
        zeroed = sem("zeroed")
        v = sem("v")
        act = sem("act")
        pe_s = sem("pe")
        eq_ready = sem("eq_ready")
        eq_used = sem("eq_used")
        placed = sem("placed")
        back = sem("back")
        block = ctx.enter_context(nc.Block())
        table = F.table
        bank_t, bank_d, bank_c = banks[0], banks[1], banks[2]

        @block.sync
        def _(sp):
            for dst, src in ((F.eaw[:], a["L0_ffn_expert_atom_weights"]), (F.atoms[:], a["L0_ffn_atoms"]),
                             (F.imp[:], a["importance"]), (F.idx_row[:], broadcast(a["L0_ffn_mask_idx"])),
                             (F.idx_col[:], a["mask_idx_columns"])):
                sp.dma_start(dst, src).then_inc(loaded, 16)
            sp.wait_ge(cleared, 1)
            for j in range(KT):
                sp.dma_start(table[j * 128 * 256:(j + 1) * 128 * 256, :].rearrange("(p r) e -> p (r e)", p=128),
                             F.m_re[:, j, :]).then_inc(zeroed, 16)
            sp.wait_ge(placed, 16 * ST)
            for j in range(KT):
                sp.dma_start(F.m_re[:, j, :], table[j * 128 * 256:(j + 1) * 128 * 256, :]
                             .rearrange("(p r) e -> p (r e)", p=128)).then_inc(back, 16)

        @block.scalar
        def _(eng):
            eng.wait_ge(v, 1)
            eng.activation(F.eaw[:], F.eaw[:], ACT.Exp, bias=F.eawmax[:], accum_out=F.eawsum[:]).then_inc(act, 1)
            eng.activation(F.imp[:], F.imp[:], ACT.Exp, scale=-1.0).then_inc(act, 1)

        @block.tensor
        def _(pe):
            pe.wait_ge(v, 3)
            pe.transpose(bank_t[0:ATOMS, 0:E0], F.eaw[:], T.ident[0:E0, 0:E0]).then_inc(pe_s, 1)
            pe.wait_ge(v, 4)
            for t in range(ST):
                last = pe.matmul(bank_d[:, t * E0:(t + 1) * E0], F.atoms[:, t * 128:(t + 1) * 128], F.eawT[:],
                                 start=True, stop=True)
            last.then_inc(pe_s, 1)
            pe.wait_ge(v, 12)
            for t in range(ST):
                pe.wait_ge(eq_ready, t + 1)
                for u in range(ST):
                    last = pe.matmul(bank_c[:, u * 24:(u + 1) * 24], F.eq[t % 2][:, u * 128:(u + 1) * 128],
                                     F.w3[:, t, :], start=(t == 0 and u == 0), stop=(t == ST - 1), skip_group_check=True)
                last.then_inc(eq_used, 1)

        @block.vector
        def _(dve):
            dve.memset(F.m_re[:], 0.0).then_inc(cleared, 1)
            dve.wait_ge(loaded, 80)
            dve.tensor_reduce(F.eawmax[:], F.eaw[:], AX.X, ALU.max, negate=True).then_inc(v, 1)
            dve.wait_ge(act, 1)
            dve.reciprocal(F.eawsum[:], F.eawsum[:]).then_inc(v, 1)
            dve.wait_ge(v, 2)
            dve.tensor_scalar(F.eaw[:], F.eaw[:], F.eawsum[:], None, ALU.mult).then_inc(v, 1)
            dve.wait_ge(pe_s, 1)
            dve.tensor_copy(F.eawT[:], bank_t[0:ATOMS, 0:E0]).then_inc(v, 1)
            dve.wait_ge(act, 2)
            dve.tensor_scalar(F.imp[:], F.imp[:], 1.0, None, ALU.add).then_inc(v, 1)
            dve.wait_ge(v, 5)
            dve.reciprocal(F.imp[:], F.imp[:]).then_inc(v, 1)
            dve.wait_ge(v, 6)
            dve.wait_ge(pe_s, 2)
            dve.tensor_tensor(F.imp[:], bank_d[:, 0:ST * E0], F.imp[:], ALU.mult).then_inc(v, 1)
            imp = F.imp[:].rearrange("p (t e) -> p t e", e=E0)
            steps = 7
            for part in range(3):
                dve.wait_ge(v, steps)
                dve.tensor_copy(F.w3[:, :, part * 8:(part + 1) * 8], imp).then_inc(v, 1)
                steps += 1
                if part < 2:
                    dve.wait_ge(v, steps)
                    dve.tensor_tensor(imp, imp, F.w3[:, :, part * 8:(part + 1) * 8], ALU.subtract).then_inc(v, 1)
                    steps += 1
            dve.tensor_copy(F.col_f[:], F.idx_col[:]).then_inc(v, 1)
            dve.wait_ge(v, 13)
            for t in range(ST):
                if t >= 2:
                    dve.wait_ge(eq_used, t - 1)
                dve.tensor_scalar(F.eq[t % 2][:], F.idx_row[:], F.col_f[:, t:t + 1], None, ALU.is_equal).then_inc(eq_ready, 1)
            dve.tensor_scalar(F.pos_hi[:], F.idx_col[:], D - 1, 8, ALU.bitwise_and, ALU.logical_shift_left).then_inc(v, 1)
            dve.tensor_scalar(F.pos[:], F.idx_col[:], 8, None, ALU.logical_shift_right).then_inc(v, 1)
            dve.wait_ge(v, 15)
            dve.tensor_tensor(F.pos[:], F.pos[:], F.pos_hi[:], ALU.bitwise_or).then_inc(v, 1)
            dve.wait_ge(eq_used, ST)
            c = bank_c[:, 0:ST * 24].rearrange("p (t s e) -> p t s e", s=3, e=E0)
            dve.tensor_copy(F.sum8[:], c[:, :, 2, :]).then_inc(v, 1)
            for part, n in ((1, 17), (0, 18)):
                dve.wait_ge(v, n)
                dve.tensor_tensor(F.sum8[:], c[:, :, part, :], F.sum8[:], ALU.add).then_inc(v, 1)
            dve.wait_ge(back, 16 * KT)
            for j in range(KT):
                dve.tensor_copy(F.m[:, j, :, :], F.m_re[:, j, :].rearrange("p (r e) -> p e r", e=E0))

        @block.gpsimd
        def _(pool):
            pool.wait_ge(v, 19)
            pool.wait_ge(zeroed, 16 * KT)
            for t in range(ST):
                if t:
                    pool.wait_ge(placed, 16 * t)
                pool.indirect_dma_start(table[:, :], bass.IndirectOffsetOnAxis(ap=F.pos[:, t:t + 1], axis=0),
                                        F.sum8[:, t, :], None).then_inc(placed, 16)


def ffn0(nc, T, F, banks):
    STEPS = 12
    with Stage(nc, "f0") as stage, ExitStack() as ctx:
        sem = stage.sem

        loaded = [sem("loaded0"), sem("loaded1")]
        xt_done = sem("xt_done")
        xt_copied = sem("xt_copied")
        base_done = sem("base_done")
        pair_done = sem("pair_done")
        added = sem("added")
        stat = sem("stat")
        base_used = sem("base_used")
        step = sem("step")
        weight_exp = sem("weight_exp")
        var_done = sem("var_done")
        rstd_done = sem("rstd_done")
        block = ctx.enter_context(nc.Block())
        pairs, base, tr = banks[0:4], banks[4], banks[5]

        @block.sync
        def _(sp):
            def load(t, par):
                sp.dma_start(F.xs[par][:], flat(T.x_all, t)).then_inc(loaded[par], 16)
            load(0, 0)
            load(1, 1)
            with sp.Fori(0, B // 2 - 1) as i:
                for par in range(2):
                    sp.wait_ge(xt_done, i * 2 + (par + 1))
                    load(i * 2 + (par + 2), par)

        @block.tensor
        def _(pe):
            def tile(i, par, first):
                t = i * 2 + par
                pe.wait_ge(loaded[par], i * 16 + 16)
                if not (first and par == 0):
                    pe.wait_ge(xt_copied, t)
                for j in range(KT):
                    last = pe.transpose(tr[:, j * 128:(j + 1) * 128], F.xs[par][:, j * 128:(j + 1) * 128], T.ident[:])
                last.then_inc(xt_done, 1)
                pe.wait_ge(xt_copied, t + 1)
                if not (first and par == 0):
                    pe.wait_ge(base_used, t)
                for j in range(KT):
                    last = pe.matmul(base[:, 0:264], F.xT[par][:, j * 128:(j + 1) * 128], T.f0_wg[:, j, :],
                                     start=(j == 0), stop=(j == KT - 1))
                last.then_inc(base_done, 1)
                for q in range(4):
                    if not (first and par == 0):
                        pe.wait_ge(added, t * E0 + (2 * q + 2 - E0))
                    for j in range(KT):
                        last = pe.matmul(pairs[q][:, :], F.xT[par][:, j * 128:(j + 1) * 128], F.m[:, j, 2 * q:2 * q + 2, :],
                                         start=(j == 0), stop=(j == KT - 1))
                    last.then_inc(pair_done, 1)
            tile(0, 0, True)
            tile(0, 1, True)
            with pe.Fori(1, B // 2) as i:
                tile(i, 0, False)
                tile(i, 1, False)

        @block.scalar
        def _(act):
            with act.Fori(0, B // 2) as i:
                for par in range(2):
                    t = i * 2 + par
                    act.wait_ge(xt_done, t + 1)
                    act.activation(F.xT[par][:], tr[:, 0:256], ACT.Copy).then_inc(xt_copied, 1)
                    act.wait_ge(step, t * STEPS + 3)
                    act.activation(F.wexp[:], F.wdiff[:], ACT.Exp).then_inc(weight_exp, 1)

        @block.gpsimd
        def _(pool):
            with pool.Fori(0, B) as t:
                pool.wait_ge(var_done, t + 1)
                pool.tensor_tensor(T.rstd[:], T.vare[:], T.half[:], ALU.pow).then_inc(rstd_done, 1)

        @block.vector
        def _(dve):
            with dve.Fori(0, B) as t:
                def after(k):
                    dve.wait_ge(step, t * STEPS + k)

                x = flat(T.x_all, t)
                dve.wait_ge(base_done, t + 1)
                dve.tensor_scalar(F.logit[:], base[:, 256:264], -50.0, 50.0, ALU.max, ALU.min).then_inc(step, 1)
                wait_apart(T, dve, step, t * STEPS + 1)
                dve.max(F.top[:], F.logit[:]).then_inc(step, 1)
                after(2)
                dve.tensor_tensor(F.wdiff[:], F.top[:, 1:2], F.top[:, 0:1], ALU.subtract).then_inc(step, 1)
                dve.max_index(F.topi[:], F.top[:], F.logit[:]).then_inc(step, 1)
                after(4)
                dve.tensor_copy(F.topf[:], F.topi[:]).then_inc(step, 1)
                dve.wait_ge(weight_exp, t + 1)
                dve.tensor_scalar(F.p1[:], F.wexp[:], 1.0, None, ALU.add).then_inc(step, 1)
                after(6)
                dve.reciprocal(F.p0[:], F.p1[:]).then_inc(step, 1)
                after(7)
                dve.tensor_tensor(F.p1[:], F.p0[:], F.wexp[:], ALU.mult).then_inc(step, 1)
                dve.tensor_scalar(F.rw[:], T.iota[:, 0:E0], F.topf[:, 0:1], F.p0[:], ALU.is_equal, ALU.mult).then_inc(step, 1)
                after(9)
                dve.tensor_scalar(F.rw1[:], T.iota[:, 0:E0], F.topf[:, 1:2], F.p1[:], ALU.is_equal, ALU.mult).then_inc(step, 1)
                after(10)
                dve.tensor_tensor(F.rw[:], F.rw[:], F.rw1[:], ALU.add).then_inc(step, 1)
                dve.tensor_tensor(F.acc[:, 0, :], base[:, 0:256], x, ALU.add).then_inc(base_used, 1)
                dve.wait_ge(base_used, t + 1)
                after(11)
                for e in range(E0):
                    if e % 2 == 0:
                        dve.wait_ge(pair_done, t * 4 + (e // 2 + 1))
                    if e:
                        dve.wait_ge(added, t * E0 + e)
                    dve.scalar_tensor_tensor(F.acc[:, (e + 1) % 2, :], pairs[e // 2][:, (e % 2) * 256:(e % 2 + 1) * 256],
                                                   F.rw[:, e:e + 1], F.acc[:, e % 2, :], ALU.mult, ALU.add).then_inc(added, 1)
                acc = F.acc[:, 0, :]
                dve.wait_ge(added, (t + 1) * E0)
                dve.bn_stats(T.stats[:], acc).then_inc(stat, 1)
                wait_apart(T, dve, stat, t * 2 + 1)
                dve.bn_aggr(T.mv[:], T.stats[:]).then_inc(stat, 1)
                dve.wait_ge(stat, t * 2 + 2)
                dve.tensor_scalar(T.vare[:], T.mv[:, 1:2], EPS, None, ALU.add).then_inc(var_done, 1)
                dve.wait_ge(rstd_done, t + 1)
                dve.tensor_scalar(x, acc, T.mv[:, 0:1], T.rstd[:], ALU.subtract, ALU.mult).then_inc(step, 1)


def route(nc, a, T, G, banks):
    with Stage(nc, "r") as stage, ExitStack() as ctx:
        sem = stage.sem

        xt_done = sem("xt_done")
        xt_copied = sem("xt_copied")
        logits_done = sem("logits_done")
        exp_done = sem("exp_done")
        step = sem("step")
        block = ctx.enter_context(nc.Block())
        tr, logits = banks[0:2], banks[2]

        @block.gpsimd
        def _(pool):
            pool.memset(T.wd[64:128, 0:UNITS - LOW, :, :].rearrange("p u j n -> p (u j n)"), 0.0).then_inc(T.high_cleared, 1)

        @block.sync
        def _(sp):
            sp.wait_ge(T.high_cleared, 1)
            T.high_count = load_units(a, T, range(LOW, UNITS), sp, T.high_loaded)

        @block.tensor
        def _(pe):
            for t in range(B):
                if t >= 2:
                    pe.wait_ge(xt_copied, t - 1)
                for j in range(KT):
                    last = pe.transpose(tr[t % 2][:, j * 128:(j + 1) * 128], T.x_all[:, t, j * 128:(j + 1) * 128], T.ident[:])
                last.then_inc(xt_done, 1)
            for t in range(B):
                pe.wait_ge(xt_copied, t + 1)
                for j in range(KT):
                    last = pe.matmul(logits[:, t * E1:(t + 1) * E1], G.xT[:, t, j * 128:(j + 1) * 128], T.f1_gate[:, j, :],
                                     start=(j == 0), stop=(j == KT - 1))
            last.then_inc(logits_done, 1)

        @block.scalar
        def _(act):
            for t in range(B):
                act.wait_ge(xt_done, t + 1)
                act.activation(G.xT[:, t, :], tr[t % 2][:, 0:256], ACT.Copy).then_inc(xt_copied, 1)
            act.wait_ge(logits_done, 1)
            act.activation(G.score[:], logits[:, 0:B * E1], ACT.Exp, scale=-1.0).then_inc(exp_done, 1)

        @block.vector
        def _(dve):
            done = 0

            def then(ins):
                nonlocal done
                done += 1
                ins.then_inc(step, 1)
                dve.wait_ge(step, done)

            dve.wait_ge(exp_done, 1)
            then(dve.tensor_scalar(G.score[:], G.score[:], 1.0, None, ALU.add))
            then(dve.reciprocal(G.score[:], G.score[:]))
            grouped_scores = G.score[:].rearrange("p (t g e) -> p t g e", t=B, g=GROUPS)
            then(dve.tensor_reduce(G.gmax[:], grouped_scores, AX.X, ALU.max))
            this = G.gmax[:].unsqueeze(3).broadcast_to([128, B, GROUPS, GROUPS])
            other = G.gmax[:].unsqueeze(2).broadcast_to([128, B, GROUPS, GROUPS])
            then(dve.tensor_tensor(G.before[:], other, this, ALU.is_gt))
            then(dve.tensor_tensor(G.tied[:], other, this, ALU.is_equal))
            lower = T.lower[:].rearrange("p (g h) -> p g h", g=GROUPS).unsqueeze(1).broadcast_to([128, B, GROUPS, GROUPS])
            then(dve.tensor_tensor(G.tied[:], G.tied[:], lower, ALU.mult))
            then(dve.tensor_tensor(G.before[:], G.before[:], G.tied[:], ALU.add))
            then(dve.tensor_reduce(G.rank[:], G.before[:], AX.X, ALU.add))
            then(dve.tensor_scalar(G.rank[:], G.rank[:], float(TOP_GROUPS), None, ALU.is_lt))
            allowed = G.rank[:].unsqueeze(3).broadcast_to([128, B, GROUPS, E1 // GROUPS])
            masked = G.masked[:].rearrange("p (t g e) -> p t g e", t=B, g=GROUPS)
            then(dve.tensor_scalar(G.masked[:], G.score[:], 1.0, None, ALU.add))
            then(dve.tensor_tensor(masked, masked, allowed, ALU.mult))
            then(dve.tensor_scalar(G.masked[:], G.masked[:], -1.0, None, ALU.add))
            for t in range(B):
                then(dve.max(G.top[:, t, :], G.masked[:, t * E1:(t + 1) * E1]))
                then(dve.max_index(G.topi[:, t, :], G.top[:, t, :], G.masked[:, t * E1:(t + 1) * E1]))
            then(dve.tensor_copy(G.topf[:], G.topi[:]))
            experts = T.iota[:, 0:E1].unsqueeze(1).broadcast_to([128, B, E1])
            chosen = G.masked[:].rearrange("p (t e) -> p t e", t=B)
            for k in range(TOP):
                index = G.topf[:, :, k:k + 1].broadcast_to([128, B, E1])
                then(dve.tensor_tensor((G.hit if k else chosen)[:], experts, index, ALU.is_equal))
                if k:
                    then(dve.tensor_tensor(chosen, chosen, G.hit[:], ALU.add))
            scores = G.score[:].rearrange("p (t e) -> p t e", t=B)
            then(dve.tensor_tensor(chosen, chosen, scores, ALU.mult))
            then(dve.tensor_reduce(G.total[:], chosen, AX.X, ALU.add))
            then(dve.reciprocal(G.total[:], G.total[:]))
            then(dve.tensor_tensor(G.w[:, :, 0:E1], chosen, G.total[:].unsqueeze(2).broadcast_to([128, B, E1]), ALU.mult))
            dve.memset(G.w[:, :, E1:UNITS], 1.0)


LOW = 18


def load_units(a, T, units, eng, sem):
    lo, hi = units.start, min(units.stop, E1)
    n = hi - lo
    for j in range(KT):
        rows = slice(j * 128, (j + 1) * 128)
        eng.dma_start(T.wgu[:, lo:hi, j, 0:MI], a["L1_ffn_w_gate"][lo:hi, rows, :].rearrange("e p m -> p e m")).then_inc(sem, 16)
        eng.dma_start(T.wgu[:, lo:hi, j, MI:2 * MI], a["L1_ffn_w_up"][lo:hi, rows, :].rearrange("e p m -> p e m")).then_inc(sem, 16)
    for e in range(lo, hi):
        eng.dma_start(T.wd[0:MH, UNITS - 1 - e, :, :], a["L1_ffn_w_down"][e].rearrange("(j p) n -> p j n", p=MH)).then_inc(sem, 16)
    count = 2 * KT + n
    for u in range(hi, units.stop):
        m = slice((u - E1) * MI, (u - E1 + 1) * MI)
        eng.dma_start(T.wgu[:, u, :, 0:MI], ktiles(a["L1_ffn_sw_gate"][:, m])).then_inc(sem, 16)
        eng.dma_start(T.wgu[:, u, :, MI:2 * MI], ktiles(a["L1_ffn_sw_up"][:, m])).then_inc(sem, 16)
        eng.dma_start(T.wd[0:MH, UNITS - 1 - u, :, :], a["L1_ffn_sw_down"][m, :].rearrange("(j p) n -> p j n", p=MH)).then_inc(sem, 16)
        count += 3
    return 16 * count


def experts(nc, a, T, G, banks, out):
    with Stage(nc, "e") as stage, ExitStack() as ctx:
        sem = stage.sem

        zero = sem("zero")
        gu_done = sem("gu_done")
        sil_ready = sem("sil_ready")
        h_ready = sem("h_ready")
        tr_done = sem("tr_done")
        ht_ready = sem("ht_ready")
        down_done = sem("down_done")
        res = sem("res")
        stat = sem("stat")
        rstd_done = sem("rstd_done")
        stored = sem("stored")
        block = ctx.enter_context(nc.Block())
        acc, gu, tr = banks[0:4], banks[4:6], banks[6:8]
        LAST = UNITS - 1

        @block.gpsimd
        def _(pool):
            pool.wait_ge(res, 17)
            pool.tensor_tensor(G.rstd[:], G.vare[:], T.half[:, 0:1].broadcast_to([128, B]), ALU.pow).then_inc(rstd_done, 1)

        @block.sync
        def _(sp):
            for t in range(B):
                sp.wait_ge(res, 17 + t + 1)
                sp.dma_start(out[t, :, :], T.x_all[:, t, :]).then_inc(stored, 16)
            sp.wait_ge(stored, 16 * B)

        @block.tensor
        def _(pe):
            def gate_up(e, t, first=False):
                u = e * B + t
                if not first:
                    pe.wait_ge(h_ready, u - 1)
                for j in range(KT):
                    last = pe.matmul(gu[t % 2][:, 0:2 * MI], G.xT[:, t, j * 128:(j + 1) * 128],
                                     T.wgu[:, bass.ds(e, 1), j, :].rearrange("p a n -> p (a n)"), start=(j == 0), stop=(j == KT - 1))
                last.then_inc(gu_done, 1)

            def transpose_h(e, t, first=False):
                u = e * B + t
                pe.wait_ge(h_ready, u + 1)
                if not first:
                    pe.wait_ge(ht_ready, u if t == 1 else u - 1)
                for j in range(2):
                    last = pe.transpose(tr[t % 2][0:MH, j * 128:(j + 1) * 128], G.h[t % 2][:, j * MH:(j + 1) * MH], T.ident[:])
                last.then_inc(tr_done, 1)

            def down(e, t):
                u = e * B + t
                pe.wait_ge(ht_ready, u + 1)
                for j in range(2):
                    last = pe.matmul(acc[t // 2][:, (t % 2) * 256:(t % 2 + 1) * 256], G.hT[t % 2][:, j * 128:(j + 1) * 128],
                                     T.wd[:, bass.ds(e * -1 + LAST, 1), j, :].rearrange("p a n -> p (a n)"),
                                     start=False, stop=True, skip_group_check=True)
                return last

            def unit(e, final):
                for t in range(B):
                    if t < B - 2:
                        gate_up(e, t + 2)
                    elif not final:
                        gate_up(e + 1, t + 2 - B)
                    if t < B - 1:
                        transpose_h(e, t + 1)
                    elif not final:
                        transpose_h(e + 1, 0)
                    last = down(e, t)
                if final:
                    last.then_inc(down_done, 1)

            pe.wait_ge(zero, 4 + 2)
            pe.wait_ge(T.low_loaded, T.low_count)
            pe.wait_ge(T.high_loaded, T.high_count)
            gate_up(0, 0, True)
            gate_up(0, 1, True)
            transpose_h(0, 0, True)
            with pe.Fori(0, LAST) as e:
                unit(e, False)
            unit(LAST, True)

        @block.scalar
        def _(act):
            def silu(e, t):
                act.wait_ge(gu_done, e * B + (t + 1))
                act.activation(G.sil[t % 2][:], gu[t % 2][:, 0:MI], ACT.Silu).then_inc(sil_ready, 1)

            def copy_ht(e, t):
                act.wait_ge(tr_done, e * B + (t + 1))
                act.activation(G.hT[t % 2][0:MH, :], tr[t % 2][0:MH, 0:256], ACT.Copy).then_inc(ht_ready, 1)

            def unit(e, final):
                for t in range(B):
                    if t < B - 2:
                        silu(e, t + 2)
                    elif not final:
                        silu(e + 1, t + 2 - B)
                    if t < B - 1:
                        copy_ht(e, t + 1)
                    elif not final:
                        copy_ht(e + 1, 0)

            act.wait_ge(zero, 6)
            silu(0, 0)
            silu(0, 1)
            copy_ht(0, 0)
            with act.Fori(0, LAST) as e:
                unit(e, False)
            unit(LAST, True)

        @block.vector
        def _(dve):
            for bank in acc:
                dve.memset(bank[:], 0.0).then_inc(zero, 1)
            for par in range(2):
                dve.memset(G.hT[par][64:128, :], 0.0).then_inc(zero, 1)

            with dve.Fori(0, UNITS) as e:
                for t in range(B):
                    u = e * B + t
                    dve.wait_ge(sil_ready, u + 1)
                    dve.scalar_tensor_tensor(G.h[t % 2][:], gu[t % 2][:, MI:2 * MI],
                                             G.w[:, t, bass.ds(e, 1)], G.sil[t % 2][:], ALU.mult, ALU.mult).then_inc(h_ready, 1)
            dve.wait_ge(down_done, 1)
            for t in range(B):
                dve.tensor_tensor(T.x_all[:, t, :], acc[t // 2][:, (t % 2) * 256:(t % 2 + 1) * 256], T.x_all[:, t, :], ALU.add).then_inc(res, 1)
            for t in range(B):
                dve.wait_ge(res, t + 1)
                dve.bn_stats(G.stats[:, t, :], T.x_all[:, t, :]).then_inc(stat, 1)
            for t in range(B):
                dve.wait_ge(stat, t + 1)
                dve.bn_aggr(G.mv[:, t, :], G.stats[:, t, :]).then_inc(res, 1)
            dve.wait_ge(res, 16)
            dve.tensor_scalar(G.vare[:], G.mv[:, :, 1], EPS, None, ALU.add).then_inc(res, 1)
            dve.wait_ge(rstd_done, 1)
            dve.wait_ge(res, 17)
            for t in range(B):
                dve.tensor_scalar(T.x_all[:, t, :], T.x_all[:, t, :], G.mv[:, t, 0:1], G.rstd[:, t:t + 1],
                                  ALU.subtract, ALU.mult).then_inc(res, 1)


def store(nc, T, out):
    with ExitStack() as c2:
        st = c2.enter_context(nc.semaphore("st"))
        block = c2.enter_context(nc.Block())

        @block.sync
        def _(sp):
            sp.wait_ge(T.low_loaded, T.low_count)
            sp.dma_start(out.rearrange("b p c -> p b c"), T.x_all[:]).then_inc(st, 16)
            sp.wait_ge(st, 16)


STAGES = ("a0", "x0", "f0", "a1", "x1", "f1")


def decoder(nc, a, out):
    with ExitStack() as ctx:
        T, F, G = Tensors(), Tensors(), Tensors()
        banks = [ctx.enter_context(nc.psum_tensor(f"bank{i}", [128, 512], F32)) for i in range(8)]
        T.SB, T.STB, T.PV, T.PA, T.PB, T.M = banks[0:2], banks[2:4], banks[4], banks[5], banks[6], banks[7]
        start = (nc.sbuf_base + 31) // 32 * 32
        end = nc.sbuf_usable_end // 32 * 32
        weights = UNITS * (2 * KT * MI + 2 * D) * 4
        keep = Memory(nc, start, end - weights)
        units = Memory(nc, end - weights, end)
        T.wgu = units("wgu", [128, UNITS, KT, 2 * MI])
        middle = units.at
        T.wd = units("wd", [128, UNITS, 2, D])

        T.x_all = keep("x_all", [128, B, D])
        T.ident = keep("ident", [128, 128])
        T.half = keep("half", [128, 1])
        T.iota = keep("iota", [128, E1])
        T.lower = keep("lower", [128, GROUPS * GROUPS])
        T.f1_gate = keep("f1_gate", [128, KT, E1])
        T.rstd, T.vare = keep("rstd", [128, 1]), keep("vare", [128, 1])
        T.stats, T.mv = keep("stats", [128, 6]), keep("mv", [128, 2])
        kept = keep.at

        G.xT = keep("g_xT", [128, B, D])
        G.w = keep("g_w", [128, B, UNITS])
        G.score, G.masked = keep("g_score", [128, B * E1]), keep("g_masked", [128, B * E1])
        G.hit = keep("g_hit", [128, B, E1])
        G.gmax, G.rank = keep("g_gmax", [128, B, GROUPS]), keep("g_rank", [128, B, GROUPS])
        G.before, G.tied = keep("g_before", [128, B, GROUPS, GROUPS]), keep("g_tied", [128, B, GROUPS, GROUPS])
        G.top, G.topi, G.topf = keep("g_top", [128, B, 8]), keep("g_topi", [128, B, 8], U32), keep("g_topf", [128, B, 8])
        G.total = keep("g_total", [128, B])
        G.sil = [keep(f"g_sil{i}", [128, MI]) for i in range(2)]
        G.h = [keep(f"g_h{i}", [128, MI]) for i in range(2)]
        G.hT = [keep(f"g_hT{i}", [128, 256]) for i in range(2)]
        G.stats, G.mv = keep("g_stats", [128, B, 6]), keep("g_mv", [128, B, 2])
        G.vare, G.rstd = keep("g_vare", [128, B]), keep("g_rstd", [128, B])

        shared_start = middle - (UNITS - LOW) * KT * 2 * MI * 4
        shared_end = middle + (UNITS - LOW) * 2 * D * 4
        early = Memory(nc, kept, end - weights)
        at = Memory(nc, shared_start, shared_end)
        T.masks, T.blockmask, T.rope = early("masks", [128, 256]), early("blockmask", [128, 12]), early("rope", [128, 16])
        T.onerows = early("onerows", [128, 24])
        T.ident_bf = early("ident_bf", [128, 128], BF16)
        T.mask_qk, T.mask_kq = early("mask_qk", [128, 512], BF16), early("mask_kq", [128, 512], BF16)
        T.b_qk, T.b_v, T.b_o = early("b_qk", [128, 512]), early("b_v", [128, 256]), early("b_o", [128, 256])
        T.a0_wqk, T.a0_wv, T.a0_wo = early("a0_wqk", [128, KT, 512]), early("a0_wv", [128, KT, 256]), early("a0_wo", [128, KT, 256])
        T.a1_wqkv, T.a1_wo = early("a1_wqkv", [128, KT, 384]), early("a1_wo", [128, KT, 256])
        T.x1_wq, T.x1_wkv, T.x1_wo = early("x1_wq", [128, KT, 256]), early("x1_wkv", [CTX, 512]), early("x1_wo", [128, KT, 256])
        T.wo = {"a0": T.a0_wo, "a1": T.a1_wo, "x1": T.x1_wo}
        T.f0_wg = early("f0_wg", [128, KT, 264])
        T.nm, T.nmf = at("nm", [128, 4, 128], F32R), at("nmf", [128, 4, 8])
        ff = Memory(nc, at.at, shared_end)
        T.kb1, T.kb2 = ([at(f"{n}_{i}", [128, 16, 128], F32R) for i in range(2)] for n in ("kb1", "kb2"))
        T.q1, T.q2 = ([at(f"{n}_{i}", [128, 4, 128], F32R) for i in range(2)] for n in ("q1", "q2"))
        T.qs, T.ks1, T.ks2 = at("qs", [128, 4, 128], F32R), at("ks1", [128, 4, 128], F32R), at("ks2", [128, 4, 64], F32R)
        T.pt = [at(f"pt{i}", [128, 512]) for i in range(2)]
        T.xs = [at(f"xs{i}", [128, D]) for i in range(2)]
        T.cs = [at(f"cs{i}", [128, CTX]) for i in range(2)]
        T.vaug = [at(f"vaug{i}", [128, 4 * (4 * 68 + 17)]) for i in range(2)]
        T.pvs = at("pvs", [128, 512])
        T.xT, T.qk = at("xT", [128, 384]), at("qk", [128, 512])
        T.att, T.atT, T.rec, T.res, T.xb = at("att", [128, D]), at("atT", [128, D]), at("rec", [128, 32]), at("res", [128, D]), at("xb", [128, D])
        T.rope_a, T.rope_b = at("rope_a", [128, 320]), at("rope_b", [128, 320])
        T.ctx_tiles = a["ctx_512"]

        ST = NS // 128
        F.table = nc.dram_tensor("sparse_table", [D * D, E0], F32).ap()
        F.m = ff("f_m", [128, KT, E0, D])
        own = ff.at
        F.m_re = ff("f_m_re", [128, KT, D * E0])
        F.eaw, F.eawmax, F.eawsum = ff("f_eaw", [E0, ATOMS]), ff("f_eawmax", [E0, 1]), ff("f_eawsum", [E0, 1])
        F.atoms, F.eawT, F.imp = ff("f_atoms", [ATOMS, NS]), ff("f_eawT", [ATOMS, E0]), ff("f_imp", [128, ST * E0])
        F.idx_row, F.idx_col = ff("f_idx_row", [128, NS], I32), ff("f_idx_col", [128, ST], I32)
        F.col_f = ff("f_col_f", [128, ST])
        F.pos_hi, F.pos = ff("f_pos_hi", [128, ST], I32), ff("f_pos", [128, ST], I32)
        F.w3, F.sum8 = ff("f_w3", [128, ST, 3 * E0], BF16), ff("f_sum8", [128, ST, E0])
        F.eq = [ff(f"f_eq{i}", [128, NS], BF16) for i in range(2)]
        own = Memory(nc, own, shared_end)
        F.xs = [own(f"f_xs{i}", [128, D]) for i in range(2)]
        F.xT = [own(f"f_xT{i}", [128, D]) for i in range(2)]
        F.acc = own("f_acc", [128, 2, D])
        F.logit, F.top, F.topi, F.topf = own("f_logit", [128, 8]), own("f_top", [128, 8]), own("f_topi", [128, 8], U32), own("f_topf", [128, 8])
        F.wdiff, F.wexp, F.p0, F.p1 = (own(n, [128, 1]) for n in ("f_wdiff", "f_wexp", "f_p0", "f_p1"))
        F.rw, F.rw1 = own("f_rw", [128, 8]), own("f_rw1", [128, 8])

        T.passed, T.low_loaded, T.low_cleared, T.high_loaded, T.high_cleared = (
            ctx.enter_context(nc.semaphore(n)) for n in ("passed", "low_loaded", "low_cleared", "high_loaded", "high_cleared"))
        load_first(nc, a, T)
        if "a0" in STAGES:
            ones_beside_v(nc, ATTN0, T)
            attention(nc, ATTN0, T)
        if "x0" in STAGES:
            ones_beside_v(nc, CROSS0, T)
            attention(nc, CROSS0, T)
        if "f0" in STAGES:
            sparse_experts(nc, a, T, F, banks)
            ffn0(nc, T, F, banks)
        if "a1" in STAGES:
            ones_beside_v(nc, ATTN1, T)
            attention(nc, ATTN1, T)
        if "x1" in STAGES:
            ones_beside_v(nc, CROSS1, T)
            attention(nc, CROSS1, T)
        if "f1" in STAGES:
            route(nc, a, T, G, banks)
            experts(nc, a, T, G, banks, out)
        else:
            store(nc, T, out)


def constants():
    q, k = np.arange(128)[:, None], np.arange(128)[None, :]
    masks = np.concatenate([np.where(k > q, MASKED, 0.0), np.where(q > k, MASKED, 0.0)], 1).astype(np.float32)
    row = np.arange(128)[:, None] % 64
    blockmask = np.concatenate([row // 8 == np.arange(8), row // 16 == np.arange(4)], 1).astype(np.float32)
    onerows = np.zeros((128, 24), np.float32)
    for j in range(8):
        onerows[[MAX_HI + j, MAX_LO + j], j] = 1.0
        if j < 4:
            onerows[[[MAX_HI + j], [MAX_LO + j]], 8 + j + 4 * np.arange(4)] = 1.0
    freq = (1.0 / 10000.0 ** (np.arange(0, 8, 2, dtype=np.float32) / 8)).astype(np.float32)
    ang = np.arange(128, dtype=np.float32)[:, None] * freq[None, :]
    cos, sin = np.cos(ang), np.sin(ang)
    rope = np.concatenate([cos, cos, -sin, sin], 1).astype(np.float32)
    g = np.arange(GROUPS)
    return {"ident": np.eye(128, dtype=np.float32), "masks": masks, "blockmask": blockmask,
            "onerows": onerows, "rope": rope,
            "iota": np.arange(E1, dtype=np.float32),
            "lower": (g[None, :] < g[:, None]).astype(np.float32).reshape(-1)}


TRANSPOSED = ("L0_attn_Wq", "L0_attn_Wk", "L0_attn_Wv", "L0_attn_Wo", "L1_attn_Wk", "L1_attn_Wv", "L1_attn_Wo",
              "L1_xattn_Wq", "L1_xattn_Wkv_expand", "L1_xattn_Wout", "L0_ffn_W", "L0_ffn_gate_w")


def layout(inputs):
    a = {k: np.asarray(v) for k, v in inputs.items()}
    for name in TRANSPOSED:
        a[name] = a[name].T
    a["L1_attn_Wq"] = a["L1_attn_Wq"].reshape(8, 4, 8, D).transpose(1, 0, 2, 3).reshape(D, D).T
    a["importance"] = a.pop("L0_ffn_importance").reshape(E0, NS // 128, 128).transpose(2, 1, 0).reshape(128, -1)
    a["mask_idx_columns"] = a["L0_ffn_mask_idx"].reshape(NS // 128, 128).T
    a = {k: np.ascontiguousarray(v) for k, v in a.items()}
    a.update(constants())
    return a


def kernel(**inputs):
    import concourse.bacc as bacc
    from concourse.bass_utils import run_bass_kernel_spmd

    nc = bacc.Bacc("TRN2", target_bir_lowering=False, num_devices=1)
    arrays = {f"in_{k}": v for k, v in layout(inputs).items()}
    aps = {k[3:]: nc.dram_tensor(k, v.shape, mybir.dt.from_np(v.dtype), kind="ExternalInput").ap() for k, v in arrays.items()}
    out = nc.dram_tensor("out", (B, S, D), F32, kind="ExternalOutput").ap()
    decoder(nc, aps, out)
    return run_bass_kernel_spmd(nc, [arrays], core_ids=[0]).results[0]["out"]
```

```python
from contextlib import ExitStack

import numpy as np

import concourse.bass as bass
from concourse import mybir

F32 = mybir.dt.float32
F32R = mybir.dt.float32r
BF16 = mybir.dt.bfloat16
I32 = mybir.dt.int32
U32 = mybir.dt.uint32
ALU = mybir.AluOpType
ACT = mybir.ActivationFunctionType
AX = mybir.AxisListType

B, S, D = 8, 128, 256
KT = D // 128
CTX = 64
EPS = 1e-5
HEAD_ROWS = 64
MAX_HI, MAX_LO = HEAD_ROWS, HEAD_ROWS + 8
MAX_END = HEAD_ROWS + 16
MASKED = -1e30
E0, ATOMS, NS = 8, 64, 2048
E1, TOP, MI = 32, 6, 176
GROUPS, TOP_GROUPS = 4, 2
UNITS = E1 + 2
MH = MI // 2
EQ = 4
LOW = 18
ENTRIES = B * TOP
PART = 6
SLOTS = (ENTRIES * S + E1 * 127) // 128 + 3 & ~3
LEAD = 2


class Cfg:

    def __init__(self, name, wide, causal, scale, own_kv, project, rope, bias, out):
        self.name, self.causal, self.scale = name, causal, scale
        self.wide = wide
        self.own_kv, self.project, self.rope, self.bias, self.out = own_kv, project, rope, bias, out
        self.quads = 4 if wide else 8
        self.blocks = 16 if wide else 8
        self.kv_heads = 16 if wide else 8
        self.d = 16 if wide else 8
        self.kcols = 4 if wide else 1
        self.rows = self.quads * (self.d + 1)

    def values(self, vaug):
        step = self.kv_heads // self.quads * self.rows
        v = vaug[:, 0:self.quads * (step + self.d + 1)].rearrange("p (i z) -> p i z", i=self.quads)
        if self.wide:
            return v[:, :, 0:step].rearrange("p i (j r) -> p i j r", r=self.rows)[:, :, :, 0:self.d + 1]
        return v[:, :, 0:self.d + 1]

    def heads(self, v):
        if self.wide:
            return v.rearrange("p (i j e) -> p i j e", i=4, e=self.d)
        return v.rearrange("p (i e) -> p i e", e=self.d)


ATTN0 = Cfg("a0", True, True, 0.25, True, True, False, True, True)
CROSS0 = Cfg("x0", False, False, 8.0 ** -0.5, False, False, False, False, False)
ATTN1 = Cfg("a1", False, True, 8.0 ** -0.5, True, True, True, False, True)
CROSS1 = Cfg("x1", True, True, 0.25, False, True, False, False, True)


def wait_apart(T, eng, sem, value):
    eng.wait_ge(sem, value)
    eng.sem_inc(T.passed, 1)


class Stage:

    def __init__(self, nc, prefix):
        self.nc, self.prefix, self.sems = nc, prefix, []

    def sem(self, name):
        self.sems.append(self.nc.alloc_semaphore(f"{self.prefix}_{name}"))
        return self.sems[-1]

    def __enter__(self):
        return self

    def __exit__(self, *failed):
        if not failed[0]:
            self.nc.clear_and_free_semaphores(self.sems)
            self.nc.all_engine_barrier()


def attention(nc, cfg, T, F):
    NQ, d, KVH = cfg.quads, cfg.d, cfg.kv_heads
    HEADS = 16 if cfg.wide else 32
    R = cfg.rows
    with Stage(nc, cfg.name) as stage, ExitStack() as ctx:
        sem = stage.sem

        loaded = [sem("loaded0"), sem("loaded1")]
        xt_done = sem("xt_done")
        xt_copied = sem("xt_copied")
        proj_done = sem("proj_done")
        qk_copied = sem("qk_copied")
        v_copied = sem("v_copied")
        t2_done = sem("t2_done")
        t2_low_done = sem("t2_low_done")
        rounded = sem("rounded")
        split = sem("split")
        q_ready = sem("q_ready")
        q_clear = sem("q_clear")
        k_ready = sem("k_ready")
        k2_ready = sem("k2_ready")
        v_cleared = sem("v_cleared")
        v_ones = sem("v_ones")
        ones_set = sem("ones_set")
        s_done = sem("s_done")
        max_done = sem("max_done")
        nm_hi = sem("nm_hi")
        nm_split = sem("nm_split")
        nm_done = sem("nm_done")
        nm_ready = sem("nm_ready")
        st_done = sem("st_done")
        exp_done = sem("exp_done")
        pv_done = sem("pv_done")
        pv_copied = sem("pv_copied")
        pv_ready = sem("pv_ready")
        rec_done = sem("rec_done")
        att_ready = sem("att_ready")
        at_done = sem("at_done")
        at_copied = sem("at_copied")
        out_done = sem("out_done")
        bias_done = sem("bias_done")
        res_done = sem("res_done")
        stat_done = sem("stat_done")
        aggr_done = sem("aggr_done")
        var_done = sem("var_done")
        rstd_done = sem("rstd_done")
        ln_done = sem("ln_done")
        permuted = sem("permuted")
        entries_copied = sem("entries_copied")
        placed = sem("placed")
        rope_a = sem("rope_a")

        block = ctx.enter_context(nc.Block())
        PA, PB, M, PV = T.PA, T.PB, T.M, T.PV
        pb_read = k_ready if cfg.wide else k2_ready
        SB, STB = T.SB, T.STB

        @block.sync
        def _(sp):
            def load(n, par):
                if cfg.project and not (isinstance(n, int) and n < 2):
                    sp.dma_start(T.xs[par][:], T.x_all[:, bass.ds(n, 1), :].rearrange("p a c -> p (a c)")).then_inc(loaded[par], 16)
                if not cfg.own_kv:
                    sp.dma_start(T.cs[par][:], T.ctx_tiles[bass.ds(n, 1), :, :].rearrange("a p c -> p (a c)")).then_inc(loaded[par], 16)

            load(0, 0)
            load(1, 1)
            with sp.Fori(1, B // 2) as i:
                for par in range(2):
                    if cfg.project:
                        sp.wait_ge(xt_done, i * 2 + (par - 1))
                    else:
                        sp.wait_ge(v_copied, i * 2 + (par - 1))
                        sp.wait_ge(split, i * 2 + (par - 1))
                    load(i * 2 + par, par)

        first_load = 0 if cfg.own_kv else 16
        per_load = first_load + (16 if cfg.project else 0)

        def wait_loaded(eng, n, par):
            if not isinstance(n, int):
                eng.wait_ge(loaded[par], (n - par) * (per_load // 2) + first_load)
            elif n > 1 or first_load:
                eng.wait_ge(loaded[par], n // 2 * per_load + first_load)

        def all_batches(eng, iteration):
            iteration(0, 0, False, True, True)
            iteration(1, 1, True, True, True)
            with eng.Fori(1, B // 2 - 1) as i:
                iteration(i * 2, 0, True, True, True)
                iteration(i * 2 + 1, 1, True, True, True)
            iteration(B - 2, 0, True, True, False)
            iteration(B - 1, 1, True, False, False)

        @block.tensor
        def _(pe):
            def transpose_x(n, par):
                wait_loaded(pe, n, par)
                if not (isinstance(n, int) and n == 0):
                    pe.wait_ge(q_ready, n)
                x = T.x_all[:, n, :] if isinstance(n, int) and n < 2 else T.xs[par][:]
                for j in range(KT):
                    last = pe.transpose(PA[:, j * 128:(j + 1) * 128], x[:, j * 128:(j + 1) * 128], T.ident[:])
                if not cfg.own_kv:
                    last = pe.transpose(PA[0:CTX, 256:384], T.cs[par][:], T.ident[:])
                last.then_inc(xt_done, 1)

            def project(n):
                pe.wait_ge(xt_copied, n + 1)
                if not (isinstance(n, int) and n == 0):
                    pe.wait_ge(pb_read, n)
                if cfg is ATTN0:
                    parts = [(PA[:, 0:512], T.a0_wqk), (PB[:, 0:256], T.a0_wv)]
                elif cfg is ATTN1:
                    parts = [(PA[:, 0:320], T.a1_wqkv[:, :, 0:320]), (PB[:, 0:64], T.a1_wqkv[:, :, 320:384])]
                else:
                    parts = [(PB[:, 0:256], T.x1_wq)]
                    pe.matmul(PA[:, 0:512], T.xT[0:CTX, 256:384], T.x1_wkv[0:CTX, :], start=True, stop=True)
                for out, w in parts:
                    for j in range(KT):
                        last = pe.matmul(out, T.xT[:, j * 128:(j + 1) * 128], w[:, j, :], start=(j == 0), stop=(j == KT - 1))
                last.then_inc(proj_done, 1)

            def transpose_qk(n):
                pe.wait_ge(rounded, n + 1)
                pe.wait_ge(split, n + 1)
                pe.wait_ge(v_copied, n + 1)
                if not cfg.project and not (isinstance(n, int) and n == 0):
                    pe.wait_ge(q_ready, n)
                    pe.wait_ge(pb_read, n)
                pe.sem_inc(T.passed, 1)
                for g in range(4):
                    pe.transpose(PA[:, g * 128:(g + 1) * 128], T.qs[:, g, :].bitcast(F32), T.ident[:])
                if not cfg.wide:
                    pe.transpose(PB[0:64, 128:256], T.ks2[:, 0, :].bitcast(F32), T.ident[:]).then_inc(t2_low_done, 1)
                for c in range(cfg.kcols):
                    last = pe.transpose(PB[:, c * 128:(c + 1) * 128], T.ks1[:, c, :].bitcast(F32), T.ident[:])
                last.then_inc(t2_done, 1)

            def transpose_k_low(n):
                if not cfg.wide:
                    return
                if not (isinstance(n, int) and n == 0):
                    wait_apart(T, pe, nm_ready, n)
                for c in range(cfg.kcols):
                    last = pe.transpose(M[0:64, c * 128:(c + 1) * 128], T.ks2[:, c, :].bitcast(F32), T.ident[:])
                last.then_inc(t2_low_done, 1)

            def scores(n, par, i):
                if i == 0:
                    pe.wait_ge(q_ready, n + 1)
                    pe.wait_ge(q_clear, n + 1)
                    pe.wait_ge(k_ready, n + 1)
                    pe.wait_ge(k2_ready, n + 1)
                    if isinstance(n, int) and n == 0:
                        pe.wait_ge(ones_set, 2)
                if not (isinstance(n, int) and n == 0 and i < 2):
                    pe.wait_ge(max_done, n * NQ + (i - 1))
                bank = SB[i % 2]
                if cfg.causal:
                    pe.matmul(bank[:, :], T.ident_bf[:], T.mask_qk[:], start=True, stop=False)
                g = i if cfg.wide else i // 2
                blocks = slice(4 * i, 4 * i + 4) if cfg.wide else slice(4 * (i % 2), 4 * (i % 2) + 4)
                pe.matmul(bank[:, :], T.q1[par][:, g, :], T.kb1[par][:, blocks, :], start=not cfg.causal, stop=False)
                pe.matmul(bank[:, :], T.q2[par][:, g, :], T.kb2[par][:, blocks, :], start=False, stop=True).then_inc(s_done, 1)

            def transpose_maxima(n):
                pe.wait_ge(nm_split, n + 1)
                if cfg.wide:
                    pe.wait_ge(k2_ready, n + 1)
                if cfg.out and not (isinstance(n, int) and n < 2):
                    pe.wait_ge(res_done, n - 1)
                for g in range(4):
                    last = pe.transpose(M[:, g * 128:(g + 1) * 128], T.nm[:, g, :].bitcast(F32), T.ident[:])
                last.then_inc(nm_done, 1)

            def scores_t(b, par, i):
                if i == 0:
                    pe.wait_ge(nm_ready, b + 1)
                if not (isinstance(b, int) and b == 0 and i < 2):
                    pe.wait_ge(exp_done, b * NQ + (i - 1))
                bank = STB[i % 2]
                if cfg.wide:
                    for j in range(4):
                        block = bank[:, j * 128:(j + 1) * 128]
                        pe.matmul(block, T.ident_bf[:], T.mask_kq[:, 0:128], start=True, stop=False)
                        pe.matmul(block, T.kb1[par][:, 4 * i + j, :], T.q1[par][:, i, :], start=False, stop=False)
                        last = pe.matmul(block, T.kb2[par][:, 4 * i + j, :], T.q2[par][:, i, :], start=False, stop=True)
                else:
                    if cfg.causal:
                        pe.matmul(bank[:, :], T.ident_bf[:], T.mask_kq[:], start=True, stop=False)
                    pe.matmul(bank[:, :], T.kb1[par][:, i, :], T.q1[par][:, :, :], start=not cfg.causal, stop=False)
                    last = pe.matmul(bank[:, :], T.kb2[par][:, i, :], T.q2[par][:, :, :], start=False, stop=True)
                last.then_inc(st_done, 1)

            def values(b, par, i):
                pe.wait_ge(exp_done, b * NQ + (i + 1))
                if i == 0:
                    pe.wait_ge(v_copied, b + 1)
                    if not (isinstance(b, int) and b == 0):
                        pe.wait_ge(att_ready, b)
                per_quad = KVH // NQ
                width = 512 // per_quad
                for j in range(per_quad):
                    block = (i * per_quad + j) * R
                    last = pe.matmul(PV[0:R, j * width:(j + 1) * width], T.vaug[par][:, block:block + R],
                                     T.pt[i % 2][:, j * width:(j + 1) * width], start=(i == 0 and j == 0), stop=(i == NQ - 1),
                                     skip_group_check=True)
                if i == NQ - 1:
                    last.then_inc(pv_done, 1)

            def transpose_pv(b):
                wait_apart(T, pe, pv_copied, b + 1)
                for j in range(4):
                    last = pe.transpose(PV[:, j * R:(j + 1) * R], T.pvs[0:R, j * 128:(j + 1) * 128], T.ident[0:R, 0:R])
                last.then_inc(pv_ready, 1)

            def project_out(m):
                pe.wait_ge(at_copied, m + 1)
                for j in range(KT):
                    last = pe.matmul(M[:, 0:256], T.atT[:, j * 128:(j + 1) * 128], T.wo[cfg.name][:, j, :],
                                     start=(j == 0), stop=(j == KT - 1))
                last.then_inc(out_done, 1)

            def transpose_att(m, has_later):
                pe.wait_ge(att_ready, m + 1)
                if has_later and cfg.wide:
                    pe.wait_ge(k2_ready, m + 3)
                elif not cfg.wide:
                    pe.wait_ge(nm_ready, min(m + 2, B) if isinstance(m, int) else m + 2)
                    if isinstance(m, int) and m == B - 1:
                        pe.wait_ge(res_done, m)
                elif isinstance(m, int) and m == B - 1:
                    pe.wait_ge(res_done, m)
                for j in range(KT):
                    last = pe.transpose(M[:, j * 128:(j + 1) * 128], T.att[:, j * 128:(j + 1) * 128], T.ident[:])
                last.then_inc(at_done, 1)

            def iteration(b, par, has_prev, has_next, has_second):
                for i in range(NQ + LEAD):
                    if i < NQ:
                        scores_t(b, par, i)
                    if i == 0 and cfg.project and has_second:
                        transpose_x(b + 2, par)
                    if 1 <= i <= NQ:
                        values(b, par, i - 1)
                    if i == 1 and cfg.project and has_second:
                        project(b + 2)
                    if i == 2 and cfg.out and has_prev:
                        transpose_att(b - 1, has_next)
                    if i >= LEAD and has_next:
                        scores(b + 1, 1 - par, i - LEAD)
                    if i == 3 and cfg.out and has_prev:
                        project_out(b - 1)
                if has_second:
                    transpose_qk(b + 2)
                transpose_pv(b)
                if has_next:
                    transpose_maxima(b + 1)
                if has_second:
                    transpose_k_low(b + 2)

            if cfg.project:
                transpose_x(0, 0)
                project(0)
            transpose_qk(0)
            transpose_k_low(0)
            if cfg.project:
                transpose_x(1, 1)
            for i in range(NQ):
                scores(0, 0, i)
            if cfg.project:
                project(1)
            transpose_maxima(0)
            transpose_qk(1)
            transpose_k_low(1)
            all_batches(pe, iteration)
            if cfg.out:
                transpose_att(B - 1, False)
                project_out(B - 1)

        @block.scalar
        def _(act):
            def copy_xt(n):
                act.wait_ge(xt_done, n + 1)
                last = act.activation(T.xT[:, 0:256], PA[:, 0:256], ACT.Copy)
                if not cfg.own_kv:
                    last = act.activation(T.xT[0:CTX, 256:384], PA[0:CTX, 256:384], ACT.Copy)
                last.then_inc(xt_copied, 1)

            def copy_proj(n):
                if cfg is CROSS1:
                    act.wait_ge(proj_done, n + 1)
                    act.activation(T.qk[:, 0:256], PB[:, 0:256], ACT.Copy)
                    act.activation(T.qk[:, 256:512], PA[:, 0:256], ACT.Copy).then_inc(qk_copied, 1)

            def copy_v(n, par):
                if cfg is ATTN0:
                    return
                if isinstance(n, int) and n < 2:
                    act.wait_ge(v_ones, 2)
                else:
                    act.wait_ge(pv_done, n - 1)
                if cfg is ATTN1:
                    act.wait_ge(proj_done, n + 1)
                    v = PB[:, 0:64]
                else:
                    v = PA[:, 256:512] if cfg.project else T.cs[par][:, :]
                act.activation(cfg.values(T.vaug[par])[..., 0:d], cfg.heads(v), ACT.Copy).then_inc(v_copied, 1)

            def round_qk(n, par):
                if cfg.project:
                    act.wait_ge(qk_copied, n + 1)
                    k = T.qk[:, 256:256 + 64 * cfg.kcols]
                else:
                    act.wait_ge(permuted, n + 1)
                    wait_loaded(act, n, par)
                    k = T.cs[par][:, :]
                if not (isinstance(n, int) and n == 0):
                    act.wait_ge(t2_low_done if cfg.wide else t2_done, n)
                act.activation(T.qs[:, :, 0:64], T.qk[:, 0:256].rearrange("p (g c) -> p g c", g=4), ACT.Copy)
                k3 = k.rearrange("p (c e) -> p c e", e=64)
                act.activation(T.ks1[:, 0:cfg.kcols, 0:64], k3, ACT.Copy)
                act.activation(T.ks1[:, 0:cfg.kcols, 64:128], k3, ACT.Copy).then_inc(rounded, 1)

            def copy_q(n, par):
                act.wait_ge(t2_done, n + 1)
                act.activation(T.q1[par][:, :, :].rearrange("p g q -> p (g q)"), PA[:, :], ACT.Copy)
                act.activation(T.q2[par][0:64, :, :].rearrange("p g q -> p (g q)"), PA[0:64, :], ACT.Copy).then_inc(q_ready, 1)

            def copy_k_low(n, par):
                if cfg.wide:
                    act.wait_ge(t2_low_done, n + 1)
                    out = T.kb2[par][0:64, :, :].rearrange("p (c j) k -> p c j k", j=4)
                    for j in range(4):
                        last = act.activation(out[:, :, j, :], M[0:64, :].rearrange("p (c k) -> p c k", c=4), ACT.Copy,
                                              scale=T.blockmask[0:64, 8 + j:9 + j])
                    last.then_inc(k2_ready, 1)

            def copy_maxima(n, par):
                act.wait_ge(nm_done, n + 1)
                act.activation(T.q2[par][MAX_HI:MAX_END, :, :].rearrange("p g q -> p (g q)"),
                               M[MAX_HI:MAX_END, :], ACT.Copy).then_inc(nm_ready, 1)

            def copy_att(m):
                act.wait_ge(at_done, m + 1)
                act.activation(T.atT[:], M[:, 0:256], ACT.Copy).then_inc(at_copied, 1)

            def iteration(b, par, has_prev, has_next, has_second):
                if has_next:
                    copy_q(b + 1, 1 - par)
                for i in range(NQ):
                    act.wait_ge(st_done, b * NQ + (i + 1))
                    act.activation(T.pt[i % 2][:, :], STB[i % 2][:, :], ACT.Exp, scale=cfg.scale).then_inc(exp_done, 1)
                    if i == 0:
                        if cfg.project and has_second:
                            copy_xt(b + 2)
                        if has_next:
                            copy_k_low(b + 1, 1 - par)
                    if i == 1 and cfg.out and has_prev:
                        copy_att(b - 1)
                    if i == 2 and has_second:
                        copy_proj(b + 2)
                    if i == 3 and has_second:
                        round_qk(b + 2, par)
                act.wait_ge(pv_done, b + 1)
                act.activation(T.pvs[0:R, :], PV[0:R, :], ACT.Copy).then_inc(pv_copied, 1)
                if has_second:
                    copy_v(b + 2, par)
                if has_next:
                    copy_maxima(b + 1, 1 - par)

            if cfg.project:
                copy_xt(0)
            copy_proj(0)
            round_qk(0, 0)
            copy_v(0, 0)
            copy_q(0, 0)
            copy_k_low(0, 0)
            if cfg.project:
                copy_xt(1)
            copy_proj(1)
            copy_maxima(0, 0)
            round_qk(1, 1)
            copy_v(1, 1)
            all_batches(act, iteration)
            if cfg.out:
                copy_att(B - 1)

        @block.vector
        def _(dve):
            def proj(n):
                if cfg is ATTN0:
                    dve.wait_ge(proj_done, n + 1)
                    dve.tensor_tensor(T.qk[:, :], PA[:, 0:512], T.b_qk[:], ALU.add).then_inc(qk_copied, 1)
                elif cfg is ATTN1:
                    dve.wait_ge(proj_done, n + 1)
                    src = PA[:, 0:320].rearrange("p (h e) -> p h e", e=d)
                    cos = T.rope[:, 0:8].unsqueeze(1).broadcast_to([128, 40, 8])
                    half = d // 2
                    a = T.rope_a[:, :].rearrange("p (h e) -> p h e", e=d)
                    r = T.rope_b[:, :].rearrange("p (h e) -> p h e", e=d)
                    dve.tensor_tensor(a, src, cos, ALU.mult).then_inc(rope_a, 1)
                    for lo in (0, half):
                        sin = T.rope[:, 8 + lo:8 + lo + half].unsqueeze(1).broadcast_to([128, 40, half])
                        dve.tensor_tensor(r[:, :, lo:lo + half], src[:, :, half - lo:d - lo], sin, ALU.mult).then_inc(rope_a, 1)
                    dve.wait_ge(rope_a, (n + 1) * 3)
                    dve.tensor_tensor(T.qk[:, 0:320], T.rope_a[:, :], T.rope_b[:, :], ALU.add).then_inc(qk_copied, 1)

            def copy_v(n, par):
                if cfg is ATTN0:
                    if isinstance(n, int) and n < 2:
                        dve.wait_ge(v_ones, 2)
                    else:
                        dve.wait_ge(pv_done, n - 1)
                    dve.tensor_tensor(cfg.values(T.vaug[par])[..., 0:d], cfg.heads(PB[:, 0:256]), cfg.heads(T.b_v[:]),
                                      ALU.add).then_inc(v_copied, 1)

            def keys(n, par):
                dve.wait_ge(t2_done, n + 1)
                if cfg.wide:
                    out = T.kb1[par][:, :, :].rearrange("p (c j) k -> p c j k", j=4)
                    for j in range(4):
                        last = dve.tensor_scalar(out[:, :, j, :], PB[:, :].rearrange("p (c k) -> p c k", c=4),
                                                 T.blockmask[:, 8 + j:9 + j], None, ALU.mult)
                    last.then_inc(k_ready, 1)
                else:
                    for rows, out, bank, done, ready in ((128, T.kb1[par], PB[:, 0:128], t2_done, k_ready), (64, T.kb2[par], PB[:, 128:256], t2_low_done, k2_ready)):
                        dve.wait_ge(done, n + 1)
                        dve.tensor_tensor(out[0:rows, 0:8, :], bank[0:rows, :].unsqueeze(1).broadcast_to([rows, 8, 128]),
                                          T.blockmask[0:rows, 0:8].unsqueeze(2).broadcast_to([rows, 8, 128]),
                                          ALU.mult).then_inc(ready, 1)

            def normalise(m):
                dve.wait_ge(pv_ready, m + 1)
                pv = PV[:, 0:HEADS * (d + 1)].rearrange("p (h e) -> p h e", e=d + 1)
                dve.reciprocal(T.rec[:, 0:HEADS], pv[:, :, d]).then_inc(rec_done, 1)
                dve.wait_ge(rec_done, m + 1)
                dve.tensor_tensor(T.att[:, :].rearrange("p (i j e) -> p j i e", j=4, e=d),
                                  PV[:, 0:4 * R].rearrange("p (j i e) -> p j i e", j=4, e=d + 1)[:, :, :, 0:d],
                                  T.rec[:, 0:HEADS].rearrange("p (j i) -> p j i", j=4).unsqueeze(3).broadcast_to([128, 4, NQ, d]),
                                  ALU.mult).then_inc(att_ready, 1)

            def residual(m):
                x = T.x_all[:, bass.ds(m, 1), :].rearrange("p a c -> p (a c)")
                if cfg.out:
                    if cfg.bias:
                        dve.tensor_tensor(T.xb[:], x, T.b_o[:], ALU.add).then_inc(bias_done, 1)
                        dve.wait_ge(bias_done, m + 1)
                        x = T.xb[:]
                    dve.wait_ge(out_done, m + 1)
                    dve.tensor_tensor(T.res[:], M[:, 0:256], x, ALU.add).then_inc(res_done, 1)
                else:
                    dve.wait_ge(att_ready, m + 1)
                    dve.tensor_tensor(T.res[:], T.att[:], x, ALU.add).then_inc(res_done, 1)

            def statistics(m):
                dve.wait_ge(res_done, m + 1)
                dve.bn_stats(T.stats[:], T.res[:]).then_inc(stat_done, 1)
                wait_apart(T, dve, stat_done, m + 1)
                dve.bn_aggr(T.mv[:], T.stats[:]).then_inc(aggr_done, 1)
                dve.wait_ge(aggr_done, m + 1)
                dve.tensor_scalar(T.vare[:], T.mv[:, 1:2], EPS, None, ALU.add).then_inc(var_done, 1)

            def norm(m):
                dve.wait_ge(rstd_done, m + 1)
                x = T.x_all[:, bass.ds(m, 1), :].rearrange("p a c -> p (a c)")
                dve.tensor_scalar(x, T.res[:], T.mv[:, 0:1], T.rstd[:], ALU.subtract, ALU.mult).then_inc(ln_done, 1)

            def maxima(n, i):
                dve.wait_ge(s_done, n * NQ + (i + 1))
                g = i if cfg.wide else i // 2
                at = 0 if cfg.wide else 4 * (i % 2)
                dve.tensor_reduce(T.nmf[:, g, at:at + 4], SB[i % 2][:, :].rearrange("p (h k) -> p h k", h=4),
                                  AX.X, ALU.max, negate=True).then_inc(max_done, 1)

            def split_maxima(n):
                heads = 4 if cfg.wide else 8
                dve.wait_ge(max_done, n * NQ + NQ)
                dve.tensor_copy(T.nm[:, :, MAX_HI:MAX_HI + heads], T.nmf[:, :, 0:heads]).then_inc(nm_hi, 1)
                dve.wait_ge(nm_hi, n + 1)
                dve.tensor_tensor(T.nm[:, :, MAX_LO:MAX_LO + heads], T.nmf[:, :, 0:heads],
                                  T.nm[:, :, MAX_HI:MAX_HI + heads].bitcast(F32), ALU.subtract).then_inc(nm_split, 1)

            def iteration(b, par, has_prev, has_next, has_second):
                if has_next:
                    keys(b + 1, 1 - par)
                for i in range(NQ):
                    if i == NQ - 1 and has_second:
                        copy_v(b + 2, par)
                    if i == 0 and cfg.project and has_second:
                        proj(b + 2)
                    if has_next:
                        maxima(b + 1, i)
                    if i == 1 and has_prev:
                        residual(b - 1)
                        statistics(b - 1)
                    if i == 2 and has_prev and not cfg.wide:
                        norm(b - 1)
                if has_next:
                    split_maxima(b + 1)
                if has_prev and cfg.wide:
                    norm(b - 1)
                normalise(b)

            blocks = T.onerows[64:128, 8:24] if cfg.wide else T.onerows[64:128, 0:8]
            for par in range(2):
                dve.tensor_copy(T.kb2[par][64:128, 0:cfg.blocks, :], blocks.unsqueeze(2).broadcast_to([64, cfg.blocks, 128])).then_inc(ones_set, 1)
            if cfg is CROSS0:
                dve.wait_ge(T.later_loaded, T.later_count)
                dve.tensor_copy(T.before_bf[:], T.before[:])
                dve.tensor_copy(T.columns_bf[:], T.columns[:])
            if cfg.project:
                proj(0)
            copy_v(0, 0)
            keys(0, 0)
            for i in range(NQ):
                maxima(0, i)
            if cfg.project:
                proj(1)
            split_maxima(0)
            copy_v(1, 1)
            all_batches(dve, iteration)
            residual(B - 1)
            statistics(B - 1)
            norm(B - 1)

        @block.gpsimd
        def _(pool):
            def permute(n):
                if not (isinstance(n, int) and n == 0):
                    pool.wait_ge(rounded, n)
                    pool.wait_ge(split, n)
                    pool.wait_ge(q_clear, n)
                pool.tensor_copy(T.qk[:, 0:256].rearrange("p (g v d) -> p g v d", g=4, d=8),
                                 T.x_all[:, bass.ds(n, 1), :].rearrange("p a (v g d) -> p (a g) v d", g=4, d=8)
                                 ).then_inc(permuted, 1)

            def low_parts(n, par):
                pool.wait_ge(rounded, n + 1)
                if not (isinstance(n, int) and n == 0):
                    pool.wait_ge(q_clear, n)
                k = T.qk[:, 256:256 + 64 * cfg.kcols] if cfg.project else T.cs[par][:, :]
                pool.tensor_tensor(T.qs[:, :, 64:128], T.qk[:, 0:256].rearrange("p (g c) -> p g c", g=4),
                                   T.qs[:, :, 0:64].bitcast(F32), ALU.subtract)
                pool.tensor_tensor(T.ks2[:, 0:cfg.kcols, :], k.rearrange("p (c e) -> p c e", e=64),
                                   T.ks1[:, 0:cfg.kcols, 0:64].bitcast(F32), ALU.subtract).then_inc(split, 1)

            def clear(n, par):
                pool.wait_ge(t2_done, n + 1)
                pool.wait_ge(split, n + 1)
                if not (isinstance(n, int) and n < 3):
                    pool.wait_ge(rstd_done, n - 2)
                pool.sem_inc(T.passed, 1)
                pool.memset(T.q2[par][64:128, :, :].bitcast(F32), 0.0).then_inc(q_clear, 1)

            def rstd(m, cleared):
                pool.wait_ge(var_done, m + 1)
                pool.wait_ge(q_clear, cleared)
                pool.tensor_tensor(T.rstd[:], T.vare[:], T.half[:], ALU.pow).then_inc(rstd_done, 1)

            def place_entries(b):
                if not (isinstance(b, int) and b == 0):
                    pool.wait_ge(placed, b * 16)
                if not (isinstance(b, int) and b == B - 1):
                    pool.wait_ge(q_clear, b + 2)
                else:
                    pool.wait_ge(q_clear, B)
                t = b + (B if cfg is CROSS0 else 0)
                pool.tensor_copy(F.pos_now[:], F.pos[:, bass.ds(t, 1)])
                pool.tensor_copy(F.sum_now[:], F.sum8[:, bass.ds(t, 1), :].rearrange("p a e -> p (a e)")).then_inc(entries_copied, 1)
                wait_apart(T, pool, entries_copied, b + 1)
                pool.indirect_dma_start(F.table[:, :], bass.IndirectOffsetOnAxis(ap=F.pos_now[:], axis=0),
                                        F.sum_now[:], None).then_inc(placed, 16)

            def iteration(b, par, has_prev, has_next, has_second):
                if has_next:
                    clear(b + 1, 1 - par)
                if not cfg.project and has_second:
                    permute(b + 2)
                if has_second and cfg.wide:
                    low_parts(b + 2, par)
                if has_prev:
                    rstd(b - 1, b + 2 if has_next else B)
                if has_second and not cfg.wide:
                    low_parts(b + 2, par)
                if cfg in (ATTN0, CROSS0):
                    place_entries(b)

            for par in range(2):
                pool.memset(T.vaug[par][:], 0.0).then_inc(v_cleared, 1)
            pool.wait_ge(v_cleared, 2)
            for par in range(2):
                pool.memset(cfg.values(T.vaug[par])[..., d:d + 1], 1.0).then_inc(v_ones, 1)
            if not cfg.project:
                permute(0)
            low_parts(0, 0)
            clear(0, 0)
            if not cfg.project:
                permute(1)
            low_parts(1, 1)
            all_batches(pool, iteration)
            rstd(B - 1, B)
            if cfg in (ATTN0, CROSS0):
                pool.wait_ge(placed, B * 16)


class Memory:

    def __init__(self, nc, start, end):
        self.nc, self.at, self.end = nc, start, end

    def __call__(self, name, shape, dt=F32):
        size = int(np.prod(shape[1:])) * (2 if dt == BF16 else 4)
        size = (size + 31) // 32 * 32
        assert self.at + size <= self.end, f"{name} does not fit: {self.at + size} > {self.end}"
        t = self.nc.alloc_sbuf_tensor_at(name, list(shape), dt, offset=self.at)
        self.at += size
        return t


class Tensors:
    pass


def flat(x_all, t):
    return x_all[:, bass.ds(t, 1), :].rearrange("p a c -> p (a c)")


def ktiles(w):
    return w.rearrange("(k p) n -> p k n", p=128)


def broadcast(v):
    return v.rearrange("(a n) -> a n", a=1).broadcast_to([128, v.shape[0]])


def load_first(nc, a, T, F, banks):
    sparse = [(F.idx_row[:], broadcast(a["L0_ffn_mask_idx"])), (F.idx_col[:], a["mask_idx_columns"]),
              (F.eaw[:], a["L0_ffn_expert_atom_weights"]), (F.atoms[:], a["L0_ffn_atoms"]), (F.imp[:], a["importance"]),
              (T.ident[:], a["ident"])]
    loads = [(T.x_all[:], a["x"].rearrange("b p c -> p b c")),
             (T.masks[:], a["masks"]), (T.blockmask[:], a["blockmask"]), (T.onerows[:], a["onerows"]),
             (T.a0_wqk[:, :, 0:256], ktiles(a["L0_attn_Wq"])), (T.a0_wqk[:, :, 256:512], ktiles(a["L0_attn_Wk"])),
             (T.a0_wv[:], ktiles(a["L0_attn_Wv"])), (T.a0_wo[:], ktiles(a["L0_attn_Wo"])),
             (T.b_qk[:, 0:256], broadcast(a["L0_attn_bq"])), (T.b_qk[:, 256:512], broadcast(a["L0_attn_bk"])),
             (T.b_v[:], broadcast(a["L0_attn_bv"])), (T.b_o[:], broadcast(a["L0_attn_bo"])),
             ]
    later = [(T.rope[:], a["rope"]), (T.a1_wqkv[:, :, 0:256], ktiles(a["L1_attn_Wq"])), (T.a1_wqkv[:, :, 256:320], ktiles(a["L1_attn_Wk"])),
             (T.a1_wqkv[:, :, 320:384], ktiles(a["L1_attn_Wv"])), (T.a1_wo[:], ktiles(a["L1_attn_Wo"])),
             (T.x1_wq[:], ktiles(a["L1_xattn_Wq"])), (T.x1_wkv[:], a["L1_xattn_Wkv_expand"]),
             (T.x1_wo[:], ktiles(a["L1_xattn_Wout"])), (T.f0_wg[:, :, 0:256], ktiles(a["L0_ffn_W"])),
             (T.f0_wg[:, :, 256:264], ktiles(a["L0_ffn_gate_w"])), (T.f1_gate[:], ktiles(a["L1_ffn_gate_w"])),
             (T.row[:], a["row"]), (T.columns[:], broadcast(a["columns"])),
             (T.spare[:], a["spare"]), (T.before[:], a["before"]), (T.iota[:], broadcast(a["iota"])), (T.lower[:], broadcast(a["lower"]))]
    ST = NS // 128
    with Stage(nc, "m") as stage, ExitStack() as ctx:
        sem = stage.sem

        loaded = sem("loaded")
        sparse_loaded = sem("sparse_loaded")
        cleared = sem("cleared")
        zeroed = sem("zeroed")
        v = sem("v")
        act = sem("act")
        pe_s = sem("pe")
        eq_ready = sem("eq_ready")
        eq_used = sem("eq_used")
        columns_ready = sem("columns_ready")
        block = ctx.enter_context(nc.Block())
        table = F.table
        bank_t, bank_d, bank_c = banks[0], banks[1], banks[2]

        @block.sync
        def _(sp):
            for dst, src in sparse:
                sp.dma_start(dst, src).then_inc(sparse_loaded, 16)
            for dst, src in loads:
                sp.dma_start(dst, src).then_inc(loaded, 16)
            sp.wait_ge(cleared, 1)
            for j in range(KT):
                sp.dma_start(table[j * 128 * 256:(j + 1) * 128 * 256, :].rearrange("(p r) e -> p (r e)", p=128),
                             F.m_re[:, j, :]).then_inc(zeroed, 16)
            for dst, src in later:
                sp.dma_start(dst, src).then_inc(T.later_loaded, 16)
            T.later_count = 16 * len(later)
            sp.wait_ge(zeroed, 16 * KT)

        @block.scalar
        def _(eng):
            eng.wait_ge(v, 1)
            eng.activation(F.eaw[:], F.eaw[:], ACT.Exp, bias=F.eawmax[:], accum_out=F.eawsum[:]).then_inc(act, 1)
            eng.activation(F.imp[:], F.imp[:], ACT.Exp, scale=-1.0).then_inc(act, 1)
            eng.wait_ge(T.low_cleared, 1)
            eng.wait_ge(loaded, 16 * len(loads))
            T.low_count = load_units(a, T, range(LOW), eng, T.low_loaded)

        @block.tensor
        def _(pe):
            pe.wait_ge(v, 3)
            pe.transpose(bank_t[0:ATOMS, 0:E0], F.eaw[:], T.ident[0:E0, 0:E0]).then_inc(pe_s, 1)
            pe.wait_ge(v, 4)
            for t in range(ST):
                last = pe.matmul(bank_d[:, t * E0:(t + 1) * E0], F.atoms[:, t * 128:(t + 1) * 128], F.eawT[:],
                                 start=True, stop=True)
            last.then_inc(pe_s, 1)
            pe.wait_ge(v, 12)
            for t in range(ST):
                pe.wait_ge(eq_ready, t + 1)
                for u in range(ST):
                    last = pe.matmul(bank_c[:, u * 24:(u + 1) * 24], F.eq[t % EQ][:, u * 128:(u + 1) * 128],
                                     F.w3[:, t, :], start=(t == 0 and u == 0), stop=(t == ST - 1), skip_group_check=True)
                last.then_inc(eq_used, 1)

        @block.vector
        def _(dve):
            dve.memset(F.m_re[:], 0.0).then_inc(cleared, 1)
            dve.memset(T.nm[:].bitcast(F32), 0.0)
            dve.memset(T.half[:], -0.5)
            dve.memset(T.ones_bf[:], 1.0)
            dve.wait_ge(sparse_loaded, 16 * len(sparse))
            dve.tensor_copy(F.col_f[:], F.idx_col[:]).then_inc(columns_ready, 1)

            def equal_places(t):
                if t == 0:
                    dve.wait_ge(columns_ready, 1)
                if t >= EQ:
                    dve.wait_ge(eq_used, t - EQ + 1)
                dve.tensor_scalar(F.eq[t % EQ][:], F.idx_row[:], F.col_f[:, t:t + 1], None, ALU.is_equal).then_inc(eq_ready, 1)

            dve.tensor_reduce(F.eawmax[:], F.eaw[:], AX.X, ALU.max, negate=True).then_inc(v, 1)
            dve.wait_ge(act, 1)
            dve.reciprocal(F.eawsum[:], F.eawsum[:]).then_inc(v, 1)
            dve.wait_ge(v, 2)
            dve.tensor_scalar(F.eaw[:], F.eaw[:], F.eawsum[:], None, ALU.mult).then_inc(v, 1)
            dve.wait_ge(pe_s, 1)
            dve.tensor_copy(F.eawT[:], bank_t[0:ATOMS, 0:E0]).then_inc(v, 1)
            dve.wait_ge(act, 2)
            dve.tensor_scalar(F.imp[:], F.imp[:], 1.0, None, ALU.add).then_inc(v, 1)
            dve.wait_ge(v, 5)
            dve.reciprocal(F.imp[:], F.imp[:]).then_inc(v, 1)
            for t in range(EQ):
                equal_places(t)
            dve.wait_ge(v, 6)
            dve.wait_ge(pe_s, 2)
            dve.tensor_tensor(F.imp[:], bank_d[:, 0:ST * E0], F.imp[:], ALU.mult).then_inc(v, 1)
            imp = F.imp[:].rearrange("p (t e) -> p t e", e=E0)
            steps = 7
            for part in range(3):
                dve.wait_ge(v, steps)
                dve.tensor_copy(F.w3[:, :, part * 8:(part + 1) * 8], imp).then_inc(v, 1)
                steps += 1
                if part < 2:
                    dve.wait_ge(v, steps)
                    dve.tensor_tensor(imp, imp, F.w3[:, :, part * 8:(part + 1) * 8], ALU.subtract).then_inc(v, 1)
                    steps += 1
            for t in range(EQ, ST):
                equal_places(t)
            dve.tensor_scalar(F.pos_hi[:], F.idx_col[:], D - 1, 8, ALU.bitwise_and, ALU.logical_shift_left).then_inc(v, 1)
            dve.tensor_scalar(F.pos[:], F.idx_col[:], 8, None, ALU.logical_shift_right).then_inc(v, 1)
            dve.wait_ge(v, 14)
            dve.tensor_tensor(F.pos[:], F.pos[:], F.pos_hi[:], ALU.bitwise_or).then_inc(v, 1)
            dve.wait_ge(eq_used, ST)
            c = bank_c[:, 0:ST * 24].rearrange("p (t s e) -> p t s e", s=3, e=E0)
            dve.tensor_copy(F.sum8[:], c[:, :, 2, :]).then_inc(v, 1)
            for part, n in ((1, 16), (0, 17)):
                dve.wait_ge(v, n)
                dve.tensor_tensor(F.sum8[:], c[:, :, part, :], F.sum8[:], ALU.add).then_inc(v, 1)
            dve.wait_ge(loaded, 16 * len(loads))
            dve.tensor_copy(T.ident_bf[:], T.ident[:])
            for i, m in enumerate((T.mask_qk, T.mask_kq)):
                dve.tensor_copy(m[:].rearrange("p (h k) -> p h k", h=4),
                                T.masks[:, i * 128:(i + 1) * 128].unsqueeze(1).broadcast_to([128, 4, 128]))

        @block.gpsimd
        def _(pool):
            pool.memset(T.wd[64:128, UNITS - LOW:, :, :].rearrange("p u j n -> p (u j n)"), 0.0).then_inc(T.low_cleared, 1)


def ffn0(nc, T, F, banks):
    STEPS = 11
    with Stage(nc, "f0") as stage, ExitStack() as ctx:
        sem = stage.sem

        back = sem("back")
        m_ready = sem("m_ready")
        loaded = [sem("loaded0"), sem("loaded1")]
        xt_done = sem("xt_done")
        xt_copied = sem("xt_copied")
        base_done = sem("base_done")
        pair_done = sem("pair_done")
        added = sem("added")
        stat = sem("stat")
        base_used = sem("base_used")
        step = sem("step")
        normed = sem("normed")
        weight_exp = sem("weight_exp")
        var_done = sem("var_done")
        rstd_done = sem("rstd_done")
        block = ctx.enter_context(nc.Block())
        pairs, base, tr = banks[0:4], banks[4], banks[5]

        @block.sync
        def _(sp):
            for j in range(KT):
                sp.dma_start(F.m_re[:, j, :], F.table[j * 128 * 256:(j + 1) * 128 * 256, :]
                             .rearrange("(p r) e -> p (r e)", p=128)).then_inc(back, 16)

            def load(t, par):
                sp.dma_start(F.xs[par][:], flat(T.x_all, t)).then_inc(loaded[par], 16)
            load(0, 0)
            load(1, 1)
            with sp.Fori(0, B // 2 - 1) as i:
                for par in range(2):
                    sp.wait_ge(xt_done, i * 2 + (par + 1))
                    load(i * 2 + (par + 2), par)

        @block.tensor
        def _(pe):
            def transpose_x(i, par, first):
                pe.wait_ge(loaded[par], i * 16 + 16)
                if not first:
                    pe.wait_ge(xt_copied, i * 2 + par)
                for j in range(KT):
                    last = pe.transpose(tr[:, j * 128:(j + 1) * 128], F.xs[par][:, j * 128:(j + 1) * 128], T.ident[:])
                last.then_inc(xt_done, 1)

            def tile(i, par, first, final=False):
                t = i * 2 + par
                pe.wait_ge(xt_copied, t + 1)
                if not (first and par == 0):
                    pe.wait_ge(base_used, t)
                for j in range(KT):
                    last = pe.matmul(base[:, 0:264], F.xT[par][:, j * 128:(j + 1) * 128], T.f0_wg[:, j, :],
                                     start=(j == 0), stop=(j == KT - 1))
                last.then_inc(base_done, 1)
                if not final:
                    transpose_x(i + par, 1 - par, False)
                if first and par == 0:
                    pe.wait_ge(m_ready, 2)
                for q in range(4):
                    if not (first and par == 0):
                        pe.wait_ge(added, t * E0 + (2 * q + 2 - E0))
                    for j in range(KT):
                        last = pe.matmul(pairs[q][:, :], F.xT[par][:, j * 128:(j + 1) * 128], F.m[:, j, 2 * q:2 * q + 2, :],
                                         start=(j == 0), stop=(j == KT - 1))
                    last.then_inc(pair_done, 1)
            transpose_x(0, 0, True)
            tile(0, 0, True)
            tile(0, 1, True)
            with pe.Fori(1, B // 2 - 1) as i:
                tile(i, 0, False)
                tile(i, 1, False)
            tile(B // 2 - 1, 0, False)
            tile(B // 2 - 1, 1, False, True)

        @block.scalar
        def _(act):
            act.wait_ge(back, 16 * KT)
            act.activation(F.m[:, 0, :, :], F.m_re[:, 0, :].rearrange("p (r e) -> p e r", e=E0), ACT.Copy).then_inc(m_ready, 1)
            with act.Fori(0, B // 2) as i:
                for par in range(2):
                    t = i * 2 + par
                    act.wait_ge(xt_done, t + 1)
                    act.activation(F.xT[par][:], tr[:, 0:256], ACT.Copy).then_inc(xt_copied, 1)
                    act.wait_ge(step, t * STEPS + 3)
                    act.activation(F.wexp[:], F.wdiff[:], ACT.Exp).then_inc(weight_exp, 1)

        @block.gpsimd
        def _(pool):
            with pool.Fori(0, B) as t:
                pool.wait_ge(var_done, t + 1)
                pool.tensor_tensor(T.rstd[:], T.vare[:], T.half[:], ALU.pow).then_inc(rstd_done, 1)

        @block.vector
        def _(dve):
            dve.wait_ge(back, 16 * KT)
            dve.tensor_copy(F.m[:, 1, :, :], F.m_re[:, 1, :].rearrange("p (r e) -> p e r", e=E0)).then_inc(m_ready, 1)

            def choose(t):
                def after(k):
                    dve.wait_ge(step, t * STEPS + k)

                dve.wait_ge(base_done, t + 1)
                dve.tensor_scalar(F.logit[:], base[:, 256:264], -50.0, 50.0, ALU.max, ALU.min).then_inc(step, 1)
                wait_apart(T, dve, step, t * STEPS + 1)
                dve.max(F.top[:], F.logit[:]).then_inc(step, 1)
                after(2)
                dve.tensor_tensor(F.wdiff[:], F.top[:, 1:2], F.top[:, 0:1], ALU.subtract).then_inc(step, 1)
                dve.max_index(F.topi[:], F.top[:], F.logit[:]).then_inc(step, 1)
                after(4)
                dve.tensor_copy(F.topf[:], F.topi[:]).then_inc(step, 1)
                dve.wait_ge(weight_exp, t + 1)
                dve.tensor_scalar(F.p1[:], F.wexp[:], 1.0, None, ALU.add).then_inc(step, 1)
                after(6)
                dve.reciprocal(F.p0[:], F.p1[:]).then_inc(step, 1)
                after(7)
                dve.tensor_tensor(F.p1[:], F.p0[:], F.wexp[:], ALU.mult).then_inc(step, 1)
                dve.tensor_scalar(F.rw[:], T.iota[:, 0:E0], F.topf[:, 0:1], F.p0[:], ALU.is_equal, ALU.mult).then_inc(step, 1)
                after(9)
                dve.tensor_scalar(F.rw1[:], T.iota[:, 0:E0], F.topf[:, 1:2], F.p1[:], ALU.is_equal, ALU.mult).then_inc(step, 1)
                after(10)
                dve.tensor_tensor(F.rw[:], F.rw[:], F.rw1[:], ALU.add).then_inc(step, 1)

            def tile(t, final):
                x = flat(T.x_all, t)
                dve.tensor_tensor(F.acc[:, 0, :], base[:, 0:256], x, ALU.add).then_inc(base_used, 1)
                dve.wait_ge(base_used, t + 1)
                dve.wait_ge(step, t * STEPS + STEPS)
                for e in range(E0):
                    if e % 2 == 0:
                        dve.wait_ge(pair_done, t * 4 + (e // 2 + 1))
                    if e:
                        dve.wait_ge(added, t * E0 + e)
                    dve.scalar_tensor_tensor(F.acc[:, (e + 1) % 2, :], pairs[e // 2][:, (e % 2) * 256:(e % 2 + 1) * 256],
                                                   F.rw[:, e:e + 1], F.acc[:, e % 2, :], ALU.mult, ALU.add).then_inc(added, 1)
                acc = F.acc[:, 0, :]
                dve.wait_ge(added, t * E0 + E0)
                dve.bn_stats(T.stats[:], acc).then_inc(stat, 1)
                wait_apart(T, dve, stat, t * 2 + 1)
                dve.bn_aggr(T.mv[:], T.stats[:]).then_inc(stat, 1)
                dve.wait_ge(stat, t * 2 + 2)
                dve.tensor_scalar(T.vare[:], T.mv[:, 1:2], EPS, None, ALU.add).then_inc(var_done, 1)
                if not final:
                    choose(t + 1)
                dve.wait_ge(rstd_done, t + 1)
                dve.tensor_scalar(x, acc, T.mv[:, 0:1], T.rstd[:], ALU.subtract, ALU.mult).then_inc(normed, 1)
                dve.wait_ge(normed, t + 1)

            choose(0)
            with dve.Fori(0, B - 1) as t:
                tile(t, False)
            tile(B - 1, True)


def route(nc, a, T, G, banks):
    with Stage(nc, "r") as stage, ExitStack() as ctx:
        sem = stage.sem

        xt_done = sem("xt_done")
        xt_copied = sem("xt_copied")
        logits_done = sem("logits_done")
        exp_done = sem("exp_done")
        step = sem("step")
        padded = sem("padded")
        chosen_ready = sem("chosen_ready")
        ranked = sem("ranked")
        onehot_ready = sem("onehot_ready")
        placed = sem("placed")
        number_ready = sem("number_ready")
        number_done = sem("number_done")
        x_stored = sem("x_stored")
        gu_done = sem("gu_done")
        sil_ready = sem("sil_ready")
        h_ready = sem("h_ready")
        tr_done = sem("tr_done")
        ht_ready = sem("ht_ready")
        down_done = sem("down_done")
        share_ready = sem("share_ready")
        shared = sem("shared")
        block = ctx.enter_context(nc.Block())
        tr, gu, share, logits, table = banks[0:2], banks[2:4], banks[4:6], banks[6], banks[7]

        @block.gpsimd
        def _(pool):
            def add_share(t):
                if t == 0:
                    pool.wait_ge(x_stored, 16)
                pool.wait_ge(share_ready, t + 1)
                pool.tensor_tensor(T.x_all[:, t, :], T.x_all[:, t, :], G.share[t % 2][:], ALU.add).then_inc(shared, 1)

            pool.memset(T.wd[64:128, 0:UNITS - LOW, :, :].rearrange("p u j n -> p (u j n)"), 0.0).then_inc(T.high_cleared, 1)
            pool.wait_ge(T.high_cleared, 1)
            for v in range(2 * B):
                pool.wait_ge(sil_ready, v + 1)
                pool.tensor_tensor(G.h[v % 2][:], G.sil[v % 2][:], G.up[v % 2][:], ALU.mult).then_inc(h_ready, 1)
                if v % 2 == 1 and v > 1:
                    add_share(v // 2 - 1)
            add_share(B - 1)

        @block.sync
        def _(sp):
            sp.dma_start(G.x_rows.rearrange("(t p) c -> p t c", p=128), T.x_all[:]).then_inc(x_stored, 16)
            sp.wait_ge(T.high_cleared, 1)
            T.high_count = load_units(a, T, range(LOW, UNITS), sp, T.high_loaded)
            sp.wait_ge(x_stored, 16)

        @block.tensor
        def _(pe):
            for t in range(B):
                if t >= 2:
                    pe.wait_ge(xt_copied, t - 1)
                for j in range(KT):
                    last = pe.transpose(tr[t % 2][:, j * 128:(j + 1) * 128], T.x_all[:, t, j * 128:(j + 1) * 128], T.ident[:])
                last.then_inc(xt_done, 1)
            for t in range(B):
                pe.wait_ge(xt_copied, t + 1)
                for j in range(KT):
                    last = pe.matmul(logits[:, t * E1:(t + 1) * E1], G.xT[:, t, j * 128:(j + 1) * 128], T.f1_gate[:, j, :],
                                     start=(j == 0), stop=(j == KT - 1))
            last.then_inc(logits_done, 1)

            def gate_up(v):
                if v >= 2:
                    pe.wait_ge(sil_ready, v - 1)
                for j in range(KT):
                    last = pe.matmul(gu[v % 2][:, 0:2 * MI], G.xT[:, v // 2, j * 128:(j + 1) * 128], T.wgu[:, v % 2, j, :],
                                     start=(j == 0), stop=(j == KT - 1))
                last.then_inc(gu_done, 1)

            def transpose_h(v):
                pe.wait_ge(h_ready, v + 1)
                if v >= 2:
                    pe.wait_ge(ht_ready, v - 1)
                for j in range(2):
                    last = pe.transpose(tr[v % 2][0:MH, j * 128:(j + 1) * 128], G.h[v % 2][:, j * MH:(j + 1) * MH], T.ident[:])
                last.then_inc(tr_done, 1)

            def down(v):
                pe.wait_ge(ht_ready, v + 1)
                t = v // 2
                if v % 2 == 0 and t >= 2:
                    pe.wait_ge(share_ready, t - 1)
                for j in range(2):
                    last = pe.matmul(share[t % 2][:, 0:D], G.hT[v % 2][:, j * 128:(j + 1) * 128], T.wd[:, UNITS - 1 - v % 2, j, :],
                                     start=(v % 2 == 0 and j == 0), stop=(v % 2 == 1 and j == 1))
                if v % 2 == 1:
                    last.then_inc(down_done, 1)

            def rank():
                pe.wait_ge(chosen_ready, 1)
                pe.matmul(table[:, 0:B * E1], T.before_bf[:], G.chosen_bf[:], start=True, stop=True)
                pe.matmul(table[:, B * E1:2 * B * E1], T.ones_bf[:], G.chosen_bf[:], start=True, stop=True).then_inc(ranked, 1)

            def collect(part):
                pe.wait_ge(onehot_ready, part + 1)
                for c in range(PART):
                    last = pe.matmul(logits[:, 0:2 * SLOTS], G.row_hot[:, part % 2, c, :],
                                     G.slot_hot[:, part % 2, c, :, :].rearrange("p a s -> p (a s)"),
                                     start=(part == 0 and c == 0), stop=(part == ENTRIES // PART - 1 and c == PART - 1))
                last.then_inc(placed, 1)

            first_collect = 2 * B - (ENTRIES // PART - 1)
            pe.wait_ge(T.low_loaded, T.low_count)
            gate_up(0)
            for v in range(2 * B):
                if v + 1 < 2 * B:
                    gate_up(v + 1)
                transpose_h(v)
                if v >= 1:
                    down(v - 1)
                if v == 3:
                    rank()
                if v >= first_collect:
                    collect(v - first_collect)
            down(2 * B - 1)
            collect(ENTRIES // PART - 1)
            pe.wait_ge(number_ready, 1)
            pe.matmul(table[0:1, 0:128], G.number[:], T.ident[:], start=True, stop=True).then_inc(number_done, 1)

        @block.scalar
        def _(act):
            for t in range(B):
                act.wait_ge(xt_done, t + 1)
                act.activation(G.xT[:, t, :], tr[t % 2][:, 0:256], ACT.Copy).then_inc(xt_copied, 1)
            act.wait_ge(logits_done, 1)
            act.activation(G.score[:], logits[:, 0:B * E1], ACT.Exp, scale=-1.0).then_inc(exp_done, 1)

            def silu(v):
                act.wait_ge(gu_done, v + 1)
                if v >= 2:
                    act.wait_ge(h_ready, v - 1)
                act.activation(G.sil[v % 2][:], gu[v % 2][:, 0:MI], ACT.Silu)
                act.activation(G.up[v % 2][:], gu[v % 2][:, MI:2 * MI], ACT.Copy).then_inc(sil_ready, 1)

            silu(0)
            for v in range(2 * B + 1):
                if v + 1 < 2 * B:
                    silu(v + 1)
                if v < 2 * B:
                    if v == 0:
                        act.wait_ge(padded, 2)
                    act.wait_ge(tr_done, v + 1)
                    act.activation(G.hT[v % 2][0:MH, :], tr[v % 2][0:MH, 0:256], ACT.Copy).then_inc(ht_ready, 1)
                if v >= 2 and v % 2 == 0:
                    t = v // 2 - 1
                    act.wait_ge(down_done, t + 1)
                    if t >= 2:
                        act.wait_ge(shared, t - 1)
                    act.activation(G.share[t % 2][:], share[t % 2][:, 0:D], ACT.Copy).then_inc(share_ready, 1)

        @block.vector
        def _(dve):
            done = 0

            def then(ins):
                nonlocal done
                done += 1
                ins.then_inc(step, 1)
                dve.wait_ge(step, done)

            for par in range(2):
                dve.memset(G.hT[par][64:128, :], 0.0).then_inc(padded, 1)
            dve.wait_ge(exp_done, 1)
            then(dve.tensor_scalar(G.score[:], G.score[:], 1.0, None, ALU.add))
            then(dve.reciprocal(G.score[:], G.score[:]))
            grouped_scores = G.score[:].rearrange("p (t g e) -> p t g e", t=B, g=GROUPS)
            then(dve.tensor_reduce(G.gmax[:], grouped_scores, AX.X, ALU.max))
            this = G.gmax[:].unsqueeze(3).broadcast_to([128, B, GROUPS, GROUPS])
            other = G.gmax[:].unsqueeze(2).broadcast_to([128, B, GROUPS, GROUPS])
            then(dve.tensor_tensor(G.before[:], other, this, ALU.is_gt))
            then(dve.tensor_tensor(G.tied[:], other, this, ALU.is_equal))
            lower = T.lower[:].rearrange("p (g h) -> p g h", g=GROUPS).unsqueeze(1).broadcast_to([128, B, GROUPS, GROUPS])
            then(dve.tensor_tensor(G.tied[:], G.tied[:], lower, ALU.mult))
            then(dve.tensor_tensor(G.before[:], G.before[:], G.tied[:], ALU.add))
            then(dve.tensor_reduce(G.rank[:], G.before[:], AX.X, ALU.add))
            then(dve.tensor_scalar(G.rank[:], G.rank[:], float(TOP_GROUPS), None, ALU.is_lt))
            allowed = G.rank[:].unsqueeze(3).broadcast_to([128, B, GROUPS, E1 // GROUPS])
            masked = G.masked[:].rearrange("p (t g e) -> p t g e", t=B, g=GROUPS)
            then(dve.tensor_scalar(G.masked[:], G.score[:], 1.0, None, ALU.add))
            then(dve.tensor_tensor(masked, masked, allowed, ALU.mult))
            then(dve.tensor_scalar(G.masked[:], G.masked[:], -1.0, None, ALU.add))
            for t in range(B):
                then(dve.max(G.top[:, t, :], G.masked[:, t * E1:(t + 1) * E1]))
                then(dve.max_index(G.topi[:, t, :], G.top[:, t, :], G.masked[:, t * E1:(t + 1) * E1]))
            then(dve.tensor_copy(G.topf[:], G.topi[:]))
            shape = [128, B, TOP, E1]
            experts = T.iota[:, 0:E1].unsqueeze(1).unsqueeze(1).broadcast_to(shape)
            then(dve.tensor_tensor(G.hit[:], experts, G.topf[:, :, 0:TOP].unsqueeze(3).broadcast_to(shape), ALU.is_equal))
            chosen = G.masked[:].rearrange("p (t e) -> p t e", t=B)
            then(dve.tensor_reduce(chosen, G.hit[:].rearrange("p t k e -> p t e k"), AX.X, ALU.add))
            dve.tensor_copy(G.chosen_bf[:], G.masked[:]).then_inc(chosen_ready, 1)
            scores = G.score[:].rearrange("p (t e) -> p t e", t=B)
            then(dve.tensor_tensor(G.part[:], G.hit[:], scores.unsqueeze(2).broadcast_to(shape), ALU.mult))
            then(dve.tensor_reduce(G.w[:], G.part[:], AX.X, ALU.add))
            then(dve.tensor_reduce(G.total[:], G.w[:], AX.X, ALU.add))
            then(dve.reciprocal(G.total[:], G.total[:]))
            then(dve.tensor_tensor(G.w[:], G.w[:], G.total[:].unsqueeze(2).broadcast_to([128, B, TOP]), ALU.mult))
            dve.wait_ge(ranked, 1)
            in_tile = table[:, B * E1:2 * B * E1].rearrange("p (t e) -> p t e", t=B)
            then(dve.tensor_reduce(G.count[:], in_tile.rearrange("p t e -> p e t"), AX.X, ALU.add))
            then(dve.tensor_scalar(G.count[:], G.count[:], 127.0, None, ALU.add))
            then(dve.tensor_copy(G.count_i[:], G.count[:]))
            then(dve.tensor_scalar(G.count_i[:], G.count_i[:], 7, None, ALU.logical_shift_right))
            then(dve.memset(G.upto[0][:], 0.0))
            then(dve.memset(G.upto[1][:], 0.0))
            then(dve.tensor_copy(G.upto[0][:, 16:48], G.count_i[:]))
            then(dve.tensor_copy(G.count[:], G.count_i[:]))
            src = 0
            for shift in (1, 2, 4, 8, 16):
                then(dve.tensor_tensor(G.upto[1 - src][:, 16:48], G.upto[src][:, 16:48], G.upto[src][:, 16 - shift:48 - shift], ALU.add))
                src = 1 - src
            upto = G.upto[src][:, 16:48]
            then(dve.tensor_scalar(G.passed[:], upto, T.row[:, 0:1], None, ALU.is_le))
            then(dve.tensor_reduce(G.number[:], G.passed[:], AX.X, ALU.add))
            then(dve.tensor_scalar(G.number[:], G.number[:], float(E1 - 1), 2.0, ALU.min, ALU.add))
            dve.sem_inc(number_ready, 1)
            then(dve.tensor_tensor(G.count[:], upto, G.count[:], ALU.subtract))
            then(dve.tensor_scalar(G.start[:, 0, :], G.count[:], 128.0, None, ALU.mult))
            for t in range(1, B):
                then(dve.tensor_tensor(G.start[:, t, :], G.start[:, t - 1, :], in_tile[:, t - 1, :], ALU.add))
            then(dve.tensor_tensor(G.start[:], G.start[:], table[:, 0:B * E1].rearrange("p (t e) -> p t e", t=B), ALU.add))
            then(dve.tensor_tensor(G.part[:], G.hit[:], G.start[:].unsqueeze(2).broadcast_to(shape), ALU.mult))
            then(dve.tensor_reduce(G.place[:].rearrange("p (k t) -> p t k", t=B), G.part[:], AX.X, ALU.add))
            then(dve.tensor_copy(G.place_i[:], G.place[:]))
            then(dve.tensor_scalar(G.row_i[:], G.place_i[:], 127, None, ALU.bitwise_and))
            then(dve.tensor_scalar(G.place_i[:], G.place_i[:], 7, None, ALU.logical_shift_right))
            then(dve.tensor_copy(G.row_f[:], G.row_i[:]))
            then(dve.tensor_copy(G.place[:], G.place_i[:]))
            for part in range(ENTRIES // PART):
                if part >= 2:
                    dve.wait_ge(placed, part - 1)
                for c in range(PART):
                    n = part * PART + c
                    dve.tensor_scalar(G.row_hot[:, part % 2, c, :], T.columns_bf[:], G.row_f[:, n:n + 1], None, ALU.is_equal)
                    dve.tensor_scalar(G.slot_hot[:, part % 2, c, 0, :], T.columns_bf[:, 0:SLOTS], G.place[:, n:n + 1], T.row[:, 0:1],
                                      ALU.is_equal, ALU.mult)
                    last = dve.tensor_scalar(G.slot_hot[:, part % 2, c, 1, :], T.columns_bf[:, 0:SLOTS], G.place[:, n:n + 1], float(n + 1),
                                             ALU.is_equal, ALU.mult)
                last.then_inc(onehot_ready, 1)
            dve.wait_ge(placed, ENTRIES // PART)
            number = logits[:, SLOTS:2 * SLOTS]
            then(dve.scalar_tensor_tensor(G.empty[:], number, 0.0, T.spare[:], ALU.is_equal, ALU.mult))
            then(dve.scalar_tensor_tensor(G.out_f[:], number, 128.0, G.empty[:], ALU.mult, ALU.add))
            then(dve.tensor_tensor(G.out_f[:], G.out_f[:], logits[:, 0:SLOTS], ALU.add))
            then(dve.tensor_scalar(G.out_f[:], G.out_f[:], -128.0, None, ALU.add))
            then(dve.tensor_copy(G.out_row[:], G.out_f[:]))
            then(dve.tensor_scalar(G.x_row[:], G.out_row[:], B * S - 1, None, ALU.bitwise_and))
            dve.wait_ge(number_done, 1)
            then(dve.tensor_copy(G.unit[:], table[0:1, 0:SLOTS]))


def load_units(a, T, units, eng, sem):
    lo, hi = max(units.start - 2, 0), units.stop - 2
    at, end = lo + 2, hi + 2
    count = 2 * KT + hi - lo
    for u in range(units.start, 2):
        m = slice(u * MI, (u + 1) * MI)
        eng.dma_start(T.wgu[:, u, :, 0:MI], ktiles(a["L1_ffn_sw_gate"][:, m])).then_inc(sem, 16)
        eng.dma_start(T.wgu[:, u, :, MI:2 * MI], ktiles(a["L1_ffn_sw_up"][:, m])).then_inc(sem, 16)
        eng.dma_start(T.wd[0:MH, UNITS - 1 - u, :, :], a["L1_ffn_sw_down"][m, :].rearrange("(j p) n -> p j n", p=MH)).then_inc(sem, 16)
        count += 3
    for j in range(KT):
        rows = slice(j * 128, (j + 1) * 128)
        eng.dma_start(T.wgu[:, at:end, j, 0:MI], a["L1_ffn_w_gate"][lo:hi, rows, :].rearrange("e p m -> p e m")).then_inc(sem, 16)
        eng.dma_start(T.wgu[:, at:end, j, MI:2 * MI], a["L1_ffn_w_up"][lo:hi, rows, :].rearrange("e p m -> p e m")).then_inc(sem, 16)
    for e in range(lo, hi):
        eng.dma_start(T.wd[0:MH, UNITS - 3 - e, :, :], a["L1_ffn_w_down"][e].rearrange("(j p) n -> p j n", p=MH)).then_inc(sem, 16)
    return 16 * count


def experts(nc, a, T, G, banks):
    with Stage(nc, "e") as stage, ExitStack() as ctx:
        sem = stage.sem

        rows_ready = sem("rows_ready")
        gathered = [sem(f"gathered{i}") for i in range(4)]
        xt_done = sem("xt_done")
        xt_copied = sem("xt_copied")
        gu_done = sem("gu_done")
        sil_ready = sem("sil_ready")
        h_ready = sem("h_ready")
        tr_done = sem("tr_done")
        ht_ready = sem("ht_ready")
        down_done = sem("down_done")
        out_ready = sem("out_ready")
        scattered = [sem(f"scattered{i}") for i in range(4)]
        block = ctx.enter_context(nc.Block())
        trx, gu, trh, down_bank = banks[0:2], banks[2:4], banks[4:6], banks[6:8]

        def steps(eng, step):
            for s in range(-5, 5):
                step(0, s)
            with eng.Fori(0, (SLOTS - 12) // 4) as i:
                for c in range(5, 9):
                    step(i, c)
            for s in range(SLOTS - 7, SLOTS + 1):
                step(0, s)

        class At:

            def __init__(self, i, c):
                self.there = not isinstance(i, int) or 0 <= c < SLOTS
                self.n = c if isinstance(i, int) else i * 4 + c
                self.buffer, self.parity = c % 4, c % 2
                self.i, self.c = i, c

            def reuse(self, before):
                return not isinstance(self.i, int) or self.c >= before

            def dma_count(self, back=0):
                return (self.i + (self.c // 4 + 1 - back)) * 16

        @block.gpsimd
        def _(pool):
            def step(i, c):
                s = At(i, c + 5)
                if s.there:
                    pool.wait_ge(rows_ready, s.n + 1)
                    if s.reuse(4):
                        pool.wait_ge(xt_done, s.n - 3)
                    pool.sem_inc(T.passed, 1)
                    pool.indirect_dma_start(G.xg[s.buffer][:], None, G.x_rows[:, :],
                                            bass.IndirectOffsetOnAxis(ap=G.x_index[s.buffer][:], axis=0)).then_inc(gathered[s.buffer], 16)
                s = At(i, c - 1)
                if s.there:
                    wait_apart(T, pool, out_ready, s.n + 1)
                    pool.indirect_dma_start(G.out_rows[:, :], bass.IndirectOffsetOnAxis(ap=G.out_index[s.buffer][:], axis=0),
                                            G.og[s.buffer][:], None).then_inc(scattered[s.buffer], 16)

            steps(pool, step)
            for par in range(4):
                pool.wait_ge(scattered[par], SLOTS // 4 * 16)

        @block.tensor
        def _(pe):
            def step(i, c):
                s = At(i, c + 1)
                if s.there:
                    unit = pe.value_load(G.unit[0:1, bass.ds(s.n, 1)], min_val=0, max_val=UNITS - 1)
                s = At(i, c + 2)
                if s.there:
                    pe.wait_ge(gathered[s.buffer], s.dma_count())
                    if s.reuse(2):
                        pe.wait_ge(xt_copied, s.n - 1)
                    for j in range(KT):
                        last = pe.transpose(trx[s.parity][:, j * 128:(j + 1) * 128], G.xg[s.buffer][:, j * 128:(j + 1) * 128], T.ident[:])
                    last.then_inc(xt_done, 1)
                s = At(i, c + 1)
                if s.there:
                    pe.wait_ge(xt_copied, s.n + 1)
                    if s.reuse(2):
                        pe.wait_ge(h_ready, s.n - 1)
                    for j in range(KT):
                        last = pe.matmul(gu[s.parity][:, 0:2 * MI], G.xgT[s.parity][:, j * 128:(j + 1) * 128],
                                         T.wgu[:, bass.ds(unit, 1), j, :].rearrange("p a n -> p (a n)"), start=(j == 0), stop=(j == KT - 1))
                    last.then_inc(gu_done, 1)
                s = At(i, c)
                if s.there:
                    pe.wait_ge(h_ready, s.n + 1)
                    if s.reuse(2):
                        pe.wait_ge(ht_ready, s.n - 1)
                    for j in range(2):
                        last = pe.transpose(trh[s.parity][0:MH, j * 128:(j + 1) * 128], G.h[s.parity][:, j * MH:(j + 1) * MH], T.ident[:])
                    last.then_inc(tr_done, 1)
                s = At(i, c - 1)
                if s.there:
                    unit = pe.value_load(G.unit[0:1, bass.ds(s.n, 1)], min_val=0, max_val=UNITS - 1)
                    pe.wait_ge(ht_ready, s.n + 1)
                    if s.reuse(2):
                        pe.wait_ge(out_ready, s.n - 1)
                    for j in range(2):
                        last = pe.matmul(down_bank[s.parity][:, 0:D], G.hT[s.parity][:, j * 128:(j + 1) * 128],
                                         T.wd[:, bass.ds(unit * -1 + (UNITS - 1), 1), j, :].rearrange("p a n -> p (a n)"),
                                         start=(j == 0), stop=(j == 1))
                    last.then_inc(down_done, 1)

            pe.wait_ge(T.low_loaded, T.low_count)
            pe.wait_ge(T.high_loaded, T.high_count)
            steps(pe, step)

        @block.scalar
        def _(act):
            def step(i, c):
                s = At(i, c + 2)
                if s.there:
                    act.wait_ge(xt_done, s.n + 1)
                    act.activation(G.xgT[s.parity][:], trx[s.parity][:, 0:D], ACT.Copy).then_inc(xt_copied, 1)
                s = At(i, c + 1)
                if s.there:
                    act.wait_ge(gu_done, s.n + 1)
                    act.activation(G.sil[s.parity][:], gu[s.parity][:, 0:MI], ACT.Silu).then_inc(sil_ready, 1)
                s = At(i, c)
                if s.there:
                    act.wait_ge(tr_done, s.n + 1)
                    act.activation(G.hT[s.parity][0:MH, :], trh[s.parity][0:MH, 0:256], ACT.Copy).then_inc(ht_ready, 1)

            steps(act, step)

        @block.vector
        def _(dve):
            def step(i, c):
                s = At(i, c + 5)
                if s.there:
                    if s.reuse(4):
                        dve.wait_ge(gathered[s.buffer], s.dma_count(1))
                    dve.tensor_copy(G.x_index[s.buffer][:], G.x_row[:, bass.ds(s.n, 1)]).then_inc(rows_ready, 1)
                s = At(i, c + 1)
                if s.there:
                    dve.wait_ge(sil_ready, s.n + 1)
                    dve.tensor_tensor(G.h[s.parity][:], gu[s.parity][:, MI:2 * MI], G.sil[s.parity][:], ALU.mult).then_inc(h_ready, 1)
                s = At(i, c - 1)
                if s.there:
                    dve.wait_ge(down_done, s.n + 1)
                    if s.reuse(4):
                        dve.wait_ge(scattered[s.buffer], s.dma_count(1))
                    dve.tensor_copy(G.out_index[s.buffer][:], G.out_row[:, bass.ds(s.n, 1)])
                    dve.tensor_copy(G.og[s.buffer][:], down_bank[s.parity][:, 0:D]).then_inc(out_ready, 1)

            steps(dve, step)


def combine(nc, T, G, out):
    with Stage(nc, "c") as stage, ExitStack() as ctx:
        sem = stage.sem

        loaded = [sem(f"loaded{t}") for t in range(B)]
        res = sem("res")
        stat = sem("stat")
        rstd_done = sem("rstd_done")
        stored = sem("stored")
        block = ctx.enter_context(nc.Block())
        sums = TOP * B
        entries = G.out_rows[0:TOP * B * S, :].rearrange("(k t p) c -> t p k c", t=B, p=128)

        @block.scalar
        def _(act):
            for t in range(1, B, 2):
                act.dma_start(G.y[:, t, :, :], entries[t]).then_inc(loaded[t], 16)

        @block.gpsimd
        def _(pool):
            pool.wait_ge(res, sums + B + 1)
            pool.tensor_tensor(G.rstd[:], G.vare[:], T.half[:, 0:1].broadcast_to([128, B]), ALU.pow).then_inc(rstd_done, 1)

        @block.sync
        def _(sp):
            for t in range(0, B, 2):
                sp.dma_start(G.y[:, t, :, :], entries[t]).then_inc(loaded[t], 16)
            for t in range(B):
                sp.wait_ge(res, sums + B + 1 + t + 1)
                sp.dma_start(out[t, :, :], T.x_all[:, t, :]).then_inc(stored, 16)
            sp.wait_ge(stored, 16 * B)

        @block.vector
        def _(dve):
            done = 0
            for pair in range(B // 2):
                for k in range(TOP):
                    for t in (2 * pair, 2 * pair + 1):
                        if k == 0:
                            dve.wait_ge(loaded[t], 16)
                        else:
                            dve.wait_ge(res, done - 1)
                        dve.scalar_tensor_tensor(T.x_all[:, t, :], G.y[:, t, k, :], G.w[:, t, k:k + 1], T.x_all[:, t, :],
                                                 ALU.mult, ALU.add).then_inc(res, 1)
                        done += 1
            for t in range(B):
                dve.wait_ge(res, sums)
                dve.bn_stats(G.stats[:, t, :], T.x_all[:, t, :]).then_inc(stat, 1)
            for t in range(B):
                dve.wait_ge(stat, t + 1)
                dve.bn_aggr(G.mv[:, t, :], G.stats[:, t, :]).then_inc(res, 1)
            dve.wait_ge(res, sums + B)
            dve.tensor_scalar(G.vare[:], G.mv[:, :, 1], EPS, None, ALU.add).then_inc(res, 1)
            dve.wait_ge(rstd_done, 1)
            for t in range(B):
                dve.tensor_scalar(T.x_all[:, t, :], T.x_all[:, t, :], G.mv[:, t, 0:1], G.rstd[:, t:t + 1],
                                  ALU.subtract, ALU.mult).then_inc(res, 1)


def store(nc, T, out):
    with ExitStack() as c2:
        st = c2.enter_context(nc.semaphore("st"))
        block = c2.enter_context(nc.Block())

        @block.sync
        def _(sp):
            sp.wait_ge(T.low_loaded, T.low_count)
            sp.dma_start(out.rearrange("b p c -> p b c"), T.x_all[:]).then_inc(st, 16)
            sp.wait_ge(st, 16)


STAGES = ("a0", "x0", "f0", "a1", "x1", "f1")


def decoder(nc, a, out):
    with ExitStack() as ctx:
        T, F, G = Tensors(), Tensors(), Tensors()
        banks = [ctx.enter_context(nc.psum_tensor(f"bank{i}", [128, 512], F32)) for i in range(8)]
        T.SB, T.STB, T.PV, T.PA, T.PB, T.M = banks[0:2], banks[2:4], banks[4], banks[5], banks[6], banks[7]
        start = (nc.sbuf_base + 31) // 32 * 32
        end = nc.sbuf_usable_end // 32 * 32
        weights = UNITS * (2 * KT * MI + 2 * D) * 4
        keep = Memory(nc, start, end - weights)
        units = Memory(nc, end - weights, end)
        T.wgu = units("wgu", [128, UNITS, KT, 2 * MI])
        middle = units.at
        T.wd = units("wd", [128, UNITS, 2, D])

        T.x_all = keep("x_all", [128, B, D])
        T.ident = keep("ident", [128, 128])
        T.half = keep("half", [128, 1])
        T.iota = keep("iota", [128, E1])
        T.lower = keep("lower", [128, GROUPS * GROUPS])
        T.row, T.columns_bf = keep("row", [128, 1]), keep("columns_bf", [128, 128], BF16)
        T.spare = keep("spare", [128, SLOTS])
        T.before_bf, T.ones_bf = keep("before_bf", [128, 128], BF16), keep("ones_bf", [128, 128], BF16)
        T.f1_gate = keep("f1_gate", [128, KT, E1])
        T.rstd, T.vare = keep("rstd", [128, 1]), keep("vare", [128, 1])
        T.stats, T.mv = keep("stats", [128, 6]), keep("mv", [128, 2])
        kept = keep.at

        BF, first = BF16, keep.at
        G.xT = keep("g_xT", [128, B, D])
        behind = keep.at
        G.hit = keep("g_hit", [128, B, TOP, E1], BF)
        onehots = Memory(nc, keep.at, keep.end)
        G.row_hot = onehots("g_row_hot", [128, 2, PART, 128], BF)
        G.slot_hot = onehots("g_slot_hot", [128, 2, PART, 2, SLOTS], BF)
        G.part = keep("g_part", [128, B, TOP, E1])
        keep.at = max(keep.at, onehots.at)
        G.w = keep("g_w", [128, B, TOP])
        G.score, G.masked = keep("g_score", [128, B * E1]), keep("g_masked", [128, B * E1])
        G.chosen_bf = keep("g_chosen_bf", [128, B * E1], BF)
        G.gmax, G.rank = keep("g_gmax", [128, B, GROUPS]), keep("g_rank", [128, B, GROUPS])
        G.before, G.tied = keep("g_before", [128, B, GROUPS, GROUPS]), keep("g_tied", [128, B, GROUPS, GROUPS])
        G.top, G.topi, G.topf = keep("g_top", [128, B, 8]), keep("g_topi", [128, B, 8], U32), keep("g_topf", [128, B, 8])
        G.total = keep("g_total", [128, B])
        G.count, G.count_i, G.passed = keep("g_count", [128, E1]), keep("g_count_i", [128, E1], I32), keep("g_passed", [128, E1])
        G.upto = [keep(f"g_upto{i}", [128, 16 + E1]) for i in range(2)]
        G.number, G.start = keep("g_number", [128, 1]), keep("g_start", [128, B, E1])
        G.place, G.place_i = keep("g_place", [128, ENTRIES]), keep("g_place_i", [128, ENTRIES], I32)
        G.row_f, G.row_i = keep("g_row_f", [128, ENTRIES]), keep("g_row_i", [128, ENTRIES], I32)
        G.empty, G.out_f = keep("g_empty", [128, SLOTS]), keep("g_out_f", [128, SLOTS])
        G.out_row, G.x_row = keep("g_out_row", [128, SLOTS], I32), keep("g_x_row", [128, SLOTS], I32)
        G.unit = keep("g_unit", [1, SLOTS], I32)
        G.sil, G.up, G.h = ([keep(f"g_{n}{i}", [128, MI]) for i in range(2)] for n in ("sil", "up", "h"))
        G.hT = [keep(f"g_hT{i}", [128, 256]) for i in range(2)]
        G.share = [keep(f"g_share{i}", [128, D]) for i in range(2)]
        G.stats, G.mv = keep("g_stats", [128, B, 6]), keep("g_mv", [128, B, 2])
        G.vare, G.rstd = keep("g_vare", [128, B]), keep("g_rstd", [128, B])
        slot = Memory(nc, first, behind + B * TOP * E1 * 2)
        G.xg, G.og = ([slot(f"g_{n}{i}", [128, D]) for i in range(4)] for n in ("xg", "og"))
        G.xgT = [slot(f"g_xgT{i}", [128, D]) for i in range(2)]
        G.x_index, G.out_index = ([slot(f"g_{n}{i}", [128, 1], I32) for i in range(4)] for n in ("x_index", "out_index"))
        G.y = Memory(nc, end - weights, end)("g_y", [128, B, TOP, D])
        G.x_rows = nc.dram_tensor("x_rows", [B * S, D], F32).ap()
        G.out_rows = nc.dram_tensor("out_rows", [(ENTRIES + SLOTS) * 128, D], F32).ap()

        shared_start = middle - (UNITS - LOW) * KT * 2 * MI * 4
        shared_end = middle + (UNITS - LOW) * 2 * D * 4
        early = Memory(nc, kept, end - weights)
        at = Memory(nc, shared_start, shared_end)
        T.before, T.columns = early("before", [128, 128]), early("columns", [128, 128])
        T.masks, T.blockmask, T.rope = early("masks", [128, 256]), early("blockmask", [128, 12]), early("rope", [128, 16])
        T.onerows = early("onerows", [128, 24])
        T.ident_bf = early("ident_bf", [128, 128], BF16)
        T.mask_qk, T.mask_kq = early("mask_qk", [128, 512], BF16), early("mask_kq", [128, 512], BF16)
        T.b_qk, T.b_v, T.b_o = early("b_qk", [128, 512]), early("b_v", [128, 256]), early("b_o", [128, 256])
        T.a0_wqk, T.a0_wv, T.a0_wo = early("a0_wqk", [128, KT, 512]), early("a0_wv", [128, KT, 256]), early("a0_wo", [128, KT, 256])
        T.a1_wqkv, T.a1_wo = early("a1_wqkv", [128, KT, 384]), early("a1_wo", [128, KT, 256])
        T.x1_wq, T.x1_wkv, T.x1_wo = early("x1_wq", [128, KT, 256]), early("x1_wkv", [CTX, 512]), early("x1_wo", [128, KT, 256])
        T.wo = {"a0": T.a0_wo, "a1": T.a1_wo, "x1": T.x1_wo}
        T.f0_wg = early("f0_wg", [128, KT, 264])
        T.nm, T.nmf = at("nm", [128, 4, 128], F32R), at("nmf", [128, 4, 8])
        ff = Memory(nc, at.at, shared_end)
        T.kb1, T.kb2 = ([at(f"{n}_{i}", [128, 16, 128], F32R) for i in range(2)] for n in ("kb1", "kb2"))
        T.q1, T.q2 = ([at(f"{n}_{i}", [128, 4, 128], F32R) for i in range(2)] for n in ("q1", "q2"))
        T.qs, T.ks1, T.ks2 = at("qs", [128, 4, 128], F32R), at("ks1", [128, 4, 128], F32R), at("ks2", [128, 4, 64], F32R)
        T.pt = [at(f"pt{i}", [128, 512]) for i in range(2)]
        T.xs = [at(f"xs{i}", [128, D]) for i in range(2)]
        T.cs = [at(f"cs{i}", [128, CTX]) for i in range(2)]
        T.vaug = [at(f"vaug{i}", [128, 4 * (4 * 68 + 17)]) for i in range(2)]
        T.pvs = at("pvs", [128, 512])
        T.xT, T.qk = at("xT", [128, 384]), at("qk", [128, 512])
        T.att, T.atT, T.rec, T.res, T.xb = at("att", [128, D]), at("atT", [128, D]), at("rec", [128, 32]), at("res", [128, D]), at("xb", [128, D])
        T.rope_a, T.rope_b = at("rope_a", [128, 320]), at("rope_b", [128, 320])
        T.ctx_tiles = a["ctx_512"]

        ST = NS // 128
        F.table = nc.dram_tensor("sparse_table", [D * D, E0], F32).ap()
        F.m, F.m_re = ff("f_m", [128, KT, E0, D]), ff("f_m_re", [128, KT, D * E0])
        own = Memory(nc, ff.at, shared_end)
        F.eaw, F.eawmax, F.eawsum = ff("f_eaw", [E0, ATOMS]), ff("f_eawmax", [E0, 1]), ff("f_eawsum", [E0, 1])
        F.atoms, F.eawT, F.imp = ff("f_atoms", [ATOMS, NS]), ff("f_eawT", [ATOMS, E0]), ff("f_imp", [128, ST * E0])
        F.idx_row, F.idx_col = ff("f_idx_row", [128, NS], I32), ff("f_idx_col", [128, ST], I32)
        F.col_f, F.pos_hi, F.w3 = ff("f_col_f", [128, ST]), ff("f_pos_hi", [128, ST], I32), ff("f_w3", [128, ST, 3 * E0], BF16)
        F.eq = [ff(f"f_eq{i}", [128, NS], BF16) for i in range(EQ)]
        F.pos, F.sum8 = early("f_pos", [128, ST], I32), early("f_sum8", [128, ST, E0])
        F.pos_now, F.sum_now = early("f_pos_now", [128, 1], I32), early("f_sum_now", [128, E0])
        F.xs = [own(f"f_xs{i}", [128, D]) for i in range(2)]
        F.xT = [own(f"f_xT{i}", [128, D]) for i in range(2)]
        F.acc = own("f_acc", [128, 2, D])
        F.logit, F.top, F.topi, F.topf = own("f_logit", [128, 8]), own("f_top", [128, 8]), own("f_topi", [128, 8], U32), own("f_topf", [128, 8])
        F.wdiff, F.wexp, F.p0, F.p1 = (own(n, [128, 1]) for n in ("f_wdiff", "f_wexp", "f_p0", "f_p1"))
        F.rw, F.rw1 = own("f_rw", [128, 8]), own("f_rw1", [128, 8])

        T.passed, T.later_loaded, T.low_loaded, T.low_cleared, T.high_loaded, T.high_cleared = (
            ctx.enter_context(nc.semaphore(n)) for n in ("passed", "later_loaded", "low_loaded", "low_cleared", "high_loaded", "high_cleared"))
        load_first(nc, a, T, F, banks)
        if "a0" in STAGES:
            attention(nc, ATTN0, T, F)
        if "x0" in STAGES:
            attention(nc, CROSS0, T, F)
        if "f0" in STAGES:
            ffn0(nc, T, F, banks)
        if "a1" in STAGES:
            attention(nc, ATTN1, T, F)
        if "x1" in STAGES:
            attention(nc, CROSS1, T, F)
        if "f1" in STAGES:
            route(nc, a, T, G, banks)
            experts(nc, a, T, G, banks)
            combine(nc, T, G, out)
        else:
            store(nc, T, out)


def constants():
    q, k = np.arange(128)[:, None], np.arange(128)[None, :]
    masks = np.concatenate([np.where(k > q, MASKED, 0.0), np.where(q > k, MASKED, 0.0)], 1).astype(np.float32)
    row = np.arange(128)[:, None] % 64
    blockmask = np.concatenate([row // 8 == np.arange(8), row // 16 == np.arange(4)], 1).astype(np.float32)
    onerows = np.zeros((128, 24), np.float32)
    for j in range(8):
        onerows[[MAX_HI + j, MAX_LO + j], j] = 1.0
        if j < 4:
            onerows[[[MAX_HI + j], [MAX_LO + j]], 8 + j + 4 * np.arange(4)] = 1.0
    freq = (1.0 / 10000.0 ** (np.arange(0, 8, 2, dtype=np.float32) / 8)).astype(np.float32)
    ang = np.arange(128, dtype=np.float32)[:, None] * freq[None, :]
    cos, sin = np.cos(ang), np.sin(ang)
    rope = np.concatenate([cos, cos, -sin, sin], 1).astype(np.float32)
    g = np.arange(GROUPS)
    return {"ident": np.eye(128, dtype=np.float32), "masks": masks, "blockmask": blockmask,
            "onerows": onerows, "rope": rope,
            "row": np.arange(128, dtype=np.float32)[:, None], "columns": np.arange(128, dtype=np.float32),
            "spare": (128.0 * (ENTRIES + 1 + np.arange(SLOTS))[None, :] + np.arange(128)[:, None]).astype(np.float32),
            "before": (q < k).astype(np.float32),
            "iota": np.arange(E1, dtype=np.float32),
            "lower": (g[None, :] < g[:, None]).astype(np.float32).reshape(-1)}


TRANSPOSED = ("L0_attn_Wq", "L0_attn_Wk", "L0_attn_Wv", "L0_attn_Wo", "L1_attn_Wk", "L1_attn_Wv", "L1_attn_Wo",
              "L1_xattn_Wq", "L1_xattn_Wkv_expand", "L1_xattn_Wout", "L0_ffn_W", "L0_ffn_gate_w")


def layout(inputs):
    a = {k: np.asarray(v) for k, v in inputs.items()}
    for name in TRANSPOSED:
        a[name] = a[name].T
    a["L1_attn_Wq"] = a["L1_attn_Wq"].reshape(8, 4, 8, D).transpose(1, 0, 2, 3).reshape(D, D).T
    a["importance"] = a.pop("L0_ffn_importance").reshape(E0, NS // 128, 128).transpose(2, 1, 0).reshape(128, -1)
    a["mask_idx_columns"] = a["L0_ffn_mask_idx"].reshape(NS // 128, 128).T
    a = {k: np.ascontiguousarray(v) for k, v in a.items()}
    a.update(constants())
    return a


def kernel(**inputs):
    import concourse.bacc as bacc
    from concourse.bass_utils import run_bass_kernel_spmd

    nc = bacc.Bacc("TRN2", target_bir_lowering=False, num_devices=1)
    arrays = {f"in_{k}": v for k, v in layout(inputs).items()}
    aps = {k[3:]: nc.dram_tensor(k, v.shape, mybir.dt.from_np(v.dtype), kind="ExternalInput").ap() for k, v in arrays.items()}
    out = nc.dram_tensor("out", (B, S, D), F32, kind="ExternalOutput").ap()
    decoder(nc, aps, out)
    return run_bass_kernel_spmd(nc, [arrays], core_ids=[0]).results[0]["out"]
```
